# Optimizing a Trainium2 kernel written in Bass

```python
import numpy as np
import jax
import jax.numpy as jnp

def _softmax(x, axis=-1):
    return jax.nn.softmax(x, axis=axis)

def _gelu(x):
    return jax.nn.gelu(x, approximate=True)

def _silu(x):
    return jax.nn.silu(x)

def _sigmoid(x):
    return jax.nn.sigmoid(x)

def _layernorm(x, axis=-1, eps=1e-05):
    m = jnp.mean(x, axis=axis, keepdims=True)
    v = jnp.var(x, axis=axis, keepdims=True)
    return (x - m) / jnp.sqrt(v + eps)

def _scatter_add(tgt, idx, src, axis=0):
    return tgt.at[idx].add(src)

def _segment_sum(src, seg, n):
    return jax.ops.segment_sum(src, seg, n)
kernel_name = 'mk_conv_attn_hybrid_d4_conv_nhwc128_r2_3707e7'

def setup_inputs(seed: int=0):
    np.random.seed(seed)
    _w = jnp.asarray

    def _rec_inputs():
        import jax
        import jax.numpy as jnp
        _gk = jax.random.key(seed)
        x = -0.000125 + 0.9999 * jax.random.normal(jax.random.fold_in(_gk, 1), (32, 32, 32, 64), jnp.float32)
        return x
    x = _rec_inputs()

    def _L0_conv_setup():
        import jax, jax.numpy as jnp
        import numpy as np
        W_DIM = 8
        SHIFT = 4
        HEADS = 4

        def _rel_pos_index(w):
            coords = np.stack(np.meshgrid(np.arange(w), np.arange(w), indexing='ij'))
            flat = coords.reshape(2, -1)
            rel = flat[:, :, None] - flat[:, None, :]
            rel = rel.transpose(1, 2, 0) + (w - 1)
            return rel[..., 0] * (2 * w - 1) + rel[..., 1]

        def _shift_mask(H, W, w, s):
            img = np.zeros((H, W), dtype=np.int32)
            cnt = 0
            for hs in (slice(0, -w), slice(-w, -s), slice(-s, None)):
                for ws in (slice(0, -w), slice(-w, -s), slice(-s, None)):
                    img[hs, ws] = cnt
                    cnt += 1
            win = img.reshape(H // w, w, W // w, w).transpose(0, 2, 1, 3).reshape(-1, w * w)
            diff = win[:, None, :] - win[:, :, None]
            return np.where(diff != 0, -1000000000.0, 0.0).astype(np.float32)

        def _ln(x, g, b):
            mu = x.mean(-1, keepdims=True)
            var = x.var(-1, keepdims=True)
            return (x - mu) / jnp.sqrt(var + 1e-05) * g + b

        def _window_partition(x, w):
            B, H, W, C = x.shape
            x = x.reshape(B, H // w, w, W // w, w, C).transpose(0, 1, 3, 2, 4, 5)
            return x.reshape(-1, w * w, C)

        def _window_reverse(win, w, B, H, W):
            C = win.shape[-1]
            x = win.reshape(B, H // w, W // w, w, w, C).transpose(0, 1, 3, 2, 4, 5)
            return x.reshape(B, H, W, C)
        key = jax.random.key(seed)
        ks = jax.random.split(key, 6)
        B, H, W, C = (32, 32, 32, 64)
        d_ff = 4 * C
        return {'x': jax.random.normal(ks[0], (B, H, W, C), jnp.float32), 'ln1_g': jnp.ones((C,), jnp.float32), 'ln1_b': jnp.zeros((C,), jnp.float32), 'qkv_w': jax.random.normal(ks[1], (C, 3 * C), jnp.float32) * 0.02, 'qkv_b': jnp.zeros((3 * C,), jnp.float32), 'proj_w': jax.random.normal(ks[2], (C, C), jnp.float32) * 0.02, 'proj_b': jnp.zeros((C,), jnp.float32), 'rpb': jax.random.normal(ks[3], ((2 * W_DIM - 1) ** 2, HEADS), jnp.float32) * 0.02, 'ln2_g': jnp.ones((C,), jnp.float32), 'ln2_b': jnp.zeros((C,), jnp.float32), 'fc1_w': jax.random.normal(ks[4], (C, d_ff), jnp.float32) * 0.02, 'fc1_b': jnp.zeros((d_ff,), jnp.float32), 'fc2_w': jax.random.normal(ks[5], (d_ff, C), jnp.float32) * 0.02, 'fc2_b': jnp.zeros((C,), jnp.float32)}
    _L0_conv_all = _L0_conv_setup()
    _L0_conv_in = {k: v for k, v in _L0_conv_all.items() if k in ('ln1_g', 'ln1_b', 'qkv_w', 'qkv_b', 'proj_w', 'proj_b', 'rpb', 'ln2_g', 'ln2_b', 'fc1_w', 'fc1_b', 'fc2_w', 'fc2_b')}
    del _L0_conv_all

    def _L1_conv_setup():
        import jax, jax.numpy as jnp
        import numpy as np
        LN_EPS = 1e-05

        def _layer_norm(x, scale, bias):
            mu = jnp.mean(x, axis=-1, keepdims=True)
            var = jnp.mean(jnp.square(x - mu), axis=-1, keepdims=True)
            return (x - mu) * jax.lax.rsqrt(var + LN_EPS) * scale + bias
        key = jax.random.key(seed)
        ks = jax.random.split(key, 8)
        B, N, C, H = (1, 192, 64, 64)
        s_in = 1.0 / np.sqrt(C)
        s_h = 1.0 / np.sqrt(H)
        return {'pair': jax.random.normal(ks[0], (B, N, N, C), jnp.float32), 'W_left': jax.random.normal(ks[1], (C, H), jnp.float32) * s_in, 'b_left': jnp.zeros((H,), jnp.float32), 'W_right': jax.random.normal(ks[2], (C, H), jnp.float32) * s_in, 'b_right': jnp.zeros((H,), jnp.float32), 'W_gate': jax.random.normal(ks[3], (C, H), jnp.float32) * s_in, 'b_gate': jnp.zeros((H,), jnp.float32), 'W_eq': jax.random.normal(ks[4], (C, H), jnp.float32) * s_in, 'b_eq': jnp.zeros((H,), jnp.float32), 'W_out': jax.random.normal(ks[5], (H, C), jnp.float32) * s_h, 'b_out': jnp.zeros((C,), jnp.float32), 'ln_scale': jnp.ones((C,), jnp.float32), 'ln_bias': jnp.zeros((C,), jnp.float32)}
    _L1_conv_all = _L1_conv_setup()
    _L1_conv_in = {k: v for k, v in _L1_conv_all.items() if k in ('W_left', 'b_left', 'W_right', 'b_right', 'W_gate', 'b_gate', 'W_eq', 'b_eq', 'W_out', 'b_out', 'ln_scale', 'ln_bias')}
    del _L1_conv_all

    def _L2_attn_setup():
        import jax, jax.numpy as jnp
        import numpy as np
        key = jax.random.key(seed)
        seq = jax.random.normal(key, (32, 1024, 64), dtype=jnp.float32)
        return {'seq': seq}
    _L2_attn_all = _L2_attn_setup()
    _L2_attn_in = {k: v for k, v in _L2_attn_all.items() if k in ()}
    del _L2_attn_all

    def _L2_ffn_setup():
        import jax, jax.numpy as jnp
        import numpy as np
        B, S, D, E, H, O, K = (256, 1024, 64, 32, 256, 64, 8)
        key = jax.random.key(seed)
        k0, k1, k2, k3 = jax.random.split(key, 4)
        x = jax.random.normal(k0, (B, S, D), dtype=jnp.float32)
        gate_w = jax.random.normal(k1, (E, D), dtype=jnp.float32) * (1.0 / np.sqrt(D))
        gate_b = jnp.zeros((E,), dtype=jnp.float32)
        weight1 = jax.random.uniform(k2, (E, D + 1, H), dtype=jnp.float32, minval=-1.0, maxval=1.0) * (1.0 / np.sqrt(D + 1))
        weight2 = jax.random.uniform(k3, (E, H + 1, O), dtype=jnp.float32, minval=-1.0, maxval=1.0) * (1.0 / np.sqrt(H + 1))
        return {'x': x, 'gate_w': gate_w, 'gate_b': gate_b, 'weight1': weight1, 'weight2': weight2}
    _L2_ffn_all = _L2_ffn_setup()
    _L2_ffn_in = {k: v for k, v in _L2_ffn_all.items() if k in ('gate_w', 'gate_b', 'weight1', 'weight2')}
    del _L2_ffn_all

    def _L3_attn_setup():
        import jax, jax.numpy as jnp
        import numpy as np
        TEMP = (2 * 64) ** 0.5
        key = jax.random.key(seed)
        ks = jax.random.split(key, 7)
        B, N, F = (16, 1024, 64)
        s = 1.0 / np.sqrt(F)
        return {'x': jax.random.normal(ks[0], (B, N, F), dtype=jnp.float32), 'Wq': jax.random.normal(ks[1], (F, F), dtype=jnp.float32) * s, 'bq': jax.random.normal(ks[2], (F,), dtype=jnp.float32) * s, 'Wk': jax.random.normal(ks[3], (F, F), dtype=jnp.float32) * s, 'bk': jax.random.normal(ks[4], (F,), dtype=jnp.float32) * s, 'Wv': jax.random.normal(ks[5], (F, F), dtype=jnp.float32) * s, 'bv': jax.random.normal(ks[6], (F,), dtype=jnp.float32) * s}
    _L3_attn_all = _L3_attn_setup()
    _L3_attn_in = {k: v for k, v in _L3_attn_all.items() if k in ('Wq', 'bq', 'Wk', 'bk', 'Wv', 'bv')}
    del _L3_attn_all

    def _L3_ffn_setup():
        import jax, jax.numpy as jnp
        import numpy as np
        B, N, D, C, E, K = (8, 4096, 64, 64, 8, 2)
        key = jax.random.key(seed)
        k0, k1, k2 = jax.random.split(key, 3)
        x = jax.random.normal(k0, (B, N, D), dtype=jnp.float32)
        router_w = jax.random.normal(k1, (D, E), dtype=jnp.float32) * 0.05
        router_b = jnp.zeros((E,), dtype=jnp.float32)
        expert_w = jax.random.normal(k2, (E, D, C), dtype=jnp.float32) * (1.0 / np.sqrt(D))
        expert_b = jnp.zeros((E, C), dtype=jnp.float32)
        return {'x': x, 'router_w': router_w, 'router_b': router_b, 'expert_w': expert_w, 'expert_b': expert_b}
    _L3_ffn_all = _L3_ffn_setup()
    _L3_ffn_in = {k: v for k, v in _L3_ffn_all.items() if k in ('router_w', 'router_b', 'expert_w', 'expert_b')}
    del _L3_ffn_all
    return {'x': x, 'L0_conv_ln1_g': _L0_conv_in['ln1_g'], 'L0_conv_ln1_b': _L0_conv_in['ln1_b'], 'L0_conv_qkv_w': _L0_conv_in['qkv_w'], 'L0_conv_qkv_b': _L0_conv_in['qkv_b'], 'L0_conv_proj_w': _L0_conv_in['proj_w'], 'L0_conv_proj_b': _L0_conv_in['proj_b'], 'L0_conv_rpb': _L0_conv_in['rpb'], 'L0_conv_ln2_g': _L0_conv_in['ln2_g'], 'L0_conv_ln2_b': _L0_conv_in['ln2_b'], 'L0_conv_fc1_w': _L0_conv_in['fc1_w'], 'L0_conv_fc1_b': _L0_conv_in['fc1_b'], 'L0_conv_fc2_w': _L0_conv_in['fc2_w'], 'L0_conv_fc2_b': _L0_conv_in['fc2_b'], 'L1_conv_W_left': _L1_conv_in['W_left'], 'L1_conv_b_left': _L1_conv_in['b_left'], 'L1_conv_W_right': _L1_conv_in['W_right'], 'L1_conv_b_right': _L1_conv_in['b_right'], 'L1_conv_W_gate': _L1_conv_in['W_gate'], 'L1_conv_b_gate': _L1_conv_in['b_gate'], 'L1_conv_W_eq': _L1_conv_in['W_eq'], 'L1_conv_b_eq': _L1_conv_in['b_eq'], 'L1_conv_W_out': _L1_conv_in['W_out'], 'L1_conv_b_out': _L1_conv_in['b_out'], 'L1_conv_ln_scale': _L1_conv_in['ln_scale'], 'L1_conv_ln_bias': _L1_conv_in['ln_bias'], 'L2_ffn_gate_w': _L2_ffn_in['gate_w'], 'L2_ffn_gate_b': _L2_ffn_in['gate_b'], 'L2_ffn_weight1': _L2_ffn_in['weight1'], 'L2_ffn_weight2': _L2_ffn_in['weight2'], 'L3_attn_Wq': _L3_attn_in['Wq'], 'L3_attn_bq': _L3_attn_in['bq'], 'L3_attn_Wk': _L3_attn_in['Wk'], 'L3_attn_bk': _L3_attn_in['bk'], 'L3_attn_Wv': _L3_attn_in['Wv'], 'L3_attn_bv': _L3_attn_in['bv'], 'L3_ffn_router_w': _L3_ffn_in['router_w'], 'L3_ffn_router_b': _L3_ffn_in['router_b'], 'L3_ffn_expert_w': _L3_ffn_in['expert_w'], 'L3_ffn_expert_b': _L3_ffn_in['expert_b']}

def reference(x, L0_conv_ln1_g, L0_conv_ln1_b, L0_conv_qkv_w, L0_conv_qkv_b, L0_conv_proj_w, L0_conv_proj_b, L0_conv_rpb, L0_conv_ln2_g, L0_conv_ln2_b, L0_conv_fc1_w, L0_conv_fc1_b, L0_conv_fc2_w, L0_conv_fc2_b, L1_conv_W_left, L1_conv_b_left, L1_conv_W_right, L1_conv_b_right, L1_conv_W_gate, L1_conv_b_gate, L1_conv_W_eq, L1_conv_b_eq, L1_conv_W_out, L1_conv_b_out, L1_conv_ln_scale, L1_conv_ln_bias, L2_ffn_gate_w, L2_ffn_gate_b, L2_ffn_weight1, L2_ffn_weight2, L3_attn_Wq, L3_attn_bq, L3_attn_Wk, L3_attn_bk, L3_attn_Wv, L3_attn_bv, L3_ffn_router_w, L3_ffn_router_b, L3_ffn_expert_w, L3_ffn_expert_b):
    import jax
    import jax.numpy as jnp

    def _L0_conv_ref(x, ln1_g, ln1_b, qkv_w, qkv_b, proj_w, proj_b, rpb, ln2_g, ln2_b, fc1_w, fc1_b, fc2_w, fc2_b):
        import jax, jax.numpy as jnp
        import numpy as np
        W_DIM = 8
        SHIFT = 4
        HEADS = 4

        def _rel_pos_index(w):
            coords = np.stack(np.meshgrid(np.arange(w), np.arange(w), indexing='ij'))
            flat = coords.reshape(2, -1)
            rel = flat[:, :, None] - flat[:, None, :]
            rel = rel.transpose(1, 2, 0) + (w - 1)
            return rel[..., 0] * (2 * w - 1) + rel[..., 1]

        def _shift_mask(H, W, w, s):
            img = np.zeros((H, W), dtype=np.int32)
            cnt = 0
            for hs in (slice(0, -w), slice(-w, -s), slice(-s, None)):
                for ws in (slice(0, -w), slice(-w, -s), slice(-s, None)):
                    img[hs, ws] = cnt
                    cnt += 1
            win = img.reshape(H // w, w, W // w, w).transpose(0, 2, 1, 3).reshape(-1, w * w)
            diff = win[:, None, :] - win[:, :, None]
            return np.where(diff != 0, -1000000000.0, 0.0).astype(np.float32)

        def _ln(x, g, b):
            mu = x.mean(-1, keepdims=True)
            var = x.var(-1, keepdims=True)
            return (x - mu) / jnp.sqrt(var + 1e-05) * g + b

        def _window_partition(x, w):
            B, H, W, C = x.shape
            x = x.reshape(B, H // w, w, W // w, w, C).transpose(0, 1, 3, 2, 4, 5)
            return x.reshape(-1, w * w, C)

        def _window_reverse(win, w, B, H, W):
            C = win.shape[-1]
            x = win.reshape(B, H // w, W // w, w, w, C).transpose(0, 1, 3, 2, 4, 5)
            return x.reshape(B, H, W, C)
        B, H, W, C = x.shape
        w, s, nh = (W_DIM, SHIFT, HEADS)
        hd = C // nh
        N = w * w
        nW = H // w * (W // w)
        h = _ln(x, ln1_g, ln1_b)
        h = jnp.roll(h, (-s, -s), axis=(1, 2))
        win = _window_partition(h, w)
        qkv = win @ qkv_w + qkv_b
        q, k, v = jnp.split(qkv, 3, axis=-1)
        nB = win.shape[0]
        q = q.reshape(nB, N, nh, hd)
        k = k.reshape(nB, N, nh, hd)
        v = v.reshape(nB, N, nh, hd)
        attn = jnp.einsum('bnhd,bmhd->bhnm', q, k) * hd ** (-0.5)
        bias = rpb[jnp.asarray(_rel_pos_index(w))]
        attn = attn + bias.transpose(2, 0, 1)[None]
        mask = jnp.asarray(_shift_mask(H, W, w, s))
        attn = attn.reshape(B, nW, nh, N, N) + mask[None, :, None]
        attn = jax.nn.softmax(attn.reshape(nB, nh, N, N), axis=-1)
        out = jnp.einsum('bhnm,bmhd->bnhd', attn, v).reshape(nB, N, C)
        out = out @ proj_w + proj_b
        out = _window_reverse(out, w, B, H, W)
        out = jnp.roll(out, (s, s), axis=(1, 2))
        x = x + out
        h2 = _ln(x, ln2_g, ln2_b)
        h2 = jax.nn.gelu(h2 @ fc1_w + fc1_b) @ fc2_w + fc2_b
        return x + h2

    def _L1_conv_ref(pair, W_left, b_left, W_right, b_right, W_gate, b_gate, W_eq, b_eq, W_out, b_out, ln_scale, ln_bias):
        import jax, jax.numpy as jnp
        import numpy as np
        LN_EPS = 1e-05

        def _layer_norm(x, scale, bias):
            mu = jnp.mean(x, axis=-1, keepdims=True)
            var = jnp.mean(jnp.square(x - mu), axis=-1, keepdims=True)
            return (x - mu) * jax.lax.rsqrt(var + LN_EPS) * scale + bias
        left = pair @ W_left + b_left
        right = pair @ W_right + b_right
        gate = jax.nn.sigmoid(pair @ W_gate + b_gate)
        left = left + (pair @ W_eq + b_eq)
        right_sum = jnp.sum(right, axis=2, keepdims=True)
        out = left * right_sum
        out = out * gate
        out = out @ W_out + b_out
        return _layer_norm(out + pair, ln_scale, ln_bias)

    def _L2_attn_ref(seq):
        import jax, jax.numpy as jnp
        import numpy as np
        attn = jnp.einsum('blc,bmc->blm', seq, seq)
        attn = jax.nn.softmax(attn, axis=2)
        out = jnp.einsum('blm,bmc->blc', attn, seq)
        return out

    def _L2_ffn_ref(x, gate_w, gate_b, weight1, weight2):
        import jax, jax.numpy as jnp
        import numpy as np
        B, S, D, E, H, O, K = (256, 1024, 64, 32, 256, 64, 8)
        Bn, Sn, Dn = x.shape
        logits = jnp.einsum('bsd,ed->bse', x, gate_w) + gate_b
        probs = jax.nn.softmax(logits, axis=1)
        vals, idx = jax.lax.top_k(probs.transpose(0, 2, 1), K)
        topv = vals.transpose(0, 2, 1)
        topi = idx.transpose(0, 2, 1)
        flat_idx = topi.reshape(Bn, K * E)
        gathered = jnp.take_along_axis(x, flat_idx[:, :, None], axis=1)
        gathered = gathered.reshape(Bn, K, E, Dn)
        pooled = jnp.einsum('bked,bke->bed', gathered, topv)
        ones = jnp.ones((E, Bn, 1), dtype=x.dtype)
        h = jnp.concatenate([pooled.transpose(1, 0, 2), ones], axis=-1)
        h = jax.nn.gelu(jnp.einsum('ebd,edh->ebh', h, weight1), approximate=False)
        h = jnp.concatenate([h, ones], axis=-1)
        out = jnp.einsum('ebh,eho->ebo', h, weight2)
        out = out.transpose(1, 0, 2)
        weighted = jnp.einsum('beo,bke->bkeo', out, topv).reshape(Bn, K * E, O)
        outputs = jnp.zeros((Bn, Sn, O), dtype=x.dtype)
        outputs = outputs.at[jnp.arange(Bn)[:, None], flat_idx].add(weighted)
        return outputs

    def _L3_attn_ref(x, Wq, bq, Wk, bk, Wv, bv):
        import jax, jax.numpy as jnp
        import numpy as np
        TEMP = (2 * 64) ** 0.5
        q = jnp.einsum('bnf,of->bno', x, Wq) + bq
        k = jnp.einsum('bnf,of->bno', x, Wk) + bk
        v = jnp.einsum('bnf,of->bno', x, Wv) + bv
        scores = jnp.einsum('bnf,bmf->bnm', q, k) / TEMP
        alpha = jax.nn.softmax(scores, axis=-1)
        out = jnp.einsum('bnm,bmf->bnf', alpha, v)
        return out

    def _L3_ffn_ref(x, router_w, router_b, expert_w, expert_b):
        import jax, jax.numpy as jnp
        import numpy as np
        B, N, D, C, E, K = (8, 4096, 64, 64, 8, 2)
        router_probs = jax.nn.softmax(x @ router_w + router_b, axis=-1)
        top_p, top_i = jax.lax.top_k(router_probs, K)
        top_p = top_p / jnp.sum(top_p, axis=-1, keepdims=True)
        expert_out = jnp.einsum('bnd,edc->bnec', x, expert_w) + expert_b
        gathered = jnp.take_along_axis(expert_out, top_i[..., None], axis=2)
        return jnp.einsum('bnk,bnkc->bnc', top_p, gathered)

    def _gn(v, G=32, eps=1e-05):
        B_, H_, W_, C_ = v.shape
        g = v.reshape(B_, H_, W_, G, C_ // G)
        m = jnp.mean(g, axis=(1, 2, 4), keepdims=True)
        s = jnp.var(g, axis=(1, 2, 4), keepdims=True)
        return ((g - m) / jnp.sqrt(s + eps)).reshape(v.shape)

    def _ln_c(v, eps=1e-06):
        m = jnp.mean(v, axis=-1, keepdims=True)
        s = jnp.var(v, axis=-1, keepdims=True)
        return (v - m) / jnp.sqrt(s + eps)

    def _ln_t(v, eps=1e-05):
        m = jnp.mean(v, axis=-1, keepdims=True)
        s = jnp.var(v, axis=-1, keepdims=True)
        return (v - m) / jnp.sqrt(s + eps)

    def _to_tokens(v):
        B_, H_, W_, C_ = v.shape
        return v.reshape(B_, H_ * W_, C_)

    def _from_tokens(t, like):
        return t.reshape(like.shape)
    x = _L0_conv_ref(x, L0_conv_ln1_g, L0_conv_ln1_b, L0_conv_qkv_w, L0_conv_qkv_b, L0_conv_proj_w, L0_conv_proj_b, L0_conv_rpb, L0_conv_ln2_g, L0_conv_ln2_b, L0_conv_fc1_w, L0_conv_fc1_b, L0_conv_fc2_w, L0_conv_fc2_b)
    x = _L1_conv_ref(x, L1_conv_W_left, L1_conv_b_left, L1_conv_W_right, L1_conv_b_right, L1_conv_W_gate, L1_conv_b_gate, L1_conv_W_eq, L1_conv_b_eq, L1_conv_W_out, L1_conv_b_out, L1_conv_ln_scale, L1_conv_ln_bias)
    t = _to_tokens(x)
    t = t + _L2_attn_ref(_ln_t(t))
    t = t + _L2_ffn_ref(_ln_t(t), L2_ffn_gate_w, L2_ffn_gate_b, L2_ffn_weight1, L2_ffn_weight2)
    t = t + _L3_attn_ref(_ln_t(t), L3_attn_Wq, L3_attn_bq, L3_attn_Wk, L3_attn_bk, L3_attn_Wv, L3_attn_bv)
    t = t + _L3_ffn_ref(_ln_t(t), L3_ffn_router_w, L3_ffn_router_b, L3_ffn_expert_w, L3_ffn_expert_b)
    x = _from_tokens(t, x)
    return x

_drawn_inputs = setup_inputs


def setup_inputs(seed=0):
    import zlib

    import numpy as np

    out = dict(_drawn_inputs(seed))
    spreads = {'L0_conv_ln1_g': (1.0, 0.6),
     'L0_conv_ln1_b': (0.0, 0.1),
     'L0_conv_qkv_b': (0.0, 0.1),
     'L0_conv_proj_b': (0.0, 0.1),
     'L0_conv_ln2_g': (1.0, 0.564),
     'L0_conv_ln2_b': (0.0, 0.1),
     'L0_conv_fc1_b': (0.0, 0.1),
     'L0_conv_fc2_b': (0.0, 0.1),
     'L1_conv_b_left': (0.0, 0.1),
     'L1_conv_b_right': (0.0, 0.1),
     'L1_conv_b_gate': (0.0, 0.1),
     'L1_conv_b_eq': (0.0, 0.1),
     'L1_conv_b_out': (0.0, 0.1),
     'L1_conv_ln_scale': (1.0, 0.2),
     'L1_conv_ln_bias': (0.0, 0.1),
     'L2_ffn_gate_b': (0.0, 2.0),
     'L3_ffn_router_b': (0.0, 0.1),
     'L3_ffn_expert_b': (0.0, 0.298)}
    factors = {'L0_conv_rpb': 57.625,
     'L2_ffn_gate_w': 8.0,
     'L2_ffn_weight1': 8.0,
     'L2_ffn_weight2': 8.0,
     'L3_attn_bk': 64.0}
    for name, (base, spread) in spreads.items():
        noise = np.random.default_rng([zlib.crc32(name.encode()), seed]).standard_normal(out[name].shape)
        drawn = base * np.exp(spread * noise) if base else spread * noise
        out[name] = jnp.asarray(drawn.astype(out[name].dtype))
    for name, factor in factors.items():
        out[name] = (out[name] * factor).astype(out[name].dtype)
    return out
```

```python
from contextlib import ExitStack

import concourse.bass as bass
from concourse import mybir

ALU = mybir.AluOpType
ACT = mybir.ActivationFunctionType
AX = mybir.AxisListType
F32 = mybir.dt.float32
F16 = mybir.dt.float16

P = 128
B, H, W, C = 32, 32, 32, 64
TOK = H * W
NT = TOK // P
WIN = 8
NW_IMG = (H // WIN) * (W // WIN)
HEADS, HD = 4, C // 4
E2, HID = 32, 256
E3 = 8
FF = 4 * C
GRP = 4
NG = B // GRP
PAIRS = B // 2
WS = 64.0
IWS = 1.0 / WS
TEMP = (2 * C) ** 0.5
SHIFT2 = 55.0

COLS = {}
NWC = 0
for _name, _n in (("q", 2 * C), ("k", 2 * C), ("v", C), ("fc1", FF), ("proj", C), ("left", C), ("gatel", C),
                  ("right", C), ("out", C), ("gate2", E2), ("q3", 2 * C), ("k3", 2 * C), ("v3", C),
                  ("router", E3), ("exp3", E3 * C)):
    COLS[_name] = slice(NWC, NWC + _n)
    NWC += _n
LN1_COLS = slice(0, COLS["v"].stop)
LN2_COLS = COLS["fc1"]

NORM_PARTS = ("sum", "centred", "squared", "sumsq", "var", "rstd", "normed", "high", "pair", "turned", "xT")


def spread(ap, n):
    return ap.unsqueeze(2).to_broadcast([ap.shape[0], ap.shape[1], n])


def over(ap, n):
    return ap.unsqueeze(1).to_broadcast([ap.shape[0], n, ap.shape[1]])


def tiles(ap, a=NT):
    return ap.rearrange("p (a b) -> p a b", a=a)



def norm_sum(nc, ln, n1, src, w):
    nc.vector.tensor_reduce(w["sum"], src, AX.X, ALU.add).then_inc(ln["sum"], 1)


def norm_centre(nc, ln, n1, src, w):
    nc.vector.wait_ge(ln["sum"], n1)
    nc.vector.scalar_tensor_tensor(w["xc"], spread(w["sum"], C), -1.0 / C, src, ALU.mult,
                                   ALU.add).then_inc(ln["centred"], 1)


def norm_square(nc, ln, n1, w):
    nc.scalar.wait_ge(ln["centred"], n1)
    nc.scalar.activation(w["sq"], w["xc"], ACT.Square, scale=C ** -0.5).then_inc(ln["squared"], 1)


def norm_sumsq(nc, ln, n1, w):
    nc.vector.wait_ge(ln["squared"], n1)
    nc.vector.tensor_reduce(w["ss"], w["sq"], AX.X, ALU.add).then_inc(ln["sumsq"], 1)


def norm_rstd(nc, ln, n1, w, nhalf, eps):
    nc.gpsimd.wait_ge(ln["sumsq"], n1)
    nc.gpsimd.tensor_tensor(w["var"], w["ss"], eps, ALU.add).then_inc(ln["var"], 1)
    nc.gpsimd.wait_ge(ln["var"], n1)
    nc.gpsimd.tensor_tensor(w["rstd"], w["var"], nhalf, ALU.pow).then_inc(ln["rstd"], 1)


def norm_apply(nc, ln, n1, w):
    nc.vector.wait_ge(ln["rstd"], n1)
    nc.vector.tensor_tensor(w["xn"], w["xc"], spread(w["rstd"], C), ALU.mult).then_inc(ln["normed"], 1)



def cut_high(nc, ln, n1, w, x):
    nc.scalar.wait_ge(ln["normed"], n1)
    nc.scalar.activation(w["hl"][:, :, 0:C], x, ACT.Identity).then_inc(ln["high"], 1)


def cut_low(nc, ln, n1, w, x):
    nc.vector.wait_ge(ln["high"], n1)
    nc.vector.tensor_tensor(w["hl"][:, :, C:2 * C], x, w["hl"][:, :, 0:C], ALU.subtract).then_inc(ln["pair"], 1)


def turn(nc, ln, n1, w, bank, ident16):
    nc.tensor.wait_ge(ln["pair"], n1)
    for g in range(NT):
        last = nc.tensor.transpose(bank[:, g * P:(g + 1) * P], w["hl"][:, g, 0:2 * C], ident16)
    last.then_inc(ln["turned"], 1)


def take_turned(nc, ln, n1, w, bank):
    nc.vector.wait_ge(ln["turned"], n1)
    nc.vector.tensor_copy(w["xT"], bank).then_inc(ln["xT"], 1)


def turn_to_windows(nc, ln, n1, w, bank, perm):
    nc.tensor.wait_ge(ln["pair"], n1)
    for g in range(NT):
        half = (g + NT - 1) % NT
        at = (half // 2) * 4 * WIN * WIN + (half % 2) * WIN * WIN // 2
        out = bank.rearrange("p (w t) -> p w t", t=WIN * WIN)[:, at // 64:at // 64 + 4, at % 64:at % 64 + 32]
        last = nc.tensor.transpose(out, w["hl"][:, g, 0:2 * C], perm)
    last.then_inc(ln["turned"], 1)


def turn_from_windows(nc, ln, n1, w, bank, perm):
    nc.tensor.wait_ge(ln["pair"], n1)
    for g in range(NT):
        rows = bank.rearrange("p (r c) -> p r c", c=W)[:, WIN * (g // 2):WIN * (g // 2) + WIN,
                                                       16 * (g % 2):16 * (g % 2) + 16]
        last = nc.tensor.transpose(rows, w["hl"][:, g, 0:2 * C], perm)
    last.then_inc(ln["turned"], 1)


def take_unrolled(nc, ln, n1, w, bank):
    nc.vector.wait_ge(ln["turned"], n1)
    s, image = WIN // 2, w["xT"].rearrange("p (r c) -> p r c", c=W)
    rolled = bank.rearrange("p (r c) -> p r c", c=W)
    for r0, r1, to_r in ((0, H - s, s), (H - s, H, 0)):
        for c0, c1, to_c in ((0, W - s, s), (W - s, W, 0)):
            last = nc.vector.tensor_copy(image[:, to_r:to_r + r1 - r0, to_c:to_c + c1 - c0], rolled[:, r0:r1, c0:c1])
    last.then_inc(ln["xT"], 1)


class Net:
    pass


def work_buffers(sb, name):
    w = {}
    for k, shape, dt in (("sum", [P, NT], F32), ("ss", [P, NT], F32), ("var", [P, NT], F32), ("rstd", [P, NT], F32),
                         ("xc", [P, NT, C], F32), ("sq", [P, NT, C], F32), ("xn", [P, NT, C], F32),
                         ("hl", [P, NT, 3 * C], F16), ("xT", [P, TOK], F16)):
        w[k] = sb(f"{name}_{k}", shape, dt)[:]
    return w


def stage_setup(net, d, k):
    nc, sem = net.nc, net.sem
    with ExitStack() as ctx:
        def sb(name, shape, dt):
            return ctx.enter_context(nc.sbuf_tensor("su_" + name, shape, dt))

        wc = sb("wc", [P, NWC], F32)
        wh = sb("wh", [P, NWC], F16)
        wl = sb("wl", [P, NWC], F16)
        weq = sb("weq", [P, C], F32)
        raw3 = sb("raw3", [C, 3, 2, C], F32)
        rawg = sb("rawg", [E2, 2, C], F32)
        gains = sb("gains", [P, 2], F32)
        lnb = sb("lnb", [C, 2, 2], F32)
        brf = sb("brf", [2, NWC + C], F32)
        beq = sb("beq", [2, C], F32)
        bh = sb("bh", [2, NWC + C], F16)
        bl = sb("bl", [2, NWC + C], F16)
        fc2 = sb("fc2", [P, 2, C], F32)
        rb = sb("rb", [P, C, HEADS], F32)
        mask = sb("mask", [P, 2, 2, C], F32)
        same = sb("same", [P, P], F32)
        perms = sb("perms", [P, 2, P], F32)
        ps_t = ctx.enter_context(nc.psum_tensor("su_ps_t", [P, 512], F32))
        ps_b = ctx.enter_context(nc.psum_tensor("su_ps_b", [2, 512], F32))
        ps_c = ctx.enter_context(nc.psum_tensor("su_ps_c", [2, 512], F32))

        loaded, chain = sem("setup_loaded"), sem("setup_chain")
        turned, folded = sem("setup_turned"), sem("setup_folded")
        b_loaded, doubled, paired = sem("setup_b_loaded"), sem("setup_doubled"), sem("setup_paired")
        raw_doubled = sem("setup_raw_doubled")
        ndma, nb = [0], [0]

        with nc.Block() as block:
            @block.sync
            def _(sp):
                def load(dst, src):
                    sp.dma_start(dst, src).then_inc(loaded, 16)
                    ndma[0] += 1

                load(net.ident[:], k["ident"])
                load(net.hmask[:], k["hmask"])
                load(perms[:, 0], k["to_windows"])
                load(perms[:, 1], k["from_windows"])
                load(same[:], k["samerow"])
                load(mask[:], k["mask"])
                pieces = [("q", 2 * C, d["L0_conv_qkv_w"]), ("fc1", 0, d["L0_conv_fc1_w"]),
                          ("proj", 0, d["L0_conv_proj_w"]), ("left", 0, d["L1_conv_W_left"]),
                          ("gatel", 0, d["L1_conv_W_gate"]), ("right", 0, d["L1_conv_W_right"]),
                          ("out", 0, d["L1_conv_W_out"]), ("router", 0, d["L3_ffn_router_w"])]
                for name, at, src in pieces:
                    a = COLS[name].start + at
                    load(wc[0:C, a:a + src.shape[1]], src)
                load(wc[0:C, COLS["exp3"]].rearrange("p (e c) -> p e c", e=E3),
                     d["L3_ffn_expert_w"].rearrange("e d c -> d e c"))
                load(weq[0:C, :], d["L1_conv_W_eq"])
                for half in (0, C):
                    load(gains[half:half + C, 0:1], d["L0_conv_ln1_g"].unsqueeze(1))
                    load(gains[half:half + C, 1:2], d["L0_conv_ln2_g"].unsqueeze(1))
                for j, name in enumerate(("L3_attn_Wq", "L3_attn_Wk", "L3_attn_Wv")):
                    load(raw3[:, j, 0, :], d[name])
                load(rawg[:, 0, :], d["L2_ffn_gate_w"])
                load(lnb[:, 0, 0:1], d["L0_conv_ln1_b"].unsqueeze(1))
                load(lnb[:, 1, 0:1], d["L0_conv_ln2_b"].unsqueeze(1))
                load(fc2[:], d["L0_conv_fc2_w"].rearrange("(a p) n -> p a n", a=2))
                load(net.lns[:], d["L1_conv_ln_scale"].unsqueeze(0).to_broadcast([P, C]))
                load(net.lnb[:], d["L1_conv_ln_bias"].unsqueeze(0).to_broadcast([P, C]))
                table = d["L0_conv_rpb"]
                side = 2 * WIN - 1
                for w2 in range(2):
                    for kr in range(WIN):
                        src = bass.AP(table.tensor, table.offset + side * HEADS * kr,
                                      [[side * HEADS, WIN], [HEADS, WIN], [1, WIN * HEADS]])
                        load(rb[64 * w2:64 * w2 + 64, WIN * kr:WIN * kr + WIN, :].rearrange("p k h -> p (k h)"), src)
                sp.wait_ge(paired, 1)
                sp.dma_start(wc[C:P, :], wc[0:C, :]).then_inc(doubled, 16)
                sp.dma_start(brf[1:2, :], brf[0:1, :]).then_inc(doubled, 16)

            @block.gpsimd
            def _(pool):
                qb = d["L0_conv_qkv_b"]
                rows = [("q", 2 * C, qb), ("fc1", 0, d["L0_conv_fc1_b"]), ("proj", 0, d["L0_conv_proj_b"]),
                        ("left", 0, d["L1_conv_b_left"]), ("gatel", 0, d["L1_conv_b_gate"]),
                        ("right", 0, d["L1_conv_b_right"]), ("out", 0, d["L1_conv_b_out"]),
                        ("gate2", 0, d["L2_ffn_gate_b"]), ("q3", 0, d["L3_attn_bq"]),
                        ("k3", 0, d["L3_attn_bk"]), ("v3", 0, d["L3_attn_bv"]),
                        ("router", 0, d["L3_ffn_router_b"]),
                        ("exp3", 0, d["L3_ffn_expert_b"].rearrange("e c -> (e c)"))]
                for name, at, src in rows:
                    a = COLS[name].start + at
                    pool.dma_start(brf[0:1, a:a + src.shape[0]], src.unsqueeze(0)).then_inc(b_loaded, 16)
                pool.dma_start(brf[0:1, NWC:NWC + C], d["L0_conv_fc2_b"].unsqueeze(0)).then_inc(b_loaded, 16)
                pool.dma_start(beq[0:1, :], d["L1_conv_b_eq"].unsqueeze(0)).then_inc(b_loaded, 16)
                nb[0] = len(rows) + 2

            @block.vector
            def _(dve):
                done = [0]

                def link(ins):
                    done[0] += 1
                    ins.then_inc(chain, 1)
                    dve.wait_ge(chain, done[0])

                nc.vector.memset(net.nhalf[:], -0.5)
                nc.vector.memset(net.eps[:], 1e-5)
                nc.vector.memset(net.ones16[:], 1.0)
                dve.wait_ge(loaded, 16 * ndma[0])
                nc.vector.tensor_copy(net.ident16[:], net.ident[:])
                nc.vector.tensor_copy(net.same16[:], same[:])
                nc.vector.tensor_copy(net.perm16[:], perms[:])
                dve.wait_ge(b_loaded, 16 * nb[0])
                nc.vector.tensor_copy(raw3[:, :, 1, :], raw3[:, :, 0, :])
                nc.vector.tensor_copy(rawg[:, 1, :], rawg[:, 0, :])
                link(nc.vector.tensor_copy(lnb[:, :, 1:2], lnb[:, :, 0:1]))
                nc.vector.engine_nop().then_inc(raw_doubled, 1)
                q, k_, v_ = COLS["q"].start, COLS["k"].start, COLS["v"].start
                for tensor in (wc[0:C, :], brf[0:1, :]):
                    link(nc.vector.tensor_copy(tensor[:, q:q + C], tensor[:, q + 2 * C:q + 3 * C]))
                    link(nc.vector.tensor_copy(tensor[:, q + C:q + 2 * C], tensor[:, q:q + C]))
                    link(nc.vector.tensor_copy(tensor[:, k_:k_ + C], tensor[:, k_ + C:k_ + 2 * C]))
                link(nc.vector.tensor_tensor(wc[0:C, COLS["left"]], wc[0:C, COLS["left"]], weq[0:C, :], ALU.add))
                link(nc.vector.tensor_tensor(brf[0:1, COLS["left"]], brf[0:1, COLS["left"]], beq[0:1, :], ALU.add))
                for name in ("q3", "k3"):
                    a = COLS[name].start
                    link(nc.vector.tensor_copy(brf[0:1, a + C:a + 2 * C], brf[0:1, a:a + C]))
                dve.wait_ge(turned, 1)
                for j, name in enumerate(("q3", "k3")):
                    for r in range(2):
                        a = COLS[name].start + r * C
                        nc.vector.tensor_copy(wc[0:C, a:a + C], ps_t[0:C, j * C:(j + 1) * C])
                nc.vector.tensor_copy(wc[0:C, COLS["v3"]], ps_t[0:C, 2 * C:3 * C])
                nc.vector.tensor_copy(wc[0:C, COLS["gate2"]], ps_t[0:C, 3 * C:3 * C + E2]).then_inc(paired, 1)
                dve.wait_ge(doubled, 32)
                dve.wait_ge(folded, 1)
                link(nc.vector.tensor_tensor(brf[:, LN1_COLS], brf[:, LN1_COLS], ps_b[:, LN1_COLS], ALU.add))
                link(nc.vector.tensor_tensor(brf[:, LN2_COLS], brf[:, LN2_COLS], ps_c[:, 0:FF], ALU.add))
                link(nc.vector.tensor_scalar(brf[:], brf[:], WS, None, ALU.mult))
                link(nc.vector.tensor_copy(bh[:], brf[:]))
                link(nc.vector.tensor_tensor(bl[:], brf[:], bh[:], ALU.subtract))
                link(nc.vector.tensor_scalar(bh[:], bh[:], net.ident[0:2, 0:1], None, ALU.mult))
                link(nc.vector.scalar_tensor_tensor(net.bias[:], bl[:], net.ident[0:2, 1:2], bh[:], ALU.mult,
                                                    ALU.add))
                link(nc.vector.tensor_scalar(wc[:, LN1_COLS], wc[:, LN1_COLS], gains[:, 0:1], WS, ALU.mult, ALU.mult))
                link(nc.vector.tensor_scalar(wc[:, LN2_COLS], wc[:, LN2_COLS], gains[:, 1:2], WS, ALU.mult, ALU.mult))
                rest = slice(LN2_COLS.stop, NWC)
                link(nc.vector.tensor_scalar(wc[:, rest], wc[:, rest], WS, None, ALU.mult))
                link(nc.vector.tensor_copy(wh[:], wc[:]))
                link(nc.vector.tensor_tensor(wl[:], wc[:], wh[:], ALU.subtract))
                nc.vector.tensor_copy(net.wa[0:C, :], wh[0:C, :])
                nc.vector.tensor_copy(net.wa[C:P, :], wl[C:P, :])
                nc.vector.tensor_copy(net.wb[0:C, :], wl[0:C, :])
                nc.vector.tensor_copy(net.wb[C:P, :], wh[C:P, :])
                link(nc.vector.tensor_scalar(fc2[:], fc2[:], WS, None, ALU.mult))
                link(nc.vector.tensor_copy(net.fc2h[:], fc2[:]))
                nc.vector.tensor_tensor(net.fc2l[:], fc2[:], net.fc2h[:], ALU.subtract)
                for last_row in range(2):
                    for jp in range(2):
                        back = rb[:].rearrange("p (r c) h -> p h r c", r=WIN)[:, :, ::-1, ::-1]
                        for hd in range(HEADS):
                            nc.vector.tensor_tensor(
                                net.sbias[:, last_row, jp, hd].rearrange("p (r c) -> p r c", c=WIN), back[:, hd],
                                mask[:, last_row, jp].rearrange("p (r c) -> p r c", c=WIN), ALU.add)

            @block.tensor
            def _(pe):
                pe.wait_ge(loaded, 16 * ndma[0])
                pe.wait_ge(raw_doubled, 1)
                for j in range(3):
                    nc.tensor.transpose(ps_t[:, j * C:(j + 1) * C], raw3[:, j].rearrange("p r c -> p (r c)"),
                                        net.ident[0:C, 0:C])
                nc.tensor.transpose(ps_t[:, 3 * C:3 * C + E2], rawg[:].rearrange("p r c -> p (r c)"),
                                    net.ident[0:E2, 0:E2]).then_inc(turned, 1)
                pe.wait_ge(doubled, 32)
                nc.tensor.matmul(ps_b[:, LN1_COLS], lnb[:, 0, :], wc[0:C, LN1_COLS], start=True, stop=True)
                nc.tensor.matmul(ps_c[:, 0:FF], lnb[:, 1, :], wc[0:C, LN2_COLS], start=True,
                                 stop=True).then_inc(folded, 1)


def matmul_pair(nc, out, lhsT, rhs_a, rhs_b, bias_l, bias_r, stop=True):
    nc.tensor.matmul(out, lhsT, rhs_a, start=True, stop=False)
    nc.tensor.matmul(out, lhsT, rhs_b, start=False, stop=False)
    return nc.tensor.matmul(out, bias_l, bias_r, start=False, stop=stop)


def natural(nc, net, out, xT, g, name):
    c = COLS[name]
    return matmul_pair(nc, out, xT[:, g * P:(g + 1) * P], net.wa[:, c], net.wb[:, c], net.ones16[:, 0:P],
                       net.bias[:, c])


def upright(nc, net, out, xT, c, lo, hi):
    nc.tensor.matmul(out, net.wa[:, c], xT[:, lo:hi], start=True, stop=False)
    nc.tensor.matmul(out, net.wb[:, c], xT[:, lo:hi], start=False, stop=False)
    return nc.tensor.matmul(out, net.bias[:, c], net.ones16[:, 0:hi - lo], start=False, stop=True)


def stage_blocks(net, x):
    nc, sem = net.nc, net.sem
    with ExitStack() as ctx:
        def sb(name, shape, dt):
            return ctx.enter_context(nc.sbuf_tensor("bl_" + name, shape, dt))

        wk, qx, kh, kl, kxh, kxl, vh, vl, att, pth, ptl, rs, rinv, on, x1, x2 = ([] for _ in range(16))
        gel, glh, gll, rh, rl, rss, th, u = ([] for _ in range(8))
        for h in range(2):
            wk.append(work_buffers(sb, f"w{h}"))
            qx.append(sb(f"qx{h}", [P, TOK], F16))
            kh.append(sb(f"kh{h}", [P, TOK], F16))
            kl.append(sb(f"kl{h}", [P, TOK], F16))
            kxh.append(sb(f"kxh{h}", [P, HEADS, TOK], F16))
            kxl.append(sb(f"kxl{h}", [P, HEADS, TOK], F16))
            vh.append(sb(f"vh{h}", [P, NW_IMG, 2, 2, HD], F16))
            vl.append(sb(f"vl{h}", [P, NW_IMG, 2, 2, HD], F16))
            att.append(sb(f"att{h}", [P, 2, 2, HEADS, C], F32))
            pth.append(sb(f"pth{h}", [P, 2, 4, P], F16))
            ptl.append(sb(f"ptl{h}", [P, 2, 4, P], F16))
            rs.append(sb(f"rs{h}", [P, NT, HEADS], F32))
            rinv.append(sb(f"rinv{h}", [P, NT, HEADS], F32))
            on.append(sb(f"on{h}", [P, NT, C], F32))
            x1.append(sb(f"x1{h}", [P, NT, C], F32))
            x2.append(sb(f"x2{h}", [P, NT, C], F32))
            gel.append(kxh[h][:].rearrange("p a b -> p (a b)").bitcast(F32).rearrange("p (a b) -> p a b", a=2))
            glh.append(kxl[h][:, 0:2, :])
            gll.append(kxl[h][:, 2:4, :])
            rh.append(sb(f"rh{h}", [P, NT, C], F16))
            rl.append(sb(f"rl{h}", [P, NT, C], F16))
            rss.append(sb(f"rss{h}", [P, NT, C], F32))
            th.append(sb(f"th{h}", [P, NT, C], F32))
            u.append(sb(f"u{h}", [P, NT, C], F32))
        ps = ctx.enter_context(nc.psum_tensor("bl_ps", [P, 8, 512], F32))

        def bank(h, j, n=1):
            return ps[:, 4 * h + j:4 * h + j + n, :].rearrange("p b n -> p (b n)")

        def bank16(h, j):
            return ps[:, 4 * h + j, :].bitcast(F16)

        ln1, ln2, ln3 = net.norms
        co, cx, cu = net.cuts
        x_loaded = sem("x_loaded")
        q_ready, q_taken, kh_taken, kl_taken, k_spread = (sem("bl_" + s) for s in (
            "q_projected", "qh_taken", "kh_taken", "kl_taken", "k_spread"))
        k_ready, ql_taken, v_ready, vh_taken, v_taken = (sem("bl_" + s) for s in (
            "k_projected", "q_taken", "v_projected", "vh_taken", "v_taken"))
        scored, biased, maxed, shifted, exped, summed = (sem("bl_" + s) for s in (
            "scored", "biased", "maxed", "shifted", "exped", "summed"))
        p_turned, ph_taken, pl_taken, weighed, inverted = (sem("bl_" + s) for s in (
            "p_turned", "ph_taken", "pl_taken", "weighed", "inverted"))
        projected, hid_ready, gelued, gh_cut, gl_cut, ffn_out = (sem("bl_" + s) for s in (
            "projected", "hid_ready", "gelued", "gh_cut", "gl_cut", "ffn_out"))
        x2_done, r_ready, rh_taken, rl_taken, lg_ready, rowsummed = (sem("bl_" + s) for s in (
            "x2_done", "r_ready", "rh_taken", "rl_taken", "lg_ready", "rowsummed"))
        rss_taken, tanhed, lefted, outed, scaled, zeroed = (sem("bl_" + s) for s in (
            "rss_taken", "tanhed", "lefted", "outed", "scaled", "zeroed"))
        stored = net.t_ready

        tv = net.t[:].rearrange("p (i h) g c -> p i h g c", h=2)
        tp, xv = pairs_of_tiles(net.t, x)

        with nc.Block() as block:
            @block.sync
            def _(sp):
                sp.dma_start(tp[:, 0], xv[:, 0]).then_inc(x_loaded, 16)
                with sp.Fori(1, PAIRS) as i:
                    sp.wait_ge(x_loaded, 16 * i)
                    sp.dma_start(tp[:, i], xv[:, i]).then_inc(x_loaded, 16)

            @block.vector
            def _(dve):
                for h in range(2):
                    nc.vector.memset(vh[h][:], 0.0)
                    nc.vector.memset(vl[h][:], 0.0).then_inc(zeroed, 1)
                with dve.Fori(0, PAIRS) as i:
                    def n1(h):
                        return 2 * i + h + 1

                    def m1(h, c):
                        return 8 * i + 2 * c + h + 1

                    dve.wait_ge(x_loaded, 16 * (i + 1))
                    for h in range(2):
                        norm_sum(nc, ln1, n1(h), tv[:, i, h], wk[h])
                    for h in range(2):
                        norm_centre(nc, ln1, n1(h), tv[:, i, h], wk[h])
                    for h in range(2):
                        norm_sumsq(nc, ln1, n1(h), wk[h])
                    for h in range(2):
                        norm_apply(nc, ln1, n1(h), wk[h])
                    for h in range(2):
                        cut_low(nc, ln1, n1(h), wk[h], wk[h]["xn"])
                    for h in range(2):
                        take_turned(nc, ln1, n1(h), wk[h], bank16(h, 0))
                    for h in range(2):
                        dve.wait_ge(q_taken, n1(h))
                        nc.vector.scalar_tensor_tensor(qx[h][C:P, :], bank(h, 0, 2)[C:P, :], IWS, qx[h][C:P, :],
                                                       ALU.mult, ALU.subtract).then_inc(ql_taken, 1)
                        dve.wait_ge(kh_taken, n1(h))
                        nc.vector.scalar_tensor_tensor(kl[h][:], bank(h, 2, 2), IWS, kh[h][:],
                                                       ALU.mult, ALU.subtract).then_inc(kl_taken, 1)
                    for h in range(2):
                        dve.wait_ge(kl_taken, n1(h))
                        for hd in range(HEADS):
                            nc.vector.tensor_scalar(kxh[h][:, hd, :], kh[h][:], net.hmask[:, hd:hd + 1], None, ALU.mult)
                            last = nc.vector.tensor_scalar(kxl[h][:, hd, :], kl[h][:], net.hmask[:, hd:hd + 1], None,
                                                           ALU.mult)
                        last.then_inc(k_spread, 1)
                    dve.wait_ge(zeroed, 2)
                    for h in range(2):
                        dve.wait_ge(vh_taken, n1(h))
                        for hp in range(2):
                            half = slice(C * hp, C * hp + C)
                            last = nc.vector.scalar_tensor_tensor(
                                vl[h][half, :, :, hp, :].rearrange("p w a d -> p (w a) d"),
                                bank(h, 0)[half, :].rearrange("p (w d) -> p w d", d=HD), IWS,
                                vh[h][half, :, :, hp, :].rearrange("p w a d -> p (w a) d"), ALU.mult, ALU.subtract)
                        last.then_inc(v_taken, 1)
                    for c in range(5):
                        for h in range(2):
                            if c < 4:
                                a = att[h][:, c % 2].rearrange("p t a k -> p (t a) k")
                                dve.wait_ge(scored, m1(h, c))
                                if c >= 2:
                                    dve.wait_ge(pl_taken, m1(h, c - 2))
                                nc.vector.scalar_tensor_tensor(
                                    a, tiles(bank(h, c % 2)), HD ** -0.5,
                                    net.sbias[:, int(c == 3)].rearrange("p t a k -> p (t a) k"),
                                    ALU.mult, ALU.add).then_inc(biased, 1)
                                dve.wait_ge(biased, m1(h, c))
                                nc.vector.tensor_reduce(wk[h]["sum"], a, AX.X, ALU.max).then_inc(maxed, 1)
                                dve.wait_ge(maxed, m1(h, c))
                                nc.vector.tensor_tensor(a, a, spread(wk[h]["sum"], C),
                                                        ALU.subtract).then_inc(shifted, 1)
                            if c >= 1:
                                a = att[h][:, (c - 1) % 2].rearrange("p t a k -> p (t a) k")
                                dve.wait_ge(exped, m1(h, c - 1))
                                nc.vector.tensor_reduce(rs[h][:, 2 * c - 2:2 * c].rearrange("p t a -> p (t a)"), a,
                                                        AX.X, ALU.add).then_inc(summed, 1)
                                dve.wait_ge(ph_taken, m1(h, c - 1))
                                nc.vector.tensor_tensor(ptl[h][:, (c - 1) % 2], tiles(bank(h, 2), 4),
                                                        pth[h][:, (c - 1) % 2], ALU.subtract).then_inc(pl_taken, 1)
                    for h in range(2):
                        dve.wait_ge(summed, m1(h, 3))
                        nc.vector.reciprocal(rinv[h][:], rs[h][:]).then_inc(inverted, 1)
                        dve.wait_ge(inverted, n1(h))
                        dve.wait_ge(weighed, m1(h, 3))
                        nc.vector.tensor_tensor(
                            on[h][:].rearrange("p t (a d) -> p (t a) d", a=HEADS),
                            bank(h, 3).rearrange("p (ta d) -> p ta d", d=HD),
                            spread(rinv[h][:].rearrange("p t a -> p (t a)"), HD), ALU.mult).then_inc(co["normed"], 1)
                    for h in range(2):
                        cut_low(nc, co, n1(h), wk[h], on[h][:])
                    for h in range(2):
                        take_unrolled(nc, co, n1(h), wk[h], bank16(h, 0))
                    for h in range(2):
                        dve.wait_ge(projected, n1(h))
                        nc.vector.scalar_tensor_tensor(x1[h][:], tiles(bank(h, 1)), IWS, tv[:, i, h],
                                                       ALU.mult, ALU.add).then_inc(stored["x1"], 1)
                    for h in range(2):
                        dve.wait_ge(stored["x1"], n1(h))
                        norm_sum(nc, ln2, n1(h), x1[h][:], wk[h])
                    for h in range(2):
                        norm_centre(nc, ln2, n1(h), x1[h][:], wk[h])
                    for h in range(2):
                        norm_sumsq(nc, ln2, n1(h), wk[h])
                    for h in range(2):
                        norm_apply(nc, ln2, n1(h), wk[h])
                    for h in range(2):
                        cut_low(nc, ln2, n1(h), wk[h], wk[h]["xn"])
                    for h in range(2):
                        take_turned(nc, ln2, n1(h), wk[h], bank16(h, 0))
                    for h in range(2):
                        for a in range(2):
                            dve.wait_ge(gelued, 4 * i + 2 * h + a + 1)
                            nc.vector.tensor_copy(glh[h][:, a], gel[h][:, a]).then_inc(gh_cut, 1)
                    for h in range(2):
                        dve.wait_ge(ffn_out, n1(h))
                        nc.vector.scalar_tensor_tensor(x2[h][:], tiles(bank(h, 2)), IWS, x1[h][:],
                                                       ALU.mult, ALU.add).then_inc(cx["normed"], 1)
                    for h in range(2):
                        cut_low(nc, cx, n1(h), wk[h], x2[h][:])
                    for h in range(2):
                        take_turned(nc, cx, n1(h), wk[h], bank16(h, 0))
                    for h in range(2):
                        dve.wait_ge(rh_taken, n1(h))
                        nc.vector.scalar_tensor_tensor(rl[h][:], tiles(bank(h, 1)), IWS, rh[h][:],
                                                       ALU.mult, ALU.subtract).then_inc(rl_taken, 1)
                    for h in range(2):
                        dve.wait_ge(rss_taken, n1(h))
                        dve.wait_ge(lg_ready, n1(h))
                        nc.vector.tensor_tensor(u[h][:], tiles(bank(h, 2)), rss[h][:], ALU.mult).then_inc(lefted, 1)
                        dve.wait_ge(lefted, n1(h))
                        dve.wait_ge(tanhed, n1(h))
                        nc.vector.scalar_tensor_tensor(u[h][:], th[h][:], 1.0, u[h][:], ALU.add,
                                                       ALU.mult).then_inc(cu["normed"], 1)
                    for h in range(2):
                        cut_low(nc, cu, n1(h), wk[h], u[h][:])
                    for h in range(2):
                        take_turned(nc, cu, n1(h), wk[h], bank16(h, 1))
                    for h in range(2):
                        dve.wait_ge(outed, n1(h))
                        nc.vector.scalar_tensor_tensor(x1[h][:], tiles(bank(h, 2)), IWS, x2[h][:],
                                                       ALU.mult, ALU.add).then_inc(stored["y"], 1)
                    for h in range(2):
                        dve.wait_ge(stored["y"], n1(h))
                        norm_sum(nc, ln3, n1(h), x1[h][:], wk[h])
                    for h in range(2):
                        norm_centre(nc, ln3, n1(h), x1[h][:], wk[h])
                    for h in range(2):
                        norm_sumsq(nc, ln3, n1(h), wk[h])
                    for h in range(2):
                        norm_apply(nc, ln3, n1(h), wk[h])
                    for h in range(2):
                        dve.wait_ge(ln3["normed"], n1(h))
                        nc.vector.tensor_tensor(on[h][:], wk[h]["xn"], over(net.lns[:], NT), ALU.mult).then_inc(scaled, 1)
                    for h in range(2):
                        dve.wait_ge(scaled, n1(h))
                        nc.vector.tensor_tensor(tv[:, i, h], on[h][:], over(net.lnb[:], NT),
                                                ALU.add).then_inc(stored["t"], 1)

            @block.scalar
            def _(act):
                with act.Fori(0, PAIRS) as i:
                    def n1(h):
                        return 2 * i + h + 1

                    def m1(h, c):
                        return 8 * i + 2 * c + h + 1

                    for h in range(2):
                        norm_square(nc, ln1, n1(h), wk[h])
                    for h in range(2):
                        cut_high(nc, ln1, n1(h), wk[h], wk[h]["xn"])
                    for h in range(2):
                        act.wait_ge(q_ready, n1(h))
                        nc.scalar.activation(qx[h][:], bank(h, 0, 2), ACT.Copy, scale=IWS).then_inc(q_taken, 1)
                        act.wait_ge(k_ready, n1(h))
                        nc.scalar.activation(kh[h][:], bank(h, 2, 2), ACT.Copy, scale=IWS).then_inc(kh_taken, 1)
                    act.wait_ge(zeroed, 2)
                    for h in range(2):
                        act.wait_ge(v_ready, n1(h))
                        for hp in range(2):
                            half = slice(C * hp, C * hp + C)
                            last = nc.scalar.activation(
                                vh[h][half, :, :, hp, :].rearrange("p w a d -> p (w a) d"),
                                bank(h, 0)[half, :].rearrange("p (w d) -> p w d", d=HD), ACT.Copy, scale=IWS)
                        last.then_inc(vh_taken, 1)
                    for c in range(4):
                        for h in range(2):
                            a = att[h][:, c % 2].rearrange("p t a k -> p (t a k)")
                            act.wait_ge(shifted, m1(h, c))
                            nc.scalar.activation(a, a, ACT.Exp).then_inc(exped, 1)
                        for h in range(2):
                            act.wait_ge(p_turned, m1(h, c))
                            nc.scalar.activation(pth[h][:, c % 2], tiles(bank(h, 2), 4), ACT.Copy).then_inc(ph_taken, 1)
                    for h in range(2):
                        cut_high(nc, co, n1(h), wk[h], on[h][:])
                    for h in range(2):
                        norm_square(nc, ln2, n1(h), wk[h])
                    for h in range(2):
                        cut_high(nc, ln2, n1(h), wk[h], wk[h]["xn"])
                    for h in range(2):
                        for a in range(2):
                            act.wait_ge(hid_ready, 4 * i + 2 * h + a + 1)
                            nc.scalar.activation(gel[h][:, a], bank(h, 2 - 2 * a, 2), ACT.Gelu_apprx_tanh,
                                                 scale=IWS).then_inc(gelued, 1)
                    for h in range(2):
                        cut_high(nc, cx, n1(h), wk[h], x2[h][:])
                    for h in range(2):
                        act.wait_ge(r_ready, n1(h))
                        nc.scalar.activation(rh[h][:], tiles(bank(h, 1)), ACT.Copy, scale=IWS).then_inc(rh_taken, 1)
                    for h in range(2):
                        act.wait_ge(lg_ready, n1(h))
                        nc.scalar.activation(th[h][:], tiles(bank(h, 3)), ACT.Tanh, scale=0.5 * IWS).then_inc(tanhed, 1)
                        act.wait_ge(rowsummed, n1(h))
                        nc.scalar.activation(rss[h][:], tiles(bank(h, 0)), ACT.Copy,
                                             scale=0.5 * IWS).then_inc(rss_taken, 1)
                    for h in range(2):
                        cut_high(nc, cu, n1(h), wk[h], u[h][:])
                    for h in range(2):
                        norm_square(nc, ln3, n1(h), wk[h])

            @block.gpsimd
            def _(pool):
                with pool.Fori(0, PAIRS) as i:
                    def n1(h):
                        return 2 * i + h + 1

                    for h in range(2):
                        norm_rstd(nc, ln1, n1(h), wk[h], net.nhalf[:], net.eps[:])
                    for h in range(2):
                        norm_rstd(nc, ln2, n1(h), wk[h], net.nhalf[:], net.eps[:])
                    for h in range(2):
                        for a in range(2):
                            pool.wait_ge(gh_cut, 4 * i + 2 * h + a + 1)
                            nc.gpsimd.tensor_tensor(gll[h][:, a], gel[h][:, a], glh[h][:, a],
                                                    ALU.subtract).then_inc(gl_cut, 1)
                    for h in range(2):
                        norm_rstd(nc, ln3, n1(h), wk[h], net.nhalf[:], net.eps[:])

            @block.tensor
            def _(pe):
                with pe.Fori(0, PAIRS) as i:
                    def n1(h):
                        return 2 * i + h + 1

                    def m1(h, c):
                        return 8 * i + 2 * c + h + 1

                    for h in range(2):
                        turn_to_windows(nc, ln1, n1(h), wk[h], bank16(h, 0), net.perm16[:, 0])
                    for h in range(2):
                        xT = wk[h]["xT"]
                        pe.wait_ge(ln1["xT"], n1(h))
                        for half in range(2):
                            last = upright(nc, net, bank(h, half), xT, COLS["q"], 512 * half, 512 * half + 512)
                        last.then_inc(q_ready, 1)
                        for half in range(2):
                            last = upright(nc, net, bank(h, 2 + half), xT, COLS["k"], 512 * half, 512 * half + 512)
                        last.then_inc(k_ready, 1)
                    for h in range(2):
                        pe.wait_ge(ql_taken, n1(h))
                        for w in range(NW_IMG):
                            for hp in range(2):
                                def heads(ap):
                                    return ap[:, COLS["v"]].rearrange("p (a b d) -> p a b d", a=2, b=2)[:, :, hp, :]
                                last = matmul_pair(nc, bank(h, 0)[C * hp:C * hp + C, 32 * w:32 * w + 32],
                                                   wk[h]["xT"][:, C * w:C * w + C], heads(net.wa), heads(net.wb),
                                                   net.ones16[:, 0:C], heads(net.bias))
                        last.then_inc(v_ready, 1)
                    for c in range(6):
                        for h in range(2):
                            if c < 4:
                                if c == 0:
                                    pe.wait_ge(k_spread, n1(h))
                                    pe.wait_ge(v_taken, n1(h))
                                else:
                                    pe.wait_ge(biased, m1(h, c - 1))
                                for t in range(2):
                                    for w in range(2):
                                        tok = slice((2 * c + t) * P + C * w, (2 * c + t) * P + C * w + C)
                                        out = bank(h, c % 2)[C * w:C * w + C, 256 * t:256 * t + 256]
                                        nc.tensor.matmul(out, qx[h][:, tok], kxh[h][:, :, tok], start=True, stop=False)
                                        last = nc.tensor.matmul(out, qx[h][:, tok], kxl[h][:, :, tok],
                                                                start=False, stop=True)
                                last.then_inc(scored, 1)
                            if 1 <= c < 5:
                                pe.wait_ge(exped, m1(h, c - 1))
                                if c >= 2:
                                    pe.wait_ge(pl_taken, m1(h, c - 2))
                                for j in range(4):
                                    last = nc.tensor.transpose(
                                        bank(h, 2)[:, P * j:P * j + P],
                                        att[h][:, (c - 1) % 2, j // 2, 2 * (j % 2):2 * (j % 2) + 2, :].rearrange(
                                            "p a k -> p (a k)"), net.ident[:])
                                last.then_inc(p_turned, 1)
                            if c >= 2:
                                pe.wait_ge(pl_taken, m1(h, c - 2))
                                for j in range(4):
                                    g, hq = 2 * (c - 2) + j // 2, j % 2
                                    for w in range(2):
                                        out = bank(h, 3)[C * w:C * w + C, C * g + 32 * hq:C * g + 32 * hq + 32]
                                        high = pth[h][:, c % 2, j, C * w:C * w + C]
                                        low = ptl[h][:, c % 2, j, C * w:C * w + C]
                                        v_high = vh[h][:, 2 * g + w, hq].rearrange("p a d -> p (a d)")
                                        v_low = vl[h][:, 2 * g + w, hq].rearrange("p a d -> p (a d)")
                                        nc.tensor.matmul(out, high, v_high, start=True, stop=False)
                                        nc.tensor.matmul(out, high, v_low, start=False, stop=False)
                                        last = nc.tensor.matmul(out, low, v_high, start=False, stop=True)
                                last.then_inc(weighed, 1)
                    for h in range(2):
                        turn_from_windows(nc, co, n1(h), wk[h], bank16(h, 0), net.perm16[:, 1])
                    for h in range(2):
                        pe.wait_ge(co["xT"], n1(h))
                        for g in range(NT):
                            last = natural(nc, net, bank(h, 1)[:, C * g:C * g + C], wk[h]["xT"], g, "proj")
                        last.then_inc(projected, 1)
                    for h in range(2):
                        turn(nc, ln2, n1(h), wk[h], bank16(h, 0), net.ident16[:])
                    for h in range(2):
                        pe.wait_ge(ln2["xT"], n1(h))
                        for a in range(2):
                            c = slice(COLS["fc1"].start + P * a, COLS["fc1"].start + P * a + P)
                            for half in range(2):
                                last = upright(nc, net, bank(h, 2 - 2 * a + half), wk[h]["xT"], c, 512 * half,
                                               512 * half + 512)
                            last.then_inc(hid_ready, 1)
                    for h in range(2):
                        pe.wait_ge(gl_cut, 4 * i + 2 * h + 2)
                        for g in range(NT):
                            out = bank(h, 2)[:, C * g:C * g + C]
                            tok = slice(P * g, P * g + P)
                            nc.tensor.matmul(out, net.ones16[:, 0:P], net.bias[:, NWC:NWC + C], start=True, stop=False)
                            for a in range(2):
                                nc.tensor.matmul(out, glh[h][:, a, tok], net.fc2h[:, a], start=False, stop=False)
                                nc.tensor.matmul(out, glh[h][:, a, tok], net.fc2l[:, a], start=False, stop=False)
                                last = nc.tensor.matmul(out, gll[h][:, a, tok], net.fc2h[:, a], start=False,
                                                        stop=(a == 1))
                        last.then_inc(ffn_out, 1)
                    for h in range(2):
                        turn(nc, cx, n1(h), wk[h], bank16(h, 0), net.ident16[:])
                    for h in range(2):
                        pe.wait_ge(cx["xT"], n1(h))
                        for g in range(NT):
                            last = natural(nc, net, bank(h, 1)[:, C * g:C * g + C], wk[h]["xT"], g, "right")
                        last.then_inc(r_ready, 1)
                        for g in range(NT):
                            natural(nc, net, bank(h, 2)[:, C * g:C * g + C], wk[h]["xT"], g, "left")
                            last = natural(nc, net, bank(h, 3)[:, C * g:C * g + C], wk[h]["xT"], g, "gatel")
                        last.then_inc(lg_ready, 1)
                    for h in range(2):
                        pe.wait_ge(rl_taken, n1(h))
                        nc.tensor.matmul(bank(h, 0), net.same16[:], rh[h][:].rearrange("p g c -> p (g c)"),
                                         start=True, stop=False)
                        last = nc.tensor.matmul(bank(h, 0), net.same16[:], rl[h][:].rearrange("p g c -> p (g c)"),
                                                start=False, stop=True)
                        last.then_inc(rowsummed, 1)
                    for h in range(2):
                        turn(nc, cu, n1(h), wk[h], bank16(h, 1), net.ident16[:])
                    for h in range(2):
                        pe.wait_ge(cu["xT"], n1(h))
                        for g in range(NT):
                            last = natural(nc, net, bank(h, 2)[:, C * g:C * g + C], wk[h]["xT"], g, "out")
                        last.then_inc(outed, 1)


def pairs_of_tiles(t, image):
    return (t[:].rearrange("p (i h) g c -> p i (h g) c", h=2),
            image.rearrange("(i h) (g r) c k -> (r c) i (h g) k", h=2, g=NT))


def finish_store(net, out):
    nc, sem = net.nc, net.sem
    tp, ov = pairs_of_tiles(net.t, out)
    x_stored = sem("x_stored")
    with nc.Block() as block:
        @block.sync
        def _(sp):
            with sp.Fori(0, PAIRS) as i:
                sp.dma_start(ov[:, i], tp[:, i]).then_inc(x_stored, 16)
            sp.wait_ge(x_stored, 16 * PAIRS)


def piece_count(n, per, k):
    return per * n + k + 1


def stage_attend(net, d):
    nc, sem = net.nc, net.sem
    RING = 4
    with ExitStack() as ctx:
        def sb(name, shape, dt):
            return ctx.enter_context(nc.sbuf_tensor("a2_" + name, shape, dt))

        wk = [work_buffers(sb, f"w{h}") for h in range(2)]
        xTb = [sb(f"xTb{h}", [P, TOK], F16) for h in range(2)]
        ex = sb("ex", [P, RING, TOK], F32)
        exh = sb("exh", [P, RING, TOK], F16)
        exl = sb("exl", [P, RING, TOK], F16)
        rs = [sb(f"rs{h}", [P, NT], F32) for h in range(2)]
        rinv = [sb(f"rinv{h}", [P, NT], F32) for h in range(2)]
        o = [sb(f"o{h}", [P, NT, C], F32) for h in range(2)]
        shift = sb("shift", [P, 1], F32)
        ps_s = ctx.enter_context(nc.psum_tensor("a2_ps_s", [P, 2, TOK], F32))
        ps_o = ctx.enter_context(nc.psum_tensor("a2_ps_o", [P, 2, 512], F32))
        ps_t = ctx.enter_context(nc.psum_tensor("a2_ps_t", [P, 2, TOK], F16))
        ln = net.norms[0]
        doubled, turned_b, xTb_done, shift_set = (sem("a2_" + s) for s in ("doubled", "turned_b", "xTb", "shift_set"))
        scored, exped, high, low_v, low_g, weighed = (sem("a2_" + s) for s in (
            "scored", "exped", "high", "low_v", "low_g", "weighed"))
        inverted, normed, added = (sem("a2_" + s) for s in ("inverted", "normed", "added"))
        tv = net.t[:].rearrange("p (i h) g c -> p i h g c", h=2)
        base = B

        def images(engine, attend, prep):
            prep(0, 0, range(8))
            with engine.Fori(0, PAIRS - 1) as i:
                attend(i, 0, (i, 1))
                attend(i, 1, (i + 1, 0))
            attend(PAIRS - 1, 0, (PAIRS - 1, 1))
            attend(PAIRS - 1, 1, None)

        with nc.Block() as block:
            @block.vector
            def _(dve):
                nc.vector.memset(shift[:], -SHIFT2).then_inc(shift_set, 1)

                def prep(i, h, pieces):
                    n, w, src = base + 2 * i + h, wk[h], tv[:, i, h]
                    for k in pieces:
                        if k == 0:
                            norm_sum(nc, ln, n + 1, src, w)
                            norm_centre(nc, ln, n + 1, src, w)
                        if k == 2:
                            norm_sumsq(nc, ln, n + 1, w)
                        if k == 3:
                            norm_apply(nc, ln, n + 1, w)
                        if k == 5:
                            cut_low(nc, ln, n + 1, w, w["xn"])
                            nc.vector.tensor_copy(w["hl"][:, :, 2 * C:3 * C],
                                                  w["hl"][:, :, 0:C]).then_inc(doubled, 1)
                        if k == 6:
                            take_turned(nc, ln, n + 1, w, ps_t[:, 0])
                            dve.wait_ge(turned_b, 2 * i + h + 1)
                            nc.vector.tensor_copy(xTb[h][:], ps_t[:, 1]).then_inc(xTb_done, 1)

                def attend(i, h, ahead):
                    n = 2 * i + h
                    for m in range(NT):
                        dve.wait_ge(exped, piece_count(n, NT, m))
                        if m >= RING:
                            dve.wait_ge(weighed, piece_count(n, NT, m - RING))
                        r = m % RING
                        nc.vector.tensor_copy(exh[:, r], ex[:, r]).then_inc(high, 1)
                        if m % 2 == 0:
                            dve.wait_ge(high, piece_count(n, NT, m))
                            nc.vector.tensor_tensor(exl[:, r], ex[:, r], exh[:, r], ALU.subtract).then_inc(low_v, 1)
                        if ahead:
                            prep(*ahead, (m,))
                    nc.vector.reciprocal(rinv[h][:], rs[h][:]).then_inc(inverted, 1)
                    dve.wait_ge(inverted, n + 1)
                    dve.wait_ge(weighed, piece_count(n, NT, NT - 1))
                    nc.vector.tensor_tensor(o[h][:], tiles(ps_o[:, h]), spread(rinv[h][:], C),
                                            ALU.mult).then_inc(normed, 1)
                    dve.wait_ge(normed, n + 1)
                    nc.vector.tensor_tensor(tv[:, i, h], tv[:, i, h], o[h][:], ALU.add).then_inc(added, 1)

                images(dve, attend, prep)
                dve.wait_ge(added, B)

            @block.scalar
            def _(act):
                act.wait_ge(shift_set, 1)

                def prep(i, h, pieces):
                    n, w = base + 2 * i + h, wk[h]
                    for k in pieces:
                        if k == 1:
                            norm_square(nc, ln, n + 1, w)
                        if k == 4:
                            cut_high(nc, ln, n + 1, w, w["xn"])

                def attend(i, h, ahead):
                    n = 2 * i + h
                    for m in range(NT):
                        r = m % RING
                        act.wait_ge(scored, piece_count(n, NT, m))
                        if m >= RING:
                            if m % 2 == 0:
                                act.wait_ge(low_v, piece_count(n, NT // 2, (m - RING) // 2))
                            else:
                                act.wait_ge(low_g, piece_count(n, NT // 2, (m - RING) // 2))
                        nc.scalar.activation(ex[:, r], ps_s[:, m % 2], ACT.Exp, bias=shift[:],
                                             accum_out=rs[h][:, m:m + 1]).then_inc(exped, 1)
                        if ahead:
                            prep(*ahead, (m,))

                images(act, attend, prep)

            @block.gpsimd
            def _(pool):
                def prep(i, h, pieces):
                    for k in pieces:
                        if k == 2:
                            norm_rstd(nc, ln, base + 2 * i + h + 1, wk[h], net.nhalf[:], net.eps[:])

                def attend(i, h, ahead):
                    n = 2 * i + h
                    for m in range(NT):
                        if m % 2:
                            pool.wait_ge(high, piece_count(n, NT, m))
                            nc.gpsimd.tensor_tensor(exl[:, m % RING], ex[:, m % RING], exh[:, m % RING],
                                                    ALU.subtract).then_inc(low_g, 1)
                        if ahead:
                            prep(*ahead, (m,))

                images(pool, attend, prep)

            @block.tensor
            def _(pe):
                def prep(i, h, pieces):
                    n, w = base + 2 * i + h, wk[h]
                    for k in pieces:
                        if k == 6:
                            turn(nc, ln, n + 1, w, ps_t[:, 0], net.ident16[:])
                            pe.wait_ge(doubled, 2 * i + h + 1)
                            for g in range(NT):
                                last = nc.tensor.transpose(ps_t[:, 1, P * g:P * g + P], w["hl"][:, g, C:3 * C],
                                                           net.ident16[:])
                            last.then_inc(turned_b, 1)

                def attend(i, h, ahead):
                    n = 2 * i + h
                    for m in range(NT + 2):
                        if m < NT:
                            if m == 0:
                                pe.wait_ge(xTb_done, n + 1)
                                pe.wait_ge(ln["xT"], base + n + 1)
                            if m >= 2:
                                pe.wait_ge(exped, piece_count(n, NT, m - 2))
                            tok = slice(P * m, P * m + P)
                            for half in range(2):
                                out = ps_s[:, m % 2, 512 * half:512 * half + 512]
                                z = wk[h]["xT"][:, 512 * half:512 * half + 512]
                                nc.tensor.matmul(out, wk[h]["xT"][:, tok], z, start=True, stop=False)
                                last = nc.tensor.matmul(out, xTb[h][:, tok], z, start=False, stop=True)
                            last.then_inc(scored, 1)
                            if ahead:
                                prep(*ahead, (m,))
                        if m >= 2:
                            k = m - 2
                            if k % 2 == 0:
                                pe.wait_ge(low_v, piece_count(n, NT // 2, k // 2))
                            else:
                                pe.wait_ge(low_g, piece_count(n, NT // 2, k // 2))
                            z_high, z_low = wk[h]["hl"][:, k, 0:C], wk[h]["hl"][:, k, C:2 * C]
                            for g in range(NT):
                                out = ps_o[:, h, C * g:C * g + C]
                                e_high = exh[:, k % RING, P * g:P * g + P]
                                e_low = exl[:, k % RING, P * g:P * g + P]
                                nc.tensor.matmul(out, e_high, z_high, start=(k == 0 and g == 0), stop=False,
                                                 skip_group_check=True)
                                nc.tensor.matmul(out, e_high, z_low, start=False, stop=False, skip_group_check=True)
                                last = nc.tensor.matmul(out, e_low, z_high, start=False, stop=(k == NT - 1),
                                                        skip_group_check=True)
                            last.then_inc(weighed, 1)

                images(pe, attend, prep)


def stage_pool(net, d):
    nc, sem = net.nc, net.sem
    with ExitStack() as ctx:
        def sb(name, shape, dt):
            return ctx.enter_context(nc.sbuf_tensor("f2_" + name, shape, dt))

        kept = sb("kept", [P, NG, TOK], F32)
        pooled = sb("pooled", [C + 1, E2, B], F32)
        experts = sb("experts", [P, NG, C], F32)
        pooled_ready, zero_set = sem("f2_pooled_ready"), sem("f2_zero_set")
        base = 2 * B
        with ExitStack() as inner:
            def sb(name, shape, dt):
                return inner.enter_context(nc.sbuf_tensor("f2_" + name, shape, dt))

            wk = [work_buffers(sb, f"w{j}") for j in range(GRP)]
            prob = sb("prob", [P, TOK], F32)
            rest = sb("rest", [P, TOK], F32)
            mask = sb("mask", [P, TOK], F32)
            mask_t = sb("mask_t", [P, NT, P], F32)
            small = sb("small", [P, 4], F32)
            top = sb("top", [P, 8], F32)
            idle = sb("idle", [P, 1], F32)
            ps_t = inner.enter_context(nc.psum_tensor("f2_ps_t", [P, 2, TOK], F16))
            ps_l = inner.enter_context(nc.psum_tensor("f2_ps_l", [P, TOK], F32))
            ps_m = inner.enter_context(nc.psum_tensor("f2_ps_m", [P, TOK], F32))
            ps_p = inner.enter_context(nc.psum_tensor("f2_ps_p", [C, P], F32))
            ln = net.norms[0]
            logits, maxed, negated, exped, inverted, probs = (sem("f2_" + s) for s in (
                "logits", "maxed", "negated", "exped", "inverted", "probs"))
            topped, replaced, masked, mask_kept, mask_turned, mask_t_taken = (sem("f2_" + s) for s in (
                "topped", "replaced", "masked", "mask_kept", "mask_turned", "mask_t_taken"))
            pool_ready = sem("f2_pool_ready")
            tg = net.t[:].rearrange("p (i j) g c -> p i j g c", j=GRP)
            pg = pooled[:].rearrange("p e (i j) -> p i j e", j=GRP)

            with nc.Block() as block:
                @block.vector
                def _(dve):
                    nc.vector.memset(pooled[C:C + 1], 1.0)
                    with dve.Fori(0, NG) as i:
                        def n1(j):
                            return base + GRP * i + j + 1

                        for j in range(GRP):
                            norm_sum(nc, ln, n1(j), tg[:, i, j], wk[j])
                        for j in range(GRP):
                            norm_centre(nc, ln, n1(j), tg[:, i, j], wk[j])
                        for j in range(GRP):
                            norm_sumsq(nc, ln, n1(j), wk[j])
                        for j in range(GRP):
                            norm_apply(nc, ln, n1(j), wk[j])
                        for j in range(GRP):
                            cut_low(nc, ln, n1(j), wk[j], wk[j]["xn"])
                        for j in range(GRP):
                            take_turned(nc, ln, n1(j), wk[j], ps_t[:, j % 2])
                        dve.wait_ge(logits, i + 1)
                        nc.vector.tensor_reduce(small[:, 0:1], ps_l[:], AX.X, ALU.max).then_inc(maxed, 1)
                        dve.wait_ge(maxed, i + 1)
                        nc.vector.tensor_scalar(small[:, 1:2], small[:, 0:1], -IWS, None, ALU.mult).then_inc(negated, 1)
                        dve.wait_ge(exped, i + 1)
                        nc.vector.reciprocal(small[:, 3:4], small[:, 2:3]).then_inc(inverted, 1)
                        dve.wait_ge(inverted, i + 1)
                        nc.vector.tensor_scalar(prob[:], rest[:], small[:, 3:4], None, ALU.mult).then_inc(probs, 1)
                        dve.wait_ge(probs, i + 1)
                        nc.vector.memset(idle[:], 0.0)
                        nc.vector.max(top[:], prob[:]).then_inc(topped, 1)
                        dve.wait_ge(topped, i + 1)
                        nc.vector.memset(idle[:], 0.0)
                        nc.vector.match_replace(rest[:], top[:], prob[:], 0.0).then_inc(replaced, 1)
                        dve.wait_ge(replaced, i + 1)
                        nc.vector.tensor_tensor(mask[:], prob[:], rest[:], ALU.subtract).then_inc(masked, 1)
                        dve.wait_ge(mask_turned, i + 1)
                        nc.vector.tensor_copy(mask_t[:].rearrange("p a b -> p (a b)"), ps_m[:]).then_inc(mask_t_taken, 1)
                        dve.wait_ge(pool_ready, i + 1)
                        nc.vector.tensor_copy(pg[0:C, i], ps_p[:].rearrange("p (j e) -> p j e", j=GRP)
                                              ).then_inc(pooled_ready, 1)
                        dve.wait_ge(pooled_ready, i + 1)
                        dve.wait_ge(mask_kept, i + 1)

                @block.scalar
                def _(act):
                    with act.Fori(0, NG) as i:
                        def n1(j):
                            return base + GRP * i + j + 1

                        for j in range(GRP):
                            norm_square(nc, ln, n1(j), wk[j])
                        for j in range(GRP):
                            cut_high(nc, ln, n1(j), wk[j], wk[j]["xn"])
                        act.wait_ge(negated, i + 1)
                        nc.scalar.activation(rest[:], ps_l[:], ACT.Exp, bias=small[:, 1:2], scale=IWS,
                                             accum_out=small[:, 2:3]).then_inc(exped, 1)
                        act.wait_ge(masked, i + 1)
                        nc.scalar.activation(kept[:, i], mask[:], ACT.Copy).then_inc(mask_kept, 1)

                @block.gpsimd
                def _(pool):
                    with pool.Fori(0, NG) as i:
                        for j in range(GRP):
                            norm_rstd(nc, ln, base + GRP * i + j + 1, wk[j], net.nhalf[:], net.eps[:])

                @block.tensor
                def _(pe):
                    with pe.Fori(0, NG) as i:
                        def n1(j):
                            return base + GRP * i + j + 1

                        for j in range(GRP):
                            if j >= 2:
                                pe.wait_ge(ln["xT"], n1(j - 2))
                            turn(nc, ln, n1(j), wk[j], ps_t[:, j % 2], net.ident16[:])
                        c = COLS["gate2"]
                        for j in range(GRP):
                            pe.wait_ge(ln["xT"], n1(j))
                            for half in range(2):
                                tok = slice(512 * half, 512 * half + 512)
                                out, x = ps_l[E2 * j:E2 * j + E2, tok], wk[j]["xT"][:, tok]
                                nc.tensor.matmul(out, net.wa[:, c], x, start=True, stop=False, tile_position=(0, E2 * j))
                                nc.tensor.matmul(out, net.wb[:, c], x, start=False, stop=False,
                                                 tile_position=(0, E2 * j))
                                last = nc.tensor.matmul(out, net.bias[:, c], net.ones16[:, 0:512], start=False,
                                                        stop=True, tile_position=(0, E2 * j))
                        last.then_inc(logits, 1)
                        pe.wait_ge(masked, i + 1)
                        for g in range(NT):
                            last = nc.tensor.transpose(ps_m[:, P * g:P * g + P], mask[:, P * g:P * g + P], net.ident[:])
                        last.then_inc(mask_turned, 1)
                        pe.wait_ge(mask_t_taken, i + 1)
                        for j in range(GRP):
                            for g in range(NT):
                                last = nc.tensor.matmul(ps_p[:, E2 * j:E2 * j + E2], wk[j]["xn"][:, g],
                                                        mask_t[:, g, E2 * j:E2 * j + E2], start=(g == 0),
                                                        stop=(g == NT - 1))
                        last.then_inc(pool_ready, 1)

        scratch = nc.dram_tensor("expert_outputs", (B, E2, C), F32, kind="Internal").ap()
        with ExitStack() as inner:
            def sb(name, shape, dt):
                return inner.enter_context(nc.sbuf_tensor("f2_" + name, shape, dt))

            w1 = sb("w1", [C + 1, E2, HID], F32)
            w2 = sb("w2", [P, 2, E2, C], F32)
            w2b = sb("w2b", [P, C], F32)
            hid = sb("hid", [P, 2, E2, B], F32)
            outs = sb("outs", [B, E2, C], F32)
            ps_h = inner.enter_context(nc.psum_tensor("f2_ps_h", [P, 2, E2, B], F32))
            ps_y = inner.enter_context(nc.psum_tensor("f2_ps_y", [B, E2, C], F32))
            w_loaded, hid_ready, gelued, out_ready, out_taken, bounced, back = (sem("f2_" + s) for s in (
                "w_loaded", "hid_ready", "gelued", "out_ready", "out_taken", "bounced", "back"))
            biased = sem("f2_biased")
            with nc.Block() as block:
                @block.sync
                def _(sp):
                    sp.dma_start(w1[:], d["L2_ffn_weight1"].rearrange("e d h -> d e h")).then_inc(w_loaded, 16)
                    for a in range(2):
                        sp.dma_start(w2[:, a], d["L2_ffn_weight2"][:, P * a:P * a + P, :].rearrange("e p o -> p e o")
                                     ).then_inc(w_loaded, 16)
                    for j in range(GRP):
                        sp.dma_start(w2b[E2 * j:E2 * j + E2, :], d["L2_ffn_weight2"][:, HID, :]).then_inc(w_loaded, 16)
                    sp.wait_ge(out_taken, 1)
                    sp.dma_start(scratch, outs[:]).then_inc(bounced, 16)
                    sp.wait_ge(bounced, 16)
                    sp.dma_start(experts[:], scratch.rearrange("(g j) e o -> (j e) g o", j=GRP)).then_inc(back, 16)

                @block.tensor
                def _(pe):
                    pe.wait_ge(w_loaded, 16 * 7)
                    for a in range(2):
                        for e in range(E2):
                            last = nc.tensor.matmul(ps_h[:, a, e], w1[:, e, P * a:P * a + P], pooled[:, e], start=True,
                                                    stop=True)
                        last.then_inc(hid_ready, 1)
                    pe.wait_ge(gelued, 2)
                    for e in range(E2):
                        nc.tensor.matmul(ps_y[:, e], hid[:, 0, e], w2[:, 0, e], start=True, stop=False)
                        last = nc.tensor.matmul(ps_y[:, e], hid[:, 1, e], w2[:, 1, e], start=False, stop=True)
                    last.then_inc(out_ready, 1)

                @block.scalar
                def _(act):
                    for a in range(2):
                        act.wait_ge(hid_ready, 2)
                        nc.scalar.activation(hid[:, a], ps_h[:, a], ACT.Gelu).then_inc(gelued, 1)

                @block.vector
                def _(dve):
                    dve.wait_ge(out_ready, 1)
                    nc.vector.tensor_copy(outs[:], ps_y[:]).then_inc(out_taken, 1)
                    dve.wait_ge(back, 16)
                    dve.wait_ge(w_loaded, 16 * 7)
                    nc.vector.tensor_tensor(experts[:], experts[:], over(w2b[:], NG), ALU.add).then_inc(biased, 1)
                    dve.wait_ge(biased, 1)

        with ExitStack() as inner:
            def sb(name, shape, dt):
                return inner.enter_context(nc.sbuf_tensor("f2_" + name, shape, dt))

            mask = [sb(f"maskb{q}", [P, TOK], F32) for q in range(2)]
            diag = [sb(f"diag{q}", [P, GRP, C], F32) for q in range(2)]
            ps_s = [inner.enter_context(nc.psum_tensor(f"f2_ps_s{q}", [P, NT, GRP, C], F32)) for q in range(2)]
            diag_zero, ready, spread_out, added = (sem("f2_" + s) for s in (
                "diag_zero", "ready", "spread_out", "added"))
            kq = kept[:].rearrange("p (i q) s -> p i q s", q=2)
            eq = experts[:].rearrange("p (i q) c -> p i q c", q=2)
            tq = net.t[:].rearrange("p (i q j) g c -> p i q j g c", q=2, j=GRP)
            with nc.Block() as block:
                @block.vector
                def _(dve):
                    for q in range(2):
                        nc.vector.memset(diag[q][:], 0.0).then_inc(diag_zero, 1)
                    dve.wait_ge(diag_zero, 2)

                    def prepare(i, q):
                        nc.vector.tensor_copy(mask[q][:], kq[:, i, q])
                        for j in range(GRP):
                            rows = slice(E2 * j, E2 * j + E2)
                            last = nc.vector.tensor_copy(diag[q][rows, j], eq[rows, i, q])
                        last.then_inc(ready, 1)

                    with dve.Fori(0, max(NG // 2, 1)) as i:
                        for q in range(min(2, NG)):
                            prepare(i, q)
                        for q in range(min(2, NG)):
                            dve.wait_ge(spread_out, 2 * i + q + 1)
                            for j in range(GRP):
                                last = nc.vector.tensor_tensor(tq[:, i, q, j], tq[:, i, q, j], ps_s[q][:, :, j, :],
                                                               ALU.add)
                            last.then_inc(added, 1)
                    dve.wait_ge(added, NG)

                @block.tensor
                def _(pe):
                    with pe.Fori(0, max(NG // 2, 1)) as i:
                        for q in range(min(2, NG)):
                            pe.wait_ge(ready, 2 * i + q + 1)
                            for g in range(NT):
                                last = nc.tensor.matmul(ps_s[q][:, g].rearrange("p j c -> p (j c)"),
                                                        mask[q][:, P * g:P * g + P],
                                                        diag[q][:].rearrange("p j c -> p (j c)"), start=True, stop=True)
                            last.then_inc(spread_out, 1)


def stage_attend_qkv(net, d):
    nc, sem = net.nc, net.sem
    with ExitStack() as ctx:
        def sb(name, shape, dt):
            return ctx.enter_context(nc.sbuf_tensor("a3_" + name, shape, dt))

        wk = [work_buffers(sb, f"w{h}") for h in range(2)]
        qx, kh, kl = ([sb(f"{s}{h}", [P, TOK], F16) for h in range(2)] for s in ("qx", "kh", "kl"))
        vh, vl = ([sb(f"{s}{h}", [P, NT, C], F16) for h in range(2)] for s in ("vh", "vl"))
        pr = sb("pr", [P, 2, TOK], F32)
        prh, prl = (sb(s, [P, 2, TOK], F16) for s in ("prh", "prl"))
        pth, ptl = (sb(s, [P, 2, TOK], F16) for s in ("pth", "ptl"))
        nmax = sb("nmax", [P, 2, NT], F32)
        rs, rinv = (sb(s, [P, 2, NT], F32) for s in ("rs", "rinv"))
        o = [sb(f"o{h}", [P, NT, C], F32) for h in range(2)]
        ps_s = ctx.enter_context(nc.psum_tensor("a3_ps_s", [P, 2, TOK], F32))
        ps_h = ctx.enter_context(nc.psum_tensor("a3_ps_h", [P, TOK], F16))
        ps_l = ctx.enter_context(nc.psum_tensor("a3_ps_l", [P, TOK], F16))
        ps_o = ctx.enter_context(nc.psum_tensor("a3_ps_o", [P, 512], F32))
        ps_w = ctx.enter_context(nc.psum_tensor("a3_ps_w", [P, 512], F32))
        ln = net.norms[0]
        base = 3 * B
        proj, proj_high, proj_low = (sem("a3_" + s) for s in ("proj", "proj_high", "proj_low"))
        scored, maxed, exped, high, low = (sem("a3_" + s) for s in ("scored", "maxed", "exped", "high", "low"))
        turned_h, turned_l, taken_h, taken_l, weighed = (sem("a3_" + s) for s in (
            "turned_h", "turned_l", "taken_h", "taken_l", "weighed"))
        inverted, bank_read, added = (sem("a3_" + s) for s in ("inverted", "bank_read", "added"))
        tv = net.t[:].rearrange("p (i h) g c -> p i h g c", h=2)
        PROJ = 5

        def images(engine, attend, prep):
            prep(0, 0, range(8))
            with engine.Fori(0, PAIRS - 1) as i:
                attend(i, 0, (i, 1))
                attend(i, 1, (i + 1, 0))
            attend(PAIRS - 1, 0, (PAIRS - 1, 1))
            attend(PAIRS - 1, 1, None)

        PIECES = {4: (0,), 5: (1, 2), 6: (3,), 7: (4,)}

        def half_of(k):
            return slice(512 * (k % 2), 512 * (k % 2) + 512)

        with nc.Block() as block:
            @block.vector
            def _(dve):
                def prep(i, h, pieces):
                    n, w, src = 2 * i + h, wk[h], tv[:, i, h]
                    for m in pieces:
                        if m == 0:
                            norm_sum(nc, ln, base + n + 1, src, w)
                            norm_centre(nc, ln, base + n + 1, src, w)
                        if m == 1:
                            norm_sumsq(nc, ln, base + n + 1, w)
                        if m == 2:
                            norm_apply(nc, ln, base + n + 1, w)
                        if m == 3:
                            cut_low(nc, ln, base + n + 1, w, w["xn"])
                        if m == 4:
                            take_turned(nc, ln, base + n + 1, w, ps_w[:].bitcast(F16))
                        for k in PIECES.get(m, ()):
                            dve.wait_ge(proj_high, piece_count(n, PROJ, k))
                            if k < 2:
                                part = qx[h][C:P, half_of(k)]
                                ins = nc.vector.scalar_tensor_tensor(part, ps_w[C:P, :], IWS / TEMP, part, ALU.mult,
                                                                     ALU.subtract)
                            elif k < 4:
                                ins = nc.vector.scalar_tensor_tensor(kl[h][:, half_of(k)], ps_w[:], IWS,
                                                                     kh[h][:, half_of(k)], ALU.mult, ALU.subtract)
                            else:
                                ins = nc.vector.scalar_tensor_tensor(vl[h][:], tiles(ps_w[:]), IWS, vh[h][:], ALU.mult,
                                                                     ALU.subtract)
                            ins.then_inc(proj_low, 1)

                def attend(i, h, ahead):
                    n = 2 * i + h
                    for m in range(NT + 2):
                        if m < NT:
                            dve.wait_ge(scored, piece_count(n, NT, m))
                            nc.vector.tensor_reduce(nmax[:, h, m:m + 1], ps_s[:, m % 2], AX.X, ALU.max,
                                                    negate=True).then_inc(maxed, 1)
                        if 1 <= m <= NT:
                            k = m - 1
                            dve.wait_ge(exped, piece_count(n, NT, k))
                            if k >= 2:
                                dve.wait_ge(turned_h, piece_count(n, NT, k - 2))
                            nc.vector.tensor_copy(prh[:, k % 2], pr[:, k % 2]).then_inc(high, 1)
                        if m >= 2:
                            k = m - 2
                            dve.wait_ge(turned_l, piece_count(n, NT, k))
                            if k >= 2:
                                dve.wait_ge(weighed, piece_count(n, NT, k - 2))
                            nc.vector.tensor_copy(ptl[:, k % 2], ps_l[:]).then_inc(taken_l, 1)
                        if ahead and m < NT:
                            prep(*ahead, (m,))
                    nc.vector.reciprocal(rinv[:, h], rs[:, h]).then_inc(inverted, 1)
                    dve.wait_ge(inverted, n + 1)
                    dve.wait_ge(weighed, piece_count(n, NT, NT - 1))
                    nc.vector.tensor_tensor(o[h][:], tiles(ps_o[:]), spread(rinv[:, h], C), ALU.mult).then_inc(bank_read, 1)
                    dve.wait_ge(bank_read, n + 2)
                    nc.vector.tensor_tensor(tv[:, i, h], tv[:, i, h], o[h][:], ALU.add).then_inc(added, 1)

                nc.vector.engine_nop().then_inc(bank_read, 1)
                images(dve, attend, prep)
                dve.wait_ge(added, B)

            @block.scalar
            def _(act):
                def prep(i, h, pieces):
                    n, w = 2 * i + h, wk[h]
                    for m in pieces:
                        if m == 0:
                            norm_square(nc, ln, base + n + 1, w)
                        if m == 2:
                            cut_high(nc, ln, base + n + 1, w, w["xn"])
                        for k in PIECES.get(m, ()):
                            act.wait_ge(proj, piece_count(n, PROJ, k))
                            if k < 2:
                                ins = nc.scalar.activation(qx[h][:, half_of(k)], ps_w[:], ACT.Copy, scale=IWS / TEMP)
                            elif k < 4:
                                ins = nc.scalar.activation(kh[h][:, half_of(k)], ps_w[:], ACT.Copy, scale=IWS)
                            else:
                                ins = nc.scalar.activation(vh[h][:], tiles(ps_w[:]), ACT.Copy, scale=IWS)
                            ins.then_inc(proj_high, 1)

                def attend(i, h, ahead):
                    n = 2 * i + h
                    for m in range(NT + 2):
                        if m < NT:
                            act.wait_ge(maxed, piece_count(n, NT, m))
                            if m >= 2:
                                act.wait_ge(low, piece_count(n, NT, m - 2))
                            nc.scalar.activation(pr[:, m % 2], ps_s[:, m % 2], ACT.Exp, bias=nmax[:, h, m:m + 1],
                                                 accum_out=rs[:, h, m:m + 1]).then_inc(exped, 1)
                        if m >= 2:
                            k = m - 2
                            act.wait_ge(turned_h, piece_count(n, NT, k))
                            if k >= 2:
                                act.wait_ge(weighed, piece_count(n, NT, k - 2))
                            nc.scalar.activation(pth[:, k % 2], ps_h[:], ACT.Copy).then_inc(taken_h, 1)
                        if ahead and m < NT:
                            prep(*ahead, (m,))

                images(act, attend, prep)

            @block.gpsimd
            def _(pool):
                def prep(i, h, pieces):
                    for m in pieces:
                        if m == 1:
                            norm_rstd(nc, ln, base + 2 * i + h + 1, wk[h], net.nhalf[:], net.eps[:])

                def attend(i, h, ahead):
                    n = 2 * i + h
                    for m in range(NT):
                        pool.wait_ge(high, piece_count(n, NT, m))
                        if m >= 2:
                            pool.wait_ge(turned_l, piece_count(n, NT, m - 2))
                        nc.gpsimd.tensor_tensor(prl[:, m % 2], pr[:, m % 2], prh[:, m % 2],
                                                ALU.subtract).then_inc(low, 1)
                        if ahead:
                            prep(*ahead, (m,))

                images(pool, attend, prep)

            @block.tensor
            def _(pe):
                def prep(i, h, pieces):
                    n, w = 2 * i + h, wk[h]
                    for m in pieces:
                        if m == 4:
                            turn(nc, ln, base + n + 1, w, ps_w[:].bitcast(F16), net.ident16[:])
                        for k in PIECES.get(m, ()):
                            if k == 0:
                                pe.wait_ge(ln["xT"], base + n + 1)
                            else:
                                pe.wait_ge(proj_low, piece_count(n, PROJ, k - 1))
                            if k < 4:
                                c = COLS["q3" if k < 2 else "k3"]
                                tok = half_of(k)
                                last = upright(nc, net, ps_w[:], w["xT"], c, tok.start, tok.stop)
                            else:
                                for g in range(NT):
                                    last = natural(nc, net, ps_w[:, C * g:C * g + C], w["xT"], g, "v3")
                            last.then_inc(proj, 1)

                def attend(i, h, ahead):
                    n = 2 * i + h
                    for m in range(NT + 3):
                        if m < NT:
                            if m == 0:
                                pe.wait_ge(proj_low, piece_count(n, PROJ, PROJ - 1))
                            if m >= 2:
                                pe.wait_ge(exped, piece_count(n, NT, m - 2))
                            tok = slice(P * m, P * m + P)
                            for half in range(2):
                                keys = slice(512 * half, 512 * half + 512)
                                nc.tensor.matmul(ps_s[:, m % 2, keys], qx[h][:, tok], kh[h][:, keys], start=True,
                                                 stop=False)
                                last = nc.tensor.matmul(ps_s[:, m % 2, keys], qx[h][:, tok], kl[h][:, keys],
                                                        start=False, stop=True)
                            last.then_inc(scored, 1)
                        if 2 <= m < NT + 2:
                            k = m - 2
                            if k >= 1:
                                pe.wait_ge(taken_h, piece_count(n, NT, k - 1))
                                pe.wait_ge(taken_l, piece_count(n, NT, k - 1))
                            pe.wait_ge(high, piece_count(n, NT, k))
                            for g in range(NT):
                                last = nc.tensor.transpose(ps_h[:, P * g:P * g + P], prh[:, k % 2, P * g:P * g + P],
                                                           net.ident16[:])
                            last.then_inc(turned_h, 1)
                            pe.wait_ge(low, piece_count(n, NT, k))
                            for g in range(NT):
                                last = nc.tensor.transpose(ps_l[:, P * g:P * g + P], prl[:, k % 2, P * g:P * g + P],
                                                           net.ident16[:])
                            last.then_inc(turned_l, 1)
                        if m >= 3:
                            k = m - 3
                            if k == 0:
                                pe.wait_ge(bank_read, n + 1)
                            pe.wait_ge(taken_h, piece_count(n, NT, k))
                            pe.wait_ge(taken_l, piece_count(n, NT, k))
                            out = ps_o[:, C * k:C * k + C]
                            for g in range(NT):
                                high_t, low_t = pth[:, k % 2, P * g:P * g + P], ptl[:, k % 2, P * g:P * g + P]
                                nc.tensor.matmul(out, high_t, vh[h][:, g], start=(g == 0), stop=False)
                                nc.tensor.matmul(out, high_t, vl[h][:, g], start=False, stop=False)
                                last = nc.tensor.matmul(out, low_t, vh[h][:, g], start=False, stop=(g == NT - 1))
                            last.then_inc(weighed, 1)
                        if ahead and m < NT:
                            prep(*ahead, (m,))

                images(pe, attend, prep)


def stage_route(net, d):
    nc, sem = net.nc, net.sem
    with ExitStack() as ctx:
        def sb(name, shape, dt):
            return ctx.enter_context(nc.sbuf_tensor("f3_" + name, shape, dt))

        wk = [work_buffers(sb, f"w{h}") for h in range(2)]
        acc = [sb(f"acc{h}", [P, NT, C], F32) for h in range(2)]
        order = sb("order", [P, E3], F32)
        sm = [{k: sb(f"{k}{h}", [P, NT, E3], F32) for k in ("lg", "eq", "first", "rest", "second", "gates")}
              for h in range(2)]
        st = [{k: sb(f"{k}{h}", [P, NT], F32) for k in ("m1", "k1", "m2", "k2", "dl", "e2", "den", "g1", "g2")}
              for h in range(2)]
        mixed = sb("mixed", [P, 3, E3, C], F32)
        ps_e = ctx.enter_context(nc.psum_tensor("f3_ps_e", [P, 4, 512], F32))
        ps_t = ctx.enter_context(nc.psum_tensor("f3_ps_t", [P, 2, TOK], F16))
        ps_r = ctx.enter_context(nc.psum_tensor("f3_ps_r", [P, 2, 512], F32))
        ln = net.norms[0]
        base = 4 * B
        routed, gate_step, diffed, e2_done = (sem("f3_" + s) for s in ("routed", "gate_step", "diffed", "e2_done"))
        expert_out, weighted, summed, added, stored = (sem("f3_" + s) for s in (
            "expert_out", "weighted", "summed", "added", "stored"))
        order_set = sem("f3_order_set")
        tv = net.t[:].rearrange("p (i h) g c -> p i h g c", h=2)
        tp, ov = pairs_of_tiles(net.t, net.out)
        STEPS = 18

        with nc.Block() as block:
            @block.sync
            def _(sp):
                with sp.Fori(0, PAIRS) as i:
                    sp.wait_ge(added, 2 * i + 2)
                    sp.dma_start(ov[:, i], tp[:, i]).then_inc(stored, 16)
                sp.wait_ge(stored, 16 * PAIRS)

            @block.vector
            def _(dve):
                for e in range(E3):
                    last = nc.vector.memset(order[:, e:e + 1], float(E3 - e))
                last.then_inc(order_set, 1)
                dve.wait_ge(order_set, 1)
                with dve.Fori(0, PAIRS) as i:
                    def n1(h):
                        return base + 2 * i + h + 1

                    for h in range(2):
                        norm_sum(nc, ln, n1(h), tv[:, i, h], wk[h])
                    for h in range(2):
                        norm_centre(nc, ln, n1(h), tv[:, i, h], wk[h])
                    for h in range(2):
                        norm_sumsq(nc, ln, n1(h), wk[h])
                    for h in range(2):
                        norm_apply(nc, ln, n1(h), wk[h])
                    for h in range(2):
                        cut_low(nc, ln, n1(h), wk[h], wk[h]["xn"])
                    for h in range(2):
                        take_turned(nc, ln, n1(h), wk[h], ps_t[:, h])
                    for h in range(2):
                        n, a, b = 2 * i + h, sm[h], st[h]
                        lg = a["lg"][:]
                        dve.wait_ge(routed, n + 1)
                        weights = over(order[:], NT)

                        def step(ins):
                            ins.then_inc(gate_step, 1)

                        step(nc.vector.tensor_copy(lg, ps_r[:, h, 0:NT * E3].rearrange("p (g e) -> p g e", e=E3)))
                        dve.wait_ge(gate_step, piece_count(n, STEPS, 0))
                        step(nc.vector.tensor_reduce(b["m1"][:], lg, AX.X, ALU.max))
                        dve.wait_ge(gate_step, piece_count(n, STEPS, 1))
                        step(nc.vector.tensor_tensor(a["eq"][:], lg, spread(b["m1"][:], E3), ALU.is_equal))
                        dve.wait_ge(gate_step, piece_count(n, STEPS, 2))
                        step(nc.vector.tensor_tensor(a["first"][:], a["eq"][:], weights, ALU.mult))
                        dve.wait_ge(gate_step, piece_count(n, STEPS, 3))
                        step(nc.vector.tensor_reduce(b["k1"][:], a["first"][:], AX.X, ALU.max))
                        dve.wait_ge(gate_step, piece_count(n, STEPS, 4))
                        step(nc.vector.tensor_tensor(a["first"][:], a["first"][:], spread(b["k1"][:], E3),
                                                     ALU.is_equal))
                        dve.wait_ge(gate_step, piece_count(n, STEPS, 5))
                        step(nc.vector.scalar_tensor_tensor(a["rest"][:], a["first"][:], -1e30, lg, ALU.mult, ALU.add))
                        dve.wait_ge(gate_step, piece_count(n, STEPS, 6))
                        step(nc.vector.tensor_reduce(b["m2"][:], a["rest"][:], AX.X, ALU.max))
                        dve.wait_ge(gate_step, piece_count(n, STEPS, 7))
                        nc.vector.tensor_tensor(b["dl"][:], b["m2"][:], b["m1"][:], ALU.subtract).then_inc(diffed, 1)
                        step(nc.vector.tensor_tensor(a["eq"][:], a["rest"][:], spread(b["m2"][:], E3), ALU.is_equal))
                        dve.wait_ge(gate_step, piece_count(n, STEPS, 8))
                        step(nc.vector.tensor_tensor(a["second"][:], a["eq"][:], weights, ALU.mult))
                        dve.wait_ge(gate_step, piece_count(n, STEPS, 9))
                        step(nc.vector.tensor_reduce(b["k2"][:], a["second"][:], AX.X, ALU.max))
                        dve.wait_ge(gate_step, piece_count(n, STEPS, 10))
                        step(nc.vector.tensor_tensor(a["second"][:], a["second"][:], spread(b["k2"][:], E3),
                                                     ALU.is_equal))
                        dve.wait_ge(e2_done, n + 1)
                        step(nc.vector.tensor_scalar(b["den"][:], b["e2"][:], WS, WS, ALU.mult, ALU.add))
                        dve.wait_ge(gate_step, piece_count(n, STEPS, 12))
                        step(nc.vector.reciprocal(b["g1"][:], b["den"][:]))
                        dve.wait_ge(gate_step, piece_count(n, STEPS, 13))
                        step(nc.vector.tensor_tensor(b["g2"][:], b["e2"][:], b["g1"][:], ALU.mult))
                        step(nc.vector.tensor_tensor(a["first"][:], a["first"][:], spread(b["g1"][:], E3), ALU.mult))
                        dve.wait_ge(gate_step, piece_count(n, STEPS, 15))
                        step(nc.vector.tensor_tensor(a["second"][:], a["second"][:], spread(b["g2"][:], E3), ALU.mult))
                        dve.wait_ge(gate_step, piece_count(n, STEPS, 16))
                        step(nc.vector.tensor_tensor(a["gates"][:], a["first"][:], a["second"][:], ALU.add))
                    for h in range(2):
                        n = 2 * i + h
                        dve.wait_ge(gate_step, piece_count(n, STEPS, 17))
                        for g in range(NT + 1):
                            if g < NT:
                                dve.wait_ge(expert_out, piece_count(n, NT, g))
                                if g >= 3:
                                    dve.wait_ge(summed, piece_count(n, NT, g - 3))
                                nc.vector.tensor_tensor(mixed[:, g % 3], ps_e[:, g % 4].rearrange("p (e c) -> p e c", e=E3),
                                                        spread(sm[h]["gates"][:, g], C), ALU.mult).then_inc(weighted, 1)
                            if g >= 1:
                                k = g - 1
                                dve.wait_ge(weighted, piece_count(n, NT, k))
                                nc.vector.tensor_reduce(acc[h][:, k], mixed[:, k % 3].rearrange("p e c -> p c e"), AX.X,
                                                        ALU.add).then_inc(summed, 1)
                        dve.wait_ge(summed, piece_count(n, NT, NT - 1))
                        nc.vector.tensor_tensor(tv[:, i, h], tv[:, i, h], acc[h][:], ALU.add).then_inc(added, 1)

            @block.scalar
            def _(act):
                with act.Fori(0, PAIRS) as i:
                    def n1(h):
                        return base + 2 * i + h + 1

                    for h in range(2):
                        norm_square(nc, ln, n1(h), wk[h])
                    for h in range(2):
                        cut_high(nc, ln, n1(h), wk[h], wk[h]["xn"])
                    for h in range(2):
                        act.wait_ge(diffed, 2 * i + h + 1)
                        nc.scalar.activation(st[h]["e2"][:], st[h]["dl"][:], ACT.Exp, scale=IWS).then_inc(e2_done, 1)

            @block.gpsimd
            def _(pool):
                with pool.Fori(0, PAIRS) as i:
                    for h in range(2):
                        norm_rstd(nc, ln, base + 2 * i + h + 1, wk[h], net.nhalf[:], net.eps[:])

            @block.tensor
            def _(pe):
                with pe.Fori(0, PAIRS) as i:
                    def n1(h):
                        return base + 2 * i + h + 1

                    for h in range(2):
                        turn(nc, ln, n1(h), wk[h], ps_t[:, h], net.ident16[:])
                    for h in range(2):
                        pe.wait_ge(ln["xT"], n1(h))
                        for g in range(NT):
                            last = natural(nc, net, ps_r[:, h, E3 * g:E3 * g + E3], wk[h]["xT"], g, "router")
                        last.then_inc(routed, 1)
                    for h in range(2):
                        n = 2 * i + h
                        for g in range(NT):
                            if g >= 4:
                                pe.wait_ge(weighted, piece_count(n, NT, g - 4))
                            elif h == 1:
                                pe.wait_ge(weighted, piece_count(2 * i, NT, NT + g - 4))
                            natural(nc, net, ps_e[:, g % 4], wk[h]["xT"], g, "exp3").then_inc(expert_out, 1)


STAGES = [stage_attend, stage_pool, stage_attend_qkv, stage_route]


INPUTS = ['x', 'L0_conv_ln1_g', 'L0_conv_ln1_b', 'L0_conv_qkv_w', 'L0_conv_qkv_b', 'L0_conv_proj_w', 'L0_conv_proj_b',
          'L0_conv_rpb', 'L0_conv_ln2_g', 'L0_conv_ln2_b', 'L0_conv_fc1_w', 'L0_conv_fc1_b', 'L0_conv_fc2_w',
          'L0_conv_fc2_b', 'L1_conv_W_left', 'L1_conv_b_left', 'L1_conv_W_right', 'L1_conv_b_right', 'L1_conv_W_gate',
          'L1_conv_b_gate', 'L1_conv_W_eq', 'L1_conv_b_eq', 'L1_conv_W_out', 'L1_conv_b_out', 'L1_conv_ln_scale',
          'L1_conv_ln_bias', 'L2_ffn_gate_w', 'L2_ffn_gate_b', 'L2_ffn_weight1', 'L2_ffn_weight2', 'L3_attn_Wq',
          'L3_attn_bq', 'L3_attn_Wk', 'L3_attn_bk', 'L3_attn_Wv', 'L3_attn_bv', 'L3_ffn_router_w', 'L3_ffn_router_b',
          'L3_ffn_expert_w', 'L3_ffn_expert_b']


def build(nc, d, k, out, stages=None):
    with ExitStack() as ctx:
        def sb(name, shape, dt):
            return ctx.enter_context(nc.sbuf_tensor(name, shape, dt))

        net = Net()
        net.nc, net.out = nc, out
        held = []

        def sem(name):
            held.append(nc.alloc_semaphore(name=name))
            return held[-1]

        net.sem = sem
        net.t = sb("tokens", [P, B, NT, C], F32)
        net.ident = sb("ident", [P, P], F32)
        net.ident16 = sb("ident16", [P, P], F16)
        net.perm16 = sb("perm16", [P, 2, P], F16)
        net.same16 = sb("same16", [P, P], F16)
        net.hmask = sb("hmask", [P, HEADS], F32)
        net.nhalf = sb("nhalf", [P, NT], F32)
        net.eps = sb("eps", [P, NT], F32)
        net.ones16 = sb("ones16", [2, 512], F16)
        net.wa = sb("wa", [P, NWC], F16)
        net.wb = sb("wb", [P, NWC], F16)
        net.bias = sb("bias", [2, NWC + C], F16)
        net.fc2h = sb("fc2h", [P, 2, C], F16)
        net.fc2l = sb("fc2l", [P, 2, C], F16)
        net.sbias = sb("sbias", [P, 2, 2, HEADS, C], F32)
        net.lns = sb("lns", [P, C], F32)
        net.lnb = sb("lnb", [P, C], F32)
        net.norms = [{part: net.sem(f"norm{j}_{part}") for part in NORM_PARTS} for j in range(3)]
        net.cuts = [{part: net.sem(f"cut{j}_{part}") for part in NORM_PARTS[6:]} for j in range(3)]
        net.t_ready = {part: net.sem(f"{part}_ready") for part in ("x1", "y", "t")}
        held.clear()

        def release():
            nc.clear_and_free_semaphores(held)
            nc.all_engine_barrier()
            held.clear()

        stage_setup(net, d, k)
        release()
        stage_blocks(net, d["x"])
        release()
        for st in STAGES:
            if stages is None or st.__name__ in stages:
                st(net, d)
                release()
        if stages is not None and "stage_route" not in stages:
            finish_store(net, out)



def constants():
    import numpy as np

    p, key = np.arange(P), np.arange(WIN * WIN)
    window, row, col = p // 64, p % 64 // WIN, p % WIN
    mask = np.zeros((P, 2, 2, 64), np.float32)
    for last_row in range(2):
        for jp in range(2):
            hidden = np.zeros((P, 64), bool)
            if last_row:
                hidden |= (row // 4)[:, None] != (key // 32)[None]
            if jp:
                hidden |= (window == 1)[:, None] & ((col // 4)[:, None] != (key % WIN // 4)[None])
            mask[:, last_row, jp] = np.where(hidden, np.float32(-1e9), np.float32(0))
    source = (np.arange(4)[None, :, None] * W
              + (WIN * np.arange(4)[:, None, None] + np.arange(WIN)[None, None, :] + WIN // 2) % W).reshape(-1)
    to_windows = np.zeros((P, P), np.float32)
    to_windows[source, p] = 1
    source = (64 * np.arange(2)[None, :, None] + WIN * np.arange(WIN)[:, None, None]
              + np.arange(WIN)[None, None, :]).reshape(-1)
    from_windows = np.zeros((P, P), np.float32)
    from_windows[source, p] = 1
    head = (np.arange(P) % 64 // HD)[:, None] == np.arange(HEADS)[None]
    return {"ident": np.eye(P, dtype=np.float32), "mask": mask, "hmask": head.astype(np.float32),
            "samerow": (p[:, None] // W == p[None] // W).astype(np.float32),
            "to_windows": to_windows, "from_windows": from_windows}


def kernel(**inputs):
    import numpy as _np
    import concourse.bacc as _bacc
    from concourse import mybir as _mybir
    from concourse.bass_utils import run_bass_kernel_spmd as _run

    nc = _bacc.Bacc("TRN2", target_bir_lowering=False, num_devices=1)
    arrays, d, k = {}, {}, {}
    for name in INPUTS:
        a = _np.ascontiguousarray(inputs[name])
        arrays[f"in_{name}_dram"] = a
        d[name] = nc.dram_tensor(f"in_{name}_dram", a.shape, _mybir.dt.from_np(a.dtype), kind="ExternalInput").ap()
    for name, a in constants().items():
        arrays[f"const_{name}_dram"] = a
        k[name] = nc.dram_tensor(f"const_{name}_dram", a.shape, _mybir.dt.from_np(a.dtype), kind="ExternalInput").ap()
    out = nc.dram_tensor("out_0_dram", (B, H, W, C), F32, kind="ExternalOutput").ap()
    build(nc, d, k, out)
    r = _run(nc, [arrays], core_ids=[0])
    return r.results[0]["out_0_dram"]
```

```python
from contextlib import ExitStack

import concourse.bass as bass
from concourse import mybir

ALU = mybir.AluOpType
ACT = mybir.ActivationFunctionType
AX = mybir.AxisListType
F32 = mybir.dt.float32
F16 = mybir.dt.float16

P = 128
B, H, W, C = 32, 32, 32, 64
TOK = H * W
NT = TOK // P
WIN = 8
NW_IMG = (H // WIN) * (W // WIN)
HEADS, HD = 4, C // 4
E2, HID = 32, 256
E3 = 8
FF = 4 * C
GRP = 4
NG = B // GRP
PAIRS = B // 2
WS = 64.0
IWS = 1.0 / WS
TEMP = (2 * C) ** 0.5
SHIFT2 = 55.0

COLS = {}
NWC = 0
for _name, _n in (("q", 2 * C), ("k", 2 * C), ("v", C), ("fc1", FF), ("proj", C), ("left", C), ("gatel", C),
                  ("right", C), ("out", C), ("gate2", E2), ("q3", 2 * C), ("k3", 2 * C), ("v3", C),
                  ("router", E3), ("exp3", E3 * C)):
    COLS[_name] = slice(NWC, NWC + _n)
    NWC += _n
LN1_COLS = slice(0, COLS["v"].stop)
LN2_COLS = COLS["fc1"]

NORM_PARTS = ("sum", "centred", "squared", "sumsq", "var", "rstd", "normed", "high", "pair", "turned", "xT")


def spread(ap, n):
    return ap.unsqueeze(2).to_broadcast([ap.shape[0], ap.shape[1], n])


def over(ap, n):
    return ap.unsqueeze(1).to_broadcast([ap.shape[0], n, ap.shape[1]])


def tiles(ap, a=NT):
    return ap.rearrange("p (a b) -> p a b", a=a)



def norm_sum(nc, ln, n1, src, w):
    nc.vector.tensor_reduce(w["sum"], src, AX.X, ALU.add).then_inc(ln["sum"], 1)


def norm_centre(nc, ln, n1, src, w):
    nc.vector.wait_ge(ln["sum"], n1)
    nc.vector.scalar_tensor_tensor(w["xc"], spread(w["sum"], C), -1.0 / C, src, ALU.mult,
                                   ALU.add).then_inc(ln["centred"], 1)


def norm_square(nc, ln, n1, w):
    nc.scalar.wait_ge(ln["centred"], n1)
    nc.scalar.activation(w["sq"], w["xc"], ACT.Square, scale=C ** -0.5).then_inc(ln["squared"], 1)


def norm_sumsq(nc, ln, n1, w):
    nc.vector.wait_ge(ln["squared"], n1)
    nc.vector.tensor_reduce(w["ss"], w["sq"], AX.X, ALU.add).then_inc(ln["sumsq"], 1)


def norm_rstd(nc, ln, n1, w, nhalf, eps):
    nc.gpsimd.wait_ge(ln["sumsq"], n1)
    nc.gpsimd.tensor_tensor(w["var"], w["ss"], eps, ALU.add).then_inc(ln["var"], 1)
    nc.gpsimd.wait_ge(ln["var"], n1)
    nc.gpsimd.tensor_tensor(w["rstd"], w["var"], nhalf, ALU.pow).then_inc(ln["rstd"], 1)


def norm_apply(nc, ln, n1, w):
    nc.vector.wait_ge(ln["rstd"], n1)
    nc.vector.tensor_tensor(w["xn"], w["xc"], spread(w["rstd"], C), ALU.mult).then_inc(ln["normed"], 1)



def cut_high(nc, ln, n1, w, x):
    nc.scalar.wait_ge(ln["normed"], n1)
    nc.scalar.activation(w["hl"][:, :, 0:C], x, ACT.Identity).then_inc(ln["high"], 1)


def cut_low(nc, ln, n1, w, x):
    nc.vector.wait_ge(ln["high"], n1)
    nc.vector.tensor_tensor(w["hl"][:, :, C:2 * C], x, w["hl"][:, :, 0:C], ALU.subtract).then_inc(ln["pair"], 1)


def turn(nc, ln, n1, w, bank, ident16):
    nc.tensor.wait_ge(ln["pair"], n1)
    for g in range(NT):
        last = nc.tensor.transpose(bank[:, g * P:(g + 1) * P], w["hl"][:, g, 0:2 * C], ident16)
    last.then_inc(ln["turned"], 1)


def take_turned(nc, ln, n1, w, bank):
    nc.vector.wait_ge(ln["turned"], n1)
    nc.vector.tensor_copy(w["xT"], bank).then_inc(ln["xT"], 1)


def turn_to_windows(nc, ln, n1, w, bank, perm):
    nc.tensor.wait_ge(ln["pair"], n1)
    for g in range(NT):
        half = (g + NT - 1) % NT
        at = (half // 2) * 4 * WIN * WIN + (half % 2) * WIN * WIN // 2
        out = bank.rearrange("p (w t) -> p w t", t=WIN * WIN)[:, at // 64:at // 64 + 4, at % 64:at % 64 + 32]
        last = nc.tensor.transpose(out, w["hl"][:, g, 0:2 * C], perm)
    last.then_inc(ln["turned"], 1)


def turn_from_windows(nc, ln, n1, w, bank, perm):
    nc.tensor.wait_ge(ln["pair"], n1)
    for g in range(NT):
        rows = bank.rearrange("p (r c) -> p r c", c=W)[:, WIN * (g // 2):WIN * (g // 2) + WIN,
                                                       16 * (g % 2):16 * (g % 2) + 16]
        last = nc.tensor.transpose(rows, w["hl"][:, g, 0:2 * C], perm)
    last.then_inc(ln["turned"], 1)


def take_unrolled(nc, ln, n1, w, bank):
    nc.vector.wait_ge(ln["turned"], n1)
    s, image = WIN // 2, w["xT"].rearrange("p (r c) -> p r c", c=W)
    rolled = bank.rearrange("p (r c) -> p r c", c=W)
    for r0, r1, to_r in ((0, H - s, s), (H - s, H, 0)):
        for c0, c1, to_c in ((0, W - s, s), (W - s, W, 0)):
            last = nc.vector.tensor_copy(image[:, to_r:to_r + r1 - r0, to_c:to_c + c1 - c0], rolled[:, r0:r1, c0:c1])
    last.then_inc(ln["xT"], 1)


class Net:
    pass


def work_buffers(sb, name):
    w = {}
    for k, shape, dt in (("sum", [P, NT], F32), ("ss", [P, NT], F32), ("var", [P, NT], F32), ("rstd", [P, NT], F32),
                         ("xc", [P, NT, C], F32), ("sq", [P, NT, C], F32), ("xn", [P, NT, C], F32),
                         ("hl", [P, NT, 3 * C], F16), ("xT", [P, TOK], F16)):
        w[k] = sb(f"{name}_{k}", shape, dt)[:]
    return w


def stage_setup(net, d, k):
    nc, sem = net.nc, net.sem
    with ExitStack() as ctx:
        def sb(name, shape, dt):
            return ctx.enter_context(nc.sbuf_tensor("su_" + name, shape, dt))

        wc = sb("wc", [P, NWC], F32)
        wh = sb("wh", [P, NWC], F16)
        wl = sb("wl", [P, NWC], F16)
        weq = sb("weq", [P, C], F32)
        raw3 = sb("raw3", [C, 3, 2, C], F32)
        rawg = sb("rawg", [E2, 2, C], F32)
        gains = sb("gains", [P, 2], F32)
        lnb = sb("lnb", [C, 2, 2], F32)
        brf = sb("brf", [2, NWC + C], F32)
        beq = sb("beq", [2, C], F32)
        bh = sb("bh", [2, NWC + C], F16)
        bl = sb("bl", [2, NWC + C], F16)
        fc2 = sb("fc2", [P, 2, C], F32)
        rb = sb("rb", [P, C, HEADS], F32)
        mask = sb("mask", [P, 2, 2, C], F32)
        same = sb("same", [P, P], F32)
        perms = sb("perms", [P, 2, P], F32)
        ps_t = ctx.enter_context(nc.psum_tensor("su_ps_t", [P, 512], F32))
        ps_b = ctx.enter_context(nc.psum_tensor("su_ps_b", [2, 512], F32))
        ps_c = ctx.enter_context(nc.psum_tensor("su_ps_c", [2, 512], F32))

        loaded, chain = sem("setup_loaded"), sem("setup_chain")
        turned, folded = sem("setup_turned"), sem("setup_folded")
        b_loaded, doubled, paired = sem("setup_b_loaded"), sem("setup_doubled"), sem("setup_paired")
        raw_doubled = sem("setup_raw_doubled")
        ndma, nb = [0], [0]

        with nc.Block() as block:
            @block.sync
            def _(sp):
                def load(dst, src):
                    sp.dma_start(dst, src).then_inc(loaded, 16)
                    ndma[0] += 1

                load(net.ident[:], k["ident"])
                load(net.hmask[:], k["hmask"])
                load(perms[:, 0], k["to_windows"])
                load(perms[:, 1], k["from_windows"])
                load(same[:], k["samerow"])
                load(mask[:], k["mask"])
                pieces = [("q", 2 * C, d["L0_conv_qkv_w"]), ("fc1", 0, d["L0_conv_fc1_w"]),
                          ("proj", 0, d["L0_conv_proj_w"]), ("left", 0, d["L1_conv_W_left"]),
                          ("gatel", 0, d["L1_conv_W_gate"]), ("right", 0, d["L1_conv_W_right"]),
                          ("out", 0, d["L1_conv_W_out"]), ("router", 0, d["L3_ffn_router_w"])]
                for name, at, src in pieces:
                    a = COLS[name].start + at
                    load(wc[0:C, a:a + src.shape[1]], src)
                load(wc[0:C, COLS["exp3"]].rearrange("p (e c) -> p e c", e=E3),
                     d["L3_ffn_expert_w"].rearrange("e d c -> d e c"))
                load(weq[0:C, :], d["L1_conv_W_eq"])
                for half in (0, C):
                    load(gains[half:half + C, 0:1], d["L0_conv_ln1_g"].unsqueeze(1))
                    load(gains[half:half + C, 1:2], d["L0_conv_ln2_g"].unsqueeze(1))
                for j, name in enumerate(("L3_attn_Wq", "L3_attn_Wk", "L3_attn_Wv")):
                    load(raw3[:, j, 0, :], d[name])
                load(rawg[:, 0, :], d["L2_ffn_gate_w"])
                load(lnb[:, 0, 0:1], d["L0_conv_ln1_b"].unsqueeze(1))
                load(lnb[:, 1, 0:1], d["L0_conv_ln2_b"].unsqueeze(1))
                load(fc2[:], d["L0_conv_fc2_w"].rearrange("(a p) n -> p a n", a=2))
                load(net.lns[:], d["L1_conv_ln_scale"].unsqueeze(0).to_broadcast([P, C]))
                load(net.lnb[:], d["L1_conv_ln_bias"].unsqueeze(0).to_broadcast([P, C]))
                table = d["L0_conv_rpb"]
                side = 2 * WIN - 1
                for w2 in range(2):
                    for kr in range(WIN):
                        src = bass.AP(table.tensor, table.offset + side * HEADS * kr,
                                      [[side * HEADS, WIN], [HEADS, WIN], [1, WIN * HEADS]])
                        load(rb[64 * w2:64 * w2 + 64, WIN * kr:WIN * kr + WIN, :].rearrange("p k h -> p (k h)"), src)
                sp.wait_ge(paired, 1)
                sp.dma_start(wc[C:P, :], wc[0:C, :]).then_inc(doubled, 16)
                sp.dma_start(brf[1:2, :], brf[0:1, :]).then_inc(doubled, 16)

            @block.gpsimd
            def _(pool):
                qb = d["L0_conv_qkv_b"]
                rows = [("q", 2 * C, qb), ("fc1", 0, d["L0_conv_fc1_b"]), ("proj", 0, d["L0_conv_proj_b"]),
                        ("left", 0, d["L1_conv_b_left"]), ("gatel", 0, d["L1_conv_b_gate"]),
                        ("right", 0, d["L1_conv_b_right"]), ("out", 0, d["L1_conv_b_out"]),
                        ("gate2", 0, d["L2_ffn_gate_b"]), ("q3", 0, d["L3_attn_bq"]),
                        ("k3", 0, d["L3_attn_bk"]), ("v3", 0, d["L3_attn_bv"]),
                        ("router", 0, d["L3_ffn_router_b"]),
                        ("exp3", 0, d["L3_ffn_expert_b"].rearrange("e c -> (e c)"))]
                for name, at, src in rows:
                    a = COLS[name].start + at
                    pool.dma_start(brf[0:1, a:a + src.shape[0]], src.unsqueeze(0)).then_inc(b_loaded, 16)
                pool.dma_start(brf[0:1, NWC:NWC + C], d["L0_conv_fc2_b"].unsqueeze(0)).then_inc(b_loaded, 16)
                pool.dma_start(beq[0:1, :], d["L1_conv_b_eq"].unsqueeze(0)).then_inc(b_loaded, 16)
                nb[0] = len(rows) + 2

            @block.vector
            def _(dve):
                done = [0]

                def link(ins):
                    done[0] += 1
                    ins.then_inc(chain, 1)
                    dve.wait_ge(chain, done[0])

                nc.vector.memset(net.nhalf[:], -0.5)
                nc.vector.memset(net.eps[:], 1e-5)
                nc.vector.memset(net.ones16[:], 1.0)
                dve.wait_ge(loaded, 16 * ndma[0])
                nc.vector.tensor_copy(net.ident16[:], net.ident[:])
                nc.vector.tensor_copy(net.same16[:], same[:])
                nc.vector.tensor_copy(net.perm16[:], perms[:])
                dve.wait_ge(b_loaded, 16 * nb[0])
                nc.vector.tensor_copy(raw3[:, :, 1, :], raw3[:, :, 0, :])
                nc.vector.tensor_copy(rawg[:, 1, :], rawg[:, 0, :])
                link(nc.vector.tensor_copy(lnb[:, :, 1:2], lnb[:, :, 0:1]))
                nc.vector.engine_nop().then_inc(raw_doubled, 1)
                q, k_, v_ = COLS["q"].start, COLS["k"].start, COLS["v"].start
                for tensor in (wc[0:C, :], brf[0:1, :]):
                    link(nc.vector.tensor_copy(tensor[:, q:q + C], tensor[:, q + 2 * C:q + 3 * C]))
                    link(nc.vector.tensor_copy(tensor[:, q + C:q + 2 * C], tensor[:, q:q + C]))
                    link(nc.vector.tensor_copy(tensor[:, k_:k_ + C], tensor[:, k_ + C:k_ + 2 * C]))
                link(nc.vector.tensor_tensor(wc[0:C, COLS["left"]], wc[0:C, COLS["left"]], weq[0:C, :], ALU.add))
                link(nc.vector.tensor_tensor(brf[0:1, COLS["left"]], brf[0:1, COLS["left"]], beq[0:1, :], ALU.add))
                for name in ("q3", "k3"):
                    a = COLS[name].start
                    link(nc.vector.tensor_copy(brf[0:1, a + C:a + 2 * C], brf[0:1, a:a + C]))
                dve.wait_ge(turned, 1)
                for j, name in enumerate(("q3", "k3")):
                    for r in range(2):
                        a = COLS[name].start + r * C
                        nc.vector.tensor_copy(wc[0:C, a:a + C], ps_t[0:C, j * C:(j + 1) * C])
                nc.vector.tensor_copy(wc[0:C, COLS["v3"]], ps_t[0:C, 2 * C:3 * C])
                nc.vector.tensor_copy(wc[0:C, COLS["gate2"]], ps_t[0:C, 3 * C:3 * C + E2]).then_inc(paired, 1)
                dve.wait_ge(doubled, 32)
                dve.wait_ge(folded, 1)
                link(nc.vector.tensor_tensor(brf[:, LN1_COLS], brf[:, LN1_COLS], ps_b[:, LN1_COLS], ALU.add))
                link(nc.vector.tensor_tensor(brf[:, LN2_COLS], brf[:, LN2_COLS], ps_c[:, 0:FF], ALU.add))
                link(nc.vector.tensor_scalar(brf[:], brf[:], WS, None, ALU.mult))
                link(nc.vector.tensor_copy(bh[:], brf[:]))
                link(nc.vector.tensor_tensor(bl[:], brf[:], bh[:], ALU.subtract))
                link(nc.vector.tensor_scalar(bh[:], bh[:], net.ident[0:2, 0:1], None, ALU.mult))
                link(nc.vector.scalar_tensor_tensor(net.bias[:], bl[:], net.ident[0:2, 1:2], bh[:], ALU.mult,
                                                    ALU.add))
                link(nc.vector.tensor_scalar(wc[:, LN1_COLS], wc[:, LN1_COLS], gains[:, 0:1], WS, ALU.mult, ALU.mult))
                link(nc.vector.tensor_scalar(wc[:, LN2_COLS], wc[:, LN2_COLS], gains[:, 1:2], WS, ALU.mult, ALU.mult))
                rest = slice(LN2_COLS.stop, NWC)
                link(nc.vector.tensor_scalar(wc[:, rest], wc[:, rest], WS, None, ALU.mult))
                link(nc.vector.tensor_copy(wh[:], wc[:]))
                link(nc.vector.tensor_tensor(wl[:], wc[:], wh[:], ALU.subtract))
                nc.vector.tensor_copy(net.wa[0:C, :], wh[0:C, :])
                nc.vector.tensor_copy(net.wa[C:P, :], wl[C:P, :])
                nc.vector.tensor_copy(net.wb[0:C, :], wl[0:C, :])
                nc.vector.tensor_copy(net.wb[C:P, :], wh[C:P, :])
                link(nc.vector.tensor_scalar(fc2[:], fc2[:], WS, None, ALU.mult))
                link(nc.vector.tensor_copy(net.fc2h[:], fc2[:]))
                nc.vector.tensor_tensor(net.fc2l[:], fc2[:], net.fc2h[:], ALU.subtract)
                for last_row in range(2):
                    for jp in range(2):
                        back = rb[:].rearrange("p (r c) h -> p h r c", r=WIN)[:, :, ::-1, ::-1]
                        for hd in range(HEADS):
                            nc.vector.tensor_tensor(
                                net.sbias[:, last_row, jp, hd].rearrange("p (r c) -> p r c", c=WIN), back[:, hd],
                                mask[:, last_row, jp].rearrange("p (r c) -> p r c", c=WIN), ALU.add)

            @block.tensor
            def _(pe):
                pe.wait_ge(loaded, 16 * ndma[0])
                pe.wait_ge(raw_doubled, 1)
                for j in range(3):
                    nc.tensor.transpose(ps_t[:, j * C:(j + 1) * C], raw3[:, j].rearrange("p r c -> p (r c)"),
                                        net.ident[0:C, 0:C])
                nc.tensor.transpose(ps_t[:, 3 * C:3 * C + E2], rawg[:].rearrange("p r c -> p (r c)"),
                                    net.ident[0:E2, 0:E2]).then_inc(turned, 1)
                pe.wait_ge(doubled, 32)
                nc.tensor.matmul(ps_b[:, LN1_COLS], lnb[:, 0, :], wc[0:C, LN1_COLS], start=True, stop=True)
                nc.tensor.matmul(ps_c[:, 0:FF], lnb[:, 1, :], wc[0:C, LN2_COLS], start=True,
                                 stop=True).then_inc(folded, 1)


def matmul_pair(nc, out, lhsT, rhs_a, rhs_b, bias_l, bias_r, stop=True):
    nc.tensor.matmul(out, lhsT, rhs_a, start=True, stop=False)
    nc.tensor.matmul(out, lhsT, rhs_b, start=False, stop=False)
    return nc.tensor.matmul(out, bias_l, bias_r, start=False, stop=stop)


def natural(nc, net, out, xT, g, name):
    c = COLS[name]
    return matmul_pair(nc, out, xT[:, g * P:(g + 1) * P], net.wa[:, c], net.wb[:, c], net.ones16[:, 0:P],
                       net.bias[:, c])


def upright(nc, net, out, xT, c, lo, hi):
    nc.tensor.matmul(out, net.wa[:, c], xT[:, lo:hi], start=True, stop=False)
    nc.tensor.matmul(out, net.wb[:, c], xT[:, lo:hi], start=False, stop=False)
    return nc.tensor.matmul(out, net.bias[:, c], net.ones16[:, 0:hi - lo], start=False, stop=True)


def stage_blocks(net, x):
    nc, sem = net.nc, net.sem
    with ExitStack() as ctx:
        def sb(name, shape, dt):
            return ctx.enter_context(nc.sbuf_tensor("bl_" + name, shape, dt))

        wk, qx, kh, kl, kxh, kxl, vh, vl, att, pth, ptl, rs, rinv, on, x1, x2 = ([] for _ in range(16))
        gel, glh, gll, rh, rl, rss, th, u = ([] for _ in range(8))
        for h in range(2):
            wk.append(work_buffers(sb, f"w{h}"))
            qx.append(sb(f"qx{h}", [P, TOK], F16))
            kh.append(sb(f"kh{h}", [P, TOK], F16))
            kl.append(sb(f"kl{h}", [P, TOK], F16))
            kxh.append(sb(f"kxh{h}", [P, HEADS, TOK], F16))
            kxl.append(sb(f"kxl{h}", [P, HEADS, TOK], F16))
            vh.append(sb(f"vh{h}", [P, NW_IMG, 2, 2, HD], F16))
            vl.append(sb(f"vl{h}", [P, NW_IMG, 2, 2, HD], F16))
            att.append(sb(f"att{h}", [P, 2, 2, HEADS, C], F32))
            pth.append(sb(f"pth{h}", [P, 2, 4, P], F16))
            ptl.append(sb(f"ptl{h}", [P, 2, 4, P], F16))
            rs.append(sb(f"rs{h}", [P, NT, HEADS], F32))
            rinv.append(sb(f"rinv{h}", [P, NT, HEADS], F32))
            on.append(sb(f"on{h}", [P, NT, C], F32))
            x1.append(sb(f"x1{h}", [P, NT, C], F32))
            x2.append(sb(f"x2{h}", [P, NT, C], F32))
            gel.append(kxh[h][:].rearrange("p a b -> p (a b)").bitcast(F32).rearrange("p (a b) -> p a b", a=2))
            glh.append(kxl[h][:, 0:2, :])
            gll.append(kxl[h][:, 2:4, :])
            rh.append(sb(f"rh{h}", [P, NT, C], F16))
            rl.append(sb(f"rl{h}", [P, NT, C], F16))
            rss.append(sb(f"rss{h}", [P, NT, C], F32))
            th.append(sb(f"th{h}", [P, NT, C], F32))
            u.append(sb(f"u{h}", [P, NT, C], F32))
        ps = ctx.enter_context(nc.psum_tensor("bl_ps", [P, 8, 512], F32))

        def bank(h, j, n=1):
            return ps[:, 4 * h + j:4 * h + j + n, :].rearrange("p b n -> p (b n)")

        def bank16(h, j):
            return ps[:, 4 * h + j, :].bitcast(F16)

        ln1, ln2, ln3 = net.norms
        co, cx, cu = net.cuts
        x_loaded = sem("x_loaded")
        q_ready, q_taken, kh_taken, kl_taken, k_spread = (sem("bl_" + s) for s in (
            "q_projected", "qh_taken", "kh_taken", "kl_taken", "k_spread"))
        k_ready, ql_taken, v_ready, vh_taken, v_taken = (sem("bl_" + s) for s in (
            "k_projected", "q_taken", "v_projected", "vh_taken", "v_taken"))
        scored, biased, maxed, shifted, exped, summed = (sem("bl_" + s) for s in (
            "scored", "biased", "maxed", "shifted", "exped", "summed"))
        p_turned, ph_taken, pl_taken, weighed, inverted = (sem("bl_" + s) for s in (
            "p_turned", "ph_taken", "pl_taken", "weighed", "inverted"))
        projected, hid_ready, gelued, gh_cut, gl_cut, ffn_out = (sem("bl_" + s) for s in (
            "projected", "hid_ready", "gelued", "gh_cut", "gl_cut", "ffn_out"))
        x2_done, r_ready, rh_taken, rl_taken, lg_ready, rowsummed = (sem("bl_" + s) for s in (
            "x2_done", "r_ready", "rh_taken", "rl_taken", "lg_ready", "rowsummed"))
        rss_taken, tanhed, lefted, outed, scaled, zeroed = (sem("bl_" + s) for s in (
            "rss_taken", "tanhed", "lefted", "outed", "scaled", "zeroed"))
        stored = net.t_ready

        tv = net.t[:].rearrange("p (i h) g c -> p i h g c", h=2)
        tp, xv = pairs_of_tiles(net.t, x)

        with nc.Block() as block:
            @block.sync
            def _(sp):
                sp.dma_start(tp[:, 0], xv[:, 0]).then_inc(x_loaded, 16)
                with sp.Fori(1, PAIRS) as i:
                    sp.wait_ge(x_loaded, 16 * i)
                    sp.dma_start(tp[:, i], xv[:, i]).then_inc(x_loaded, 16)

            @block.vector
            def _(dve):
                for h in range(2):
                    nc.vector.memset(vh[h][:], 0.0)
                    nc.vector.memset(vl[h][:], 0.0).then_inc(zeroed, 1)
                with dve.Fori(0, PAIRS) as i:
                    def n1(h):
                        return 2 * i + h + 1

                    def m1(h, c):
                        return 8 * i + 2 * c + h + 1

                    dve.wait_ge(x_loaded, 16 * (i + 1))
                    for h in range(2):
                        norm_sum(nc, ln1, n1(h), tv[:, i, h], wk[h])
                    for h in range(2):
                        norm_centre(nc, ln1, n1(h), tv[:, i, h], wk[h])
                    for h in range(2):
                        norm_sumsq(nc, ln1, n1(h), wk[h])
                    for h in range(2):
                        norm_apply(nc, ln1, n1(h), wk[h])
                    for h in range(2):
                        cut_low(nc, ln1, n1(h), wk[h], wk[h]["xn"])
                    for h in range(2):
                        take_turned(nc, ln1, n1(h), wk[h], bank16(h, 0))
                    for h in range(2):
                        dve.wait_ge(q_taken, n1(h))
                        nc.vector.scalar_tensor_tensor(qx[h][C:P, :], bank(h, 0, 2)[C:P, :], IWS, qx[h][C:P, :],
                                                       ALU.mult, ALU.subtract).then_inc(ql_taken, 1)
                        dve.wait_ge(kh_taken, n1(h))
                        nc.vector.scalar_tensor_tensor(kl[h][:], bank(h, 2, 2), IWS, kh[h][:],
                                                       ALU.mult, ALU.subtract).then_inc(kl_taken, 1)
                    for h in range(2):
                        dve.wait_ge(kl_taken, n1(h))
                        for hd in range(HEADS):
                            nc.vector.tensor_scalar(kxh[h][:, hd, :], kh[h][:], net.hmask[:, hd:hd + 1], None, ALU.mult)
                            last = nc.vector.tensor_scalar(kxl[h][:, hd, :], kl[h][:], net.hmask[:, hd:hd + 1], None,
                                                           ALU.mult)
                        last.then_inc(k_spread, 1)
                    dve.wait_ge(zeroed, 2)
                    for h in range(2):
                        dve.wait_ge(vh_taken, n1(h))
                        for hp in range(2):
                            half = slice(C * hp, C * hp + C)
                            last = nc.vector.scalar_tensor_tensor(
                                vl[h][half, :, :, hp, :].rearrange("p w a d -> p (w a) d"),
                                bank(h, 0)[half, :].rearrange("p (w d) -> p w d", d=HD), IWS,
                                vh[h][half, :, :, hp, :].rearrange("p w a d -> p (w a) d"), ALU.mult, ALU.subtract)
                        last.then_inc(v_taken, 1)
                    for c in range(5):
                        for h in range(2):
                            if c < 4:
                                a = att[h][:, c % 2].rearrange("p t a k -> p (t a) k")
                                dve.wait_ge(scored, m1(h, c))
                                if c >= 2:
                                    dve.wait_ge(pl_taken, m1(h, c - 2))
                                nc.vector.scalar_tensor_tensor(
                                    a, tiles(bank(h, c % 2)), HD ** -0.5,
                                    net.sbias[:, int(c == 3)].rearrange("p t a k -> p (t a) k"),
                                    ALU.mult, ALU.add).then_inc(biased, 1)
                                dve.wait_ge(biased, m1(h, c))
                                nc.vector.tensor_reduce(wk[h]["sum"], a, AX.X, ALU.max).then_inc(maxed, 1)
                                dve.wait_ge(maxed, m1(h, c))
                                nc.vector.tensor_tensor(a, a, spread(wk[h]["sum"], C),
                                                        ALU.subtract).then_inc(shifted, 1)
                            if c >= 1:
                                a = att[h][:, (c - 1) % 2].rearrange("p t a k -> p (t a) k")
                                dve.wait_ge(exped, m1(h, c - 1))
                                nc.vector.tensor_reduce(rs[h][:, 2 * c - 2:2 * c].rearrange("p t a -> p (t a)"), a,
                                                        AX.X, ALU.add).then_inc(summed, 1)
                                dve.wait_ge(ph_taken, m1(h, c - 1))
                                nc.vector.tensor_tensor(ptl[h][:, (c - 1) % 2], tiles(bank(h, 2), 4),
                                                        pth[h][:, (c - 1) % 2], ALU.subtract).then_inc(pl_taken, 1)
                    for h in range(2):
                        dve.wait_ge(summed, m1(h, 3))
                        nc.vector.reciprocal(rinv[h][:], rs[h][:]).then_inc(inverted, 1)
                        dve.wait_ge(inverted, n1(h))
                        dve.wait_ge(weighed, m1(h, 3))
                        nc.vector.tensor_tensor(
                            on[h][:].rearrange("p t (a d) -> p (t a) d", a=HEADS),
                            bank(h, 3).rearrange("p (ta d) -> p ta d", d=HD),
                            spread(rinv[h][:].rearrange("p t a -> p (t a)"), HD), ALU.mult).then_inc(co["normed"], 1)
                    for h in range(2):
                        cut_low(nc, co, n1(h), wk[h], on[h][:])
                    for h in range(2):
                        take_unrolled(nc, co, n1(h), wk[h], bank16(h, 0))
                    for h in range(2):
                        dve.wait_ge(projected, n1(h))
                        nc.vector.scalar_tensor_tensor(x1[h][:], tiles(bank(h, 1)), IWS, tv[:, i, h],
                                                       ALU.mult, ALU.add).then_inc(stored["x1"], 1)
                    for h in range(2):
                        dve.wait_ge(stored["x1"], n1(h))
                        norm_sum(nc, ln2, n1(h), x1[h][:], wk[h])
                    for h in range(2):
                        norm_centre(nc, ln2, n1(h), x1[h][:], wk[h])
                    for h in range(2):
                        norm_sumsq(nc, ln2, n1(h), wk[h])
                    for h in range(2):
                        norm_apply(nc, ln2, n1(h), wk[h])
                    for h in range(2):
                        cut_low(nc, ln2, n1(h), wk[h], wk[h]["xn"])
                    for h in range(2):
                        take_turned(nc, ln2, n1(h), wk[h], bank16(h, 0))
                    for h in range(2):
                        for a in range(2):
                            dve.wait_ge(gelued, 4 * i + 2 * h + a + 1)
                            nc.vector.tensor_copy(glh[h][:, a], gel[h][:, a]).then_inc(gh_cut, 1)
                    for h in range(2):
                        dve.wait_ge(ffn_out, n1(h))
                        nc.vector.scalar_tensor_tensor(x2[h][:], tiles(bank(h, 2)), IWS, x1[h][:],
                                                       ALU.mult, ALU.add).then_inc(cx["normed"], 1)
                    for h in range(2):
                        cut_low(nc, cx, n1(h), wk[h], x2[h][:])
                    for h in range(2):
                        take_turned(nc, cx, n1(h), wk[h], bank16(h, 0))
                    for h in range(2):
                        dve.wait_ge(rh_taken, n1(h))
                        nc.vector.scalar_tensor_tensor(rl[h][:], tiles(bank(h, 1)), IWS, rh[h][:],
                                                       ALU.mult, ALU.subtract).then_inc(rl_taken, 1)
                    for h in range(2):
                        dve.wait_ge(rss_taken, n1(h))
                        dve.wait_ge(lg_ready, n1(h))
                        nc.vector.tensor_tensor(u[h][:], tiles(bank(h, 2)), rss[h][:], ALU.mult).then_inc(lefted, 1)
                        dve.wait_ge(lefted, n1(h))
                        dve.wait_ge(tanhed, n1(h))
                        nc.vector.scalar_tensor_tensor(u[h][:], th[h][:], 1.0, u[h][:], ALU.add,
                                                       ALU.mult).then_inc(cu["normed"], 1)
                    for h in range(2):
                        cut_low(nc, cu, n1(h), wk[h], u[h][:])
                    for h in range(2):
                        take_turned(nc, cu, n1(h), wk[h], bank16(h, 1))
                    for h in range(2):
                        dve.wait_ge(outed, n1(h))
                        nc.vector.scalar_tensor_tensor(x1[h][:], tiles(bank(h, 2)), IWS, x2[h][:],
                                                       ALU.mult, ALU.add).then_inc(stored["y"], 1)
                    for h in range(2):
                        dve.wait_ge(stored["y"], n1(h))
                        norm_sum(nc, ln3, n1(h), x1[h][:], wk[h])
                    for h in range(2):
                        norm_centre(nc, ln3, n1(h), x1[h][:], wk[h])
                    for h in range(2):
                        norm_sumsq(nc, ln3, n1(h), wk[h])
                    for h in range(2):
                        norm_apply(nc, ln3, n1(h), wk[h])
                    for h in range(2):
                        dve.wait_ge(ln3["normed"], n1(h))
                        nc.vector.tensor_tensor(on[h][:], wk[h]["xn"], over(net.lns[:], NT), ALU.mult).then_inc(scaled, 1)
                    for h in range(2):
                        dve.wait_ge(scaled, n1(h))
                        nc.vector.tensor_tensor(tv[:, i, h], on[h][:], over(net.lnb[:], NT),
                                                ALU.add).then_inc(stored["t"], 1)

            @block.scalar
            def _(act):
                with act.Fori(0, PAIRS) as i:
                    def n1(h):
                        return 2 * i + h + 1

                    def m1(h, c):
                        return 8 * i + 2 * c + h + 1

                    for h in range(2):
                        norm_square(nc, ln1, n1(h), wk[h])
                    for h in range(2):
                        cut_high(nc, ln1, n1(h), wk[h], wk[h]["xn"])
                    for h in range(2):
                        act.wait_ge(q_ready, n1(h))
                        nc.scalar.activation(qx[h][:], bank(h, 0, 2), ACT.Copy, scale=IWS).then_inc(q_taken, 1)
                        act.wait_ge(k_ready, n1(h))
                        nc.scalar.activation(kh[h][:], bank(h, 2, 2), ACT.Copy, scale=IWS).then_inc(kh_taken, 1)
                    act.wait_ge(zeroed, 2)
                    for h in range(2):
                        act.wait_ge(v_ready, n1(h))
                        for hp in range(2):
                            half = slice(C * hp, C * hp + C)
                            last = nc.scalar.activation(
                                vh[h][half, :, :, hp, :].rearrange("p w a d -> p (w a) d"),
                                bank(h, 0)[half, :].rearrange("p (w d) -> p w d", d=HD), ACT.Copy, scale=IWS)
                        last.then_inc(vh_taken, 1)
                    for c in range(4):
                        for h in range(2):
                            a = att[h][:, c % 2].rearrange("p t a k -> p (t a k)")
                            act.wait_ge(shifted, m1(h, c))
                            nc.scalar.activation(a, a, ACT.Exp).then_inc(exped, 1)
                        for h in range(2):
                            act.wait_ge(p_turned, m1(h, c))
                            nc.scalar.activation(pth[h][:, c % 2], tiles(bank(h, 2), 4), ACT.Copy).then_inc(ph_taken, 1)
                    for h in range(2):
                        cut_high(nc, co, n1(h), wk[h], on[h][:])
                    for h in range(2):
                        norm_square(nc, ln2, n1(h), wk[h])
                    for h in range(2):
                        cut_high(nc, ln2, n1(h), wk[h], wk[h]["xn"])
                    for h in range(2):
                        for a in range(2):
                            act.wait_ge(hid_ready, 4 * i + 2 * h + a + 1)
                            nc.scalar.activation(gel[h][:, a], bank(h, 2 - 2 * a, 2), ACT.Gelu_apprx_tanh,
                                                 scale=IWS).then_inc(gelued, 1)
                    for h in range(2):
                        cut_high(nc, cx, n1(h), wk[h], x2[h][:])
                    for h in range(2):
                        act.wait_ge(r_ready, n1(h))
                        nc.scalar.activation(rh[h][:], tiles(bank(h, 1)), ACT.Copy, scale=IWS).then_inc(rh_taken, 1)
                    for h in range(2):
                        act.wait_ge(lg_ready, n1(h))
                        nc.scalar.activation(th[h][:], tiles(bank(h, 3)), ACT.Tanh, scale=0.5 * IWS).then_inc(tanhed, 1)
                        act.wait_ge(rowsummed, n1(h))
                        nc.scalar.activation(rss[h][:], tiles(bank(h, 0)), ACT.Copy,
                                             scale=0.5 * IWS).then_inc(rss_taken, 1)
                    for h in range(2):
                        cut_high(nc, cu, n1(h), wk[h], u[h][:])
                    for h in range(2):
                        norm_square(nc, ln3, n1(h), wk[h])

            @block.gpsimd
            def _(pool):
                with pool.Fori(0, PAIRS) as i:
                    def n1(h):
                        return 2 * i + h + 1

                    for h in range(2):
                        norm_rstd(nc, ln1, n1(h), wk[h], net.nhalf[:], net.eps[:])
                    for h in range(2):
                        norm_rstd(nc, ln2, n1(h), wk[h], net.nhalf[:], net.eps[:])
                    for h in range(2):
                        for a in range(2):
                            pool.wait_ge(gh_cut, 4 * i + 2 * h + a + 1)
                            nc.gpsimd.tensor_tensor(gll[h][:, a], gel[h][:, a], glh[h][:, a],
                                                    ALU.subtract).then_inc(gl_cut, 1)
                    for h in range(2):
                        norm_rstd(nc, ln3, n1(h), wk[h], net.nhalf[:], net.eps[:])

            @block.tensor
            def _(pe):
                with pe.Fori(0, PAIRS) as i:
                    def n1(h):
                        return 2 * i + h + 1

                    def m1(h, c):
                        return 8 * i + 2 * c + h + 1

                    for h in range(2):
                        turn_to_windows(nc, ln1, n1(h), wk[h], bank16(h, 0), net.perm16[:, 0])
                    for h in range(2):
                        xT = wk[h]["xT"]
                        pe.wait_ge(ln1["xT"], n1(h))
                        for half in range(2):
                            last = upright(nc, net, bank(h, half), xT, COLS["q"], 512 * half, 512 * half + 512)
                        last.then_inc(q_ready, 1)
                        for half in range(2):
                            last = upright(nc, net, bank(h, 2 + half), xT, COLS["k"], 512 * half, 512 * half + 512)
                        last.then_inc(k_ready, 1)
                    for h in range(2):
                        pe.wait_ge(ql_taken, n1(h))
                        for w in range(NW_IMG):
                            for hp in range(2):
                                def heads(ap):
                                    return ap[:, COLS["v"]].rearrange("p (a b d) -> p a b d", a=2, b=2)[:, :, hp, :]
                                last = matmul_pair(nc, bank(h, 0)[C * hp:C * hp + C, 32 * w:32 * w + 32],
                                                   wk[h]["xT"][:, C * w:C * w + C], heads(net.wa), heads(net.wb),
                                                   net.ones16[:, 0:C], heads(net.bias))
                        last.then_inc(v_ready, 1)
                    for c in range(6):
                        for h in range(2):
                            if c < 4:
                                if c == 0:
                                    pe.wait_ge(k_spread, n1(h))
                                    pe.wait_ge(v_taken, n1(h))
                                else:
                                    pe.wait_ge(biased, m1(h, c - 1))
                                for t in range(2):
                                    for w in range(2):
                                        tok = slice((2 * c + t) * P + C * w, (2 * c + t) * P + C * w + C)
                                        out = bank(h, c % 2)[C * w:C * w + C, 256 * t:256 * t + 256]
                                        nc.tensor.matmul(out, qx[h][:, tok], kxh[h][:, :, tok], start=True, stop=False)
                                        last = nc.tensor.matmul(out, qx[h][:, tok], kxl[h][:, :, tok],
                                                                start=False, stop=True)
                                last.then_inc(scored, 1)
                            if 1 <= c < 5:
                                pe.wait_ge(exped, m1(h, c - 1))
                                if c >= 2:
                                    pe.wait_ge(pl_taken, m1(h, c - 2))
                                for j in range(4):
                                    last = nc.tensor.transpose(
                                        bank(h, 2)[:, P * j:P * j + P],
                                        att[h][:, (c - 1) % 2, j // 2, 2 * (j % 2):2 * (j % 2) + 2, :].rearrange(
                                            "p a k -> p (a k)"), net.ident[:])
                                last.then_inc(p_turned, 1)
                            if c >= 2:
                                pe.wait_ge(pl_taken, m1(h, c - 2))
                                for j in range(4):
                                    g, hq = 2 * (c - 2) + j // 2, j % 2
                                    for w in range(2):
                                        out = bank(h, 3)[C * w:C * w + C, C * g + 32 * hq:C * g + 32 * hq + 32]
                                        high = pth[h][:, c % 2, j, C * w:C * w + C]
                                        low = ptl[h][:, c % 2, j, C * w:C * w + C]
                                        v_high = vh[h][:, 2 * g + w, hq].rearrange("p a d -> p (a d)")
                                        v_low = vl[h][:, 2 * g + w, hq].rearrange("p a d -> p (a d)")
                                        nc.tensor.matmul(out, high, v_high, start=True, stop=False)
                                        nc.tensor.matmul(out, high, v_low, start=False, stop=False)
                                        last = nc.tensor.matmul(out, low, v_high, start=False, stop=True)
                                last.then_inc(weighed, 1)
                    for h in range(2):
                        turn_from_windows(nc, co, n1(h), wk[h], bank16(h, 0), net.perm16[:, 1])
                    for h in range(2):
                        pe.wait_ge(co["xT"], n1(h))
                        for g in range(NT):
                            last = natural(nc, net, bank(h, 1)[:, C * g:C * g + C], wk[h]["xT"], g, "proj")
                        last.then_inc(projected, 1)
                    for h in range(2):
                        turn(nc, ln2, n1(h), wk[h], bank16(h, 0), net.ident16[:])
                    for h in range(2):
                        pe.wait_ge(ln2["xT"], n1(h))
                        for a in range(2):
                            c = slice(COLS["fc1"].start + P * a, COLS["fc1"].start + P * a + P)
                            for half in range(2):
                                last = upright(nc, net, bank(h, 2 - 2 * a + half), wk[h]["xT"], c, 512 * half,
                                               512 * half + 512)
                            last.then_inc(hid_ready, 1)
                    for h in range(2):
                        pe.wait_ge(gl_cut, 4 * i + 2 * h + 2)
                        for g in range(NT):
                            out = bank(h, 2)[:, C * g:C * g + C]
                            tok = slice(P * g, P * g + P)
                            nc.tensor.matmul(out, net.ones16[:, 0:P], net.bias[:, NWC:NWC + C], start=True, stop=False)
                            for a in range(2):
                                nc.tensor.matmul(out, glh[h][:, a, tok], net.fc2h[:, a], start=False, stop=False)
                                nc.tensor.matmul(out, glh[h][:, a, tok], net.fc2l[:, a], start=False, stop=False)
                                last = nc.tensor.matmul(out, gll[h][:, a, tok], net.fc2h[:, a], start=False,
                                                        stop=(a == 1))
                        last.then_inc(ffn_out, 1)
                    for h in range(2):
                        turn(nc, cx, n1(h), wk[h], bank16(h, 0), net.ident16[:])
                    for h in range(2):
                        pe.wait_ge(cx["xT"], n1(h))
                        for g in range(NT):
                            last = natural(nc, net, bank(h, 1)[:, C * g:C * g + C], wk[h]["xT"], g, "right")
                        last.then_inc(r_ready, 1)
                        for g in range(NT):
                            natural(nc, net, bank(h, 2)[:, C * g:C * g + C], wk[h]["xT"], g, "left")
                            last = natural(nc, net, bank(h, 3)[:, C * g:C * g + C], wk[h]["xT"], g, "gatel")
                        last.then_inc(lg_ready, 1)
                    for h in range(2):
                        pe.wait_ge(rl_taken, n1(h))
                        nc.tensor.matmul(bank(h, 0), net.same16[:], rh[h][:].rearrange("p g c -> p (g c)"),
                                         start=True, stop=False)
                        last = nc.tensor.matmul(bank(h, 0), net.same16[:], rl[h][:].rearrange("p g c -> p (g c)"),
                                                start=False, stop=True)
                        last.then_inc(rowsummed, 1)
                    for h in range(2):
                        turn(nc, cu, n1(h), wk[h], bank16(h, 1), net.ident16[:])
                    for h in range(2):
                        pe.wait_ge(cu["xT"], n1(h))
                        for g in range(NT):
                            last = natural(nc, net, bank(h, 2)[:, C * g:C * g + C], wk[h]["xT"], g, "out")
                        last.then_inc(outed, 1)


def pairs_of_tiles(t, image):
    return (t[:].rearrange("p (i h) g c -> p i (h g) c", h=2),
            image.rearrange("(i h) (g r) c k -> (r c) i (h g) k", h=2, g=NT))


def finish_store(net, out):
    nc, sem = net.nc, net.sem
    tp, ov = pairs_of_tiles(net.t, out)
    x_stored = sem("x_stored")
    with nc.Block() as block:
        @block.sync
        def _(sp):
            with sp.Fori(0, PAIRS) as i:
                sp.dma_start(ov[:, i], tp[:, i]).then_inc(x_stored, 16)
            sp.wait_ge(x_stored, 16 * PAIRS)


def piece_count(n, per, k):
    return per * n + k + 1


def stage_attend(net, d):
    nc, sem = net.nc, net.sem
    RING = 4
    with ExitStack() as ctx:
        def sb(name, shape, dt):
            return ctx.enter_context(nc.sbuf_tensor("a2_" + name, shape, dt))

        wk = [work_buffers(sb, f"w{h}") for h in range(2)]
        xTb = [sb(f"xTb{h}", [P, TOK], F16) for h in range(2)]
        ex = sb("ex", [P, RING, TOK], F32)
        exh = sb("exh", [P, RING, TOK], F16)
        exl = sb("exl", [P, RING, TOK], F16)
        rs = [sb(f"rs{h}", [P, NT], F32) for h in range(2)]
        rinv = [sb(f"rinv{h}", [P, NT], F32) for h in range(2)]
        o = [sb(f"o{h}", [P, NT, C], F32) for h in range(2)]
        shift = sb("shift", [P, 1], F32)
        ps_s = ctx.enter_context(nc.psum_tensor("a2_ps_s", [P, 2, TOK], F32))
        ps_o = ctx.enter_context(nc.psum_tensor("a2_ps_o", [P, 2, 512], F32))
        ps_t = ctx.enter_context(nc.psum_tensor("a2_ps_t", [P, 2, TOK], F16))
        ln = net.norms[0]
        doubled, turned_b, xTb_done, shift_set = (sem("a2_" + s) for s in ("doubled", "turned_b", "xTb", "shift_set"))
        scored, exped, high, low_v, low_g, weighed = (sem("a2_" + s) for s in (
            "scored", "exped", "high", "low_v", "low_g", "weighed"))
        inverted, normed, added = (sem("a2_" + s) for s in ("inverted", "normed", "added"))
        tv = net.t[:].rearrange("p (i h) g c -> p i h g c", h=2)
        base = B

        def images(engine, attend, prep):
            prep(0, 0, range(8))
            with engine.Fori(0, PAIRS - 1) as i:
                attend(i, 0, (i, 1))
                attend(i, 1, (i + 1, 0))
            attend(PAIRS - 1, 0, (PAIRS - 1, 1))
            attend(PAIRS - 1, 1, None)

        with nc.Block() as block:
            @block.vector
            def _(dve):
                nc.vector.memset(shift[:], -SHIFT2).then_inc(shift_set, 1)

                def prep(i, h, pieces):
                    n, w, src = base + 2 * i + h, wk[h], tv[:, i, h]
                    for k in pieces:
                        if k == 0:
                            norm_sum(nc, ln, n + 1, src, w)
                            norm_centre(nc, ln, n + 1, src, w)
                        if k == 2:
                            norm_sumsq(nc, ln, n + 1, w)
                        if k == 3:
                            norm_apply(nc, ln, n + 1, w)
                        if k == 5:
                            cut_low(nc, ln, n + 1, w, w["xn"])
                            nc.vector.tensor_copy(w["hl"][:, :, 2 * C:3 * C],
                                                  w["hl"][:, :, 0:C]).then_inc(doubled, 1)
                        if k == 6:
                            take_turned(nc, ln, n + 1, w, ps_t[:, 0])
                            dve.wait_ge(turned_b, 2 * i + h + 1)
                            nc.vector.tensor_copy(xTb[h][:], ps_t[:, 1]).then_inc(xTb_done, 1)

                def attend(i, h, ahead):
                    n = 2 * i + h
                    for m in range(NT):
                        dve.wait_ge(exped, piece_count(n, NT, m))
                        if m >= RING:
                            dve.wait_ge(weighed, piece_count(n, NT, m - RING))
                        r = m % RING
                        nc.vector.tensor_copy(exh[:, r], ex[:, r]).then_inc(high, 1)
                        if m % 2 == 0:
                            dve.wait_ge(high, piece_count(n, NT, m))
                            nc.vector.tensor_tensor(exl[:, r], ex[:, r], exh[:, r], ALU.subtract).then_inc(low_v, 1)
                        if ahead:
                            prep(*ahead, (m,))
                    nc.vector.reciprocal(rinv[h][:], rs[h][:]).then_inc(inverted, 1)
                    dve.wait_ge(inverted, n + 1)
                    dve.wait_ge(weighed, piece_count(n, NT, NT - 1))
                    nc.vector.tensor_tensor(o[h][:], tiles(ps_o[:, h]), spread(rinv[h][:], C),
                                            ALU.mult).then_inc(normed, 1)
                    dve.wait_ge(normed, n + 1)
                    nc.vector.tensor_tensor(tv[:, i, h], tv[:, i, h], o[h][:], ALU.add).then_inc(added, 1)

                images(dve, attend, prep)
                dve.wait_ge(added, B)

            @block.scalar
            def _(act):
                act.wait_ge(shift_set, 1)

                def prep(i, h, pieces):
                    n, w = base + 2 * i + h, wk[h]
                    for k in pieces:
                        if k == 1:
                            norm_square(nc, ln, n + 1, w)
                        if k == 4:
                            cut_high(nc, ln, n + 1, w, w["xn"])

                def attend(i, h, ahead):
                    n = 2 * i + h
                    for m in range(NT):
                        r = m % RING
                        act.wait_ge(scored, piece_count(n, NT, m))
                        if m >= RING:
                            if m % 2 == 0:
                                act.wait_ge(low_v, piece_count(n, NT // 2, (m - RING) // 2))
                            else:
                                act.wait_ge(low_g, piece_count(n, NT // 2, (m - RING) // 2))
                        nc.scalar.activation(ex[:, r], ps_s[:, m % 2], ACT.Exp, bias=shift[:],
                                             accum_out=rs[h][:, m:m + 1]).then_inc(exped, 1)
                        if ahead:
                            prep(*ahead, (m,))

                images(act, attend, prep)

            @block.gpsimd
            def _(pool):
                def prep(i, h, pieces):
                    for k in pieces:
                        if k == 2:
                            norm_rstd(nc, ln, base + 2 * i + h + 1, wk[h], net.nhalf[:], net.eps[:])

                def attend(i, h, ahead):
                    n = 2 * i + h
                    for m in range(NT):
                        if m % 2:
                            pool.wait_ge(high, piece_count(n, NT, m))
                            nc.gpsimd.tensor_tensor(exl[:, m % RING], ex[:, m % RING], exh[:, m % RING],
                                                    ALU.subtract).then_inc(low_g, 1)
                        if ahead:
                            prep(*ahead, (m,))

                images(pool, attend, prep)

            @block.tensor
            def _(pe):
                def prep(i, h, pieces):
                    n, w = base + 2 * i + h, wk[h]
                    for k in pieces:
                        if k == 6:
                            turn(nc, ln, n + 1, w, ps_t[:, 0], net.ident16[:])
                            pe.wait_ge(doubled, 2 * i + h + 1)
                            for g in range(NT):
                                last = nc.tensor.transpose(ps_t[:, 1, P * g:P * g + P], w["hl"][:, g, C:3 * C],
                                                           net.ident16[:])
                            last.then_inc(turned_b, 1)

                def attend(i, h, ahead):
                    n = 2 * i + h
                    for m in range(NT + 2):
                        if m < NT:
                            if m == 0:
                                pe.wait_ge(xTb_done, n + 1)
                                pe.wait_ge(ln["xT"], base + n + 1)
                            if m >= 2:
                                pe.wait_ge(exped, piece_count(n, NT, m - 2))
                            tok = slice(P * m, P * m + P)
                            for half in range(2):
                                out = ps_s[:, m % 2, 512 * half:512 * half + 512]
                                z = wk[h]["xT"][:, 512 * half:512 * half + 512]
                                nc.tensor.matmul(out, wk[h]["xT"][:, tok], z, start=True, stop=False)
                                last = nc.tensor.matmul(out, xTb[h][:, tok], z, start=False, stop=True)
                            last.then_inc(scored, 1)
                            if ahead:
                                prep(*ahead, (m,))
                        if m >= 2:
                            k = m - 2
                            if k % 2 == 0:
                                pe.wait_ge(low_v, piece_count(n, NT // 2, k // 2))
                            else:
                                pe.wait_ge(low_g, piece_count(n, NT // 2, k // 2))
                            z_high, z_low = wk[h]["hl"][:, k, 0:C], wk[h]["hl"][:, k, C:2 * C]
                            for g in range(NT):
                                out = ps_o[:, h, C * g:C * g + C]
                                e_high = exh[:, k % RING, P * g:P * g + P]
                                e_low = exl[:, k % RING, P * g:P * g + P]
                                nc.tensor.matmul(out, e_high, z_high, start=(k == 0 and g == 0), stop=False,
                                                 skip_group_check=True)
                                nc.tensor.matmul(out, e_high, z_low, start=False, stop=False, skip_group_check=True)
                                last = nc.tensor.matmul(out, e_low, z_high, start=False, stop=(k == NT - 1),
                                                        skip_group_check=True)
                            last.then_inc(weighed, 1)

                images(pe, attend, prep)


def stage_pool(net, d):
    nc, sem = net.nc, net.sem
    with ExitStack() as ctx:
        def sb(name, shape, dt):
            return ctx.enter_context(nc.sbuf_tensor("f2_" + name, shape, dt))

        kept = sb("kept", [P, NG, TOK], F32)
        pooled = sb("pooled", [C + 1, E2, B], F32)
        experts = sb("experts", [P, NG, C], F32)
        pooled_ready, zero_set = sem("f2_pooled_ready"), sem("f2_zero_set")
        base = 2 * B
        with ExitStack() as inner:
            def sb(name, shape, dt):
                return inner.enter_context(nc.sbuf_tensor("f2_" + name, shape, dt))

            wk = [work_buffers(sb, f"w{j}") for j in range(GRP)]
            prob = sb("prob", [P, TOK], F32)
            rest = sb("rest", [P, TOK], F32)
            mask = sb("mask", [P, TOK], F32)
            mask_t = sb("mask_t", [P, NT, P], F32)
            small = sb("small", [P, 4], F32)
            top = sb("top", [P, 8], F32)
            idle = sb("idle", [P, 1], F32)
            ps_t = inner.enter_context(nc.psum_tensor("f2_ps_t", [P, 2, TOK], F16))
            ps_l = inner.enter_context(nc.psum_tensor("f2_ps_l", [P, TOK], F32))
            ps_m = inner.enter_context(nc.psum_tensor("f2_ps_m", [P, TOK], F32))
            ps_p = inner.enter_context(nc.psum_tensor("f2_ps_p", [C, P], F32))
            ln = net.norms[0]
            logits, maxed, negated, exped, inverted, probs = (sem("f2_" + s) for s in (
                "logits", "maxed", "negated", "exped", "inverted", "probs"))
            topped, replaced, masked, mask_kept, mask_turned, mask_t_taken = (sem("f2_" + s) for s in (
                "topped", "replaced", "masked", "mask_kept", "mask_turned", "mask_t_taken"))
            pool_ready = sem("f2_pool_ready")
            tg = net.t[:].rearrange("p (i j) g c -> p i j g c", j=GRP)
            pg = pooled[:].rearrange("p e (i j) -> p i j e", j=GRP)

            with nc.Block() as block:
                @block.vector
                def _(dve):
                    nc.vector.memset(pooled[C:C + 1], 1.0)
                    with dve.Fori(0, NG) as i:
                        def n1(j):
                            return base + GRP * i + j + 1

                        for j in range(GRP):
                            norm_sum(nc, ln, n1(j), tg[:, i, j], wk[j])
                        for j in range(GRP):
                            norm_centre(nc, ln, n1(j), tg[:, i, j], wk[j])
                        for j in range(GRP):
                            norm_sumsq(nc, ln, n1(j), wk[j])
                        for j in range(GRP):
                            norm_apply(nc, ln, n1(j), wk[j])
                        for j in range(GRP):
                            cut_low(nc, ln, n1(j), wk[j], wk[j]["xn"])
                        for j in range(GRP):
                            take_turned(nc, ln, n1(j), wk[j], ps_t[:, j % 2])
                        dve.wait_ge(logits, i + 1)
                        nc.vector.tensor_reduce(small[:, 0:1], ps_l[:], AX.X, ALU.max).then_inc(maxed, 1)
                        dve.wait_ge(maxed, i + 1)
                        nc.vector.tensor_scalar(small[:, 1:2], small[:, 0:1], -IWS, None, ALU.mult).then_inc(negated, 1)
                        dve.wait_ge(exped, i + 1)
                        nc.vector.reciprocal(small[:, 3:4], small[:, 2:3]).then_inc(inverted, 1)
                        dve.wait_ge(inverted, i + 1)
                        nc.vector.tensor_scalar(prob[:], rest[:], small[:, 3:4], None, ALU.mult).then_inc(probs, 1)
                        dve.wait_ge(probs, i + 1)
                        nc.vector.memset(idle[:], 0.0)
                        nc.vector.max(top[:], prob[:]).then_inc(topped, 1)
                        dve.wait_ge(topped, i + 1)
                        nc.vector.memset(idle[:], 0.0)
                        nc.vector.match_replace(rest[:], top[:], prob[:], 0.0).then_inc(replaced, 1)
                        dve.wait_ge(replaced, i + 1)
                        nc.vector.tensor_tensor(mask[:], prob[:], rest[:], ALU.subtract).then_inc(masked, 1)
                        dve.wait_ge(mask_turned, i + 1)
                        nc.vector.tensor_copy(mask_t[:].rearrange("p a b -> p (a b)"), ps_m[:]).then_inc(mask_t_taken, 1)
                        dve.wait_ge(pool_ready, i + 1)
                        nc.vector.tensor_copy(pg[0:C, i], ps_p[:].rearrange("p (j e) -> p j e", j=GRP)
                                              ).then_inc(pooled_ready, 1)
                        dve.wait_ge(pooled_ready, i + 1)
                        dve.wait_ge(mask_kept, i + 1)

                @block.scalar
                def _(act):
                    with act.Fori(0, NG) as i:
                        def n1(j):
                            return base + GRP * i + j + 1

                        for j in range(GRP):
                            norm_square(nc, ln, n1(j), wk[j])
                        for j in range(GRP):
                            cut_high(nc, ln, n1(j), wk[j], wk[j]["xn"])
                        act.wait_ge(negated, i + 1)
                        nc.scalar.activation(rest[:], ps_l[:], ACT.Exp, bias=small[:, 1:2], scale=IWS,
                                             accum_out=small[:, 2:3]).then_inc(exped, 1)
                        act.wait_ge(masked, i + 1)
                        nc.scalar.activation(kept[:, i], mask[:], ACT.Copy).then_inc(mask_kept, 1)

                @block.gpsimd
                def _(pool):
                    with pool.Fori(0, NG) as i:
                        for j in range(GRP):
                            norm_rstd(nc, ln, base + GRP * i + j + 1, wk[j], net.nhalf[:], net.eps[:])

                @block.tensor
                def _(pe):
                    with pe.Fori(0, NG) as i:
                        def n1(j):
                            return base + GRP * i + j + 1

                        for j in range(GRP):
                            if j >= 2:
                                pe.wait_ge(ln["xT"], n1(j - 2))
                            turn(nc, ln, n1(j), wk[j], ps_t[:, j % 2], net.ident16[:])
                        c = COLS["gate2"]
                        for j in range(GRP):
                            pe.wait_ge(ln["xT"], n1(j))
                            for half in range(2):
                                tok = slice(512 * half, 512 * half + 512)
                                out, x = ps_l[E2 * j:E2 * j + E2, tok], wk[j]["xT"][:, tok]
                                nc.tensor.matmul(out, net.wa[:, c], x, start=True, stop=False, tile_position=(0, E2 * j))
                                nc.tensor.matmul(out, net.wb[:, c], x, start=False, stop=False,
                                                 tile_position=(0, E2 * j))
                                last = nc.tensor.matmul(out, net.bias[:, c], net.ones16[:, 0:512], start=False,
                                                        stop=True, tile_position=(0, E2 * j))
                        last.then_inc(logits, 1)
                        pe.wait_ge(masked, i + 1)
                        for g in range(NT):
                            last = nc.tensor.transpose(ps_m[:, P * g:P * g + P], mask[:, P * g:P * g + P], net.ident[:])
                        last.then_inc(mask_turned, 1)
                        pe.wait_ge(mask_t_taken, i + 1)
                        for j in range(GRP):
                            for g in range(NT):
                                last = nc.tensor.matmul(ps_p[:, E2 * j:E2 * j + E2], wk[j]["xn"][:, g],
                                                        mask_t[:, g, E2 * j:E2 * j + E2], start=(g == 0),
                                                        stop=(g == NT - 1))
                        last.then_inc(pool_ready, 1)

        scratch = nc.dram_tensor("expert_outputs", (B, E2, C), F32, kind="Internal").ap()
        with ExitStack() as inner:
            def sb(name, shape, dt):
                return inner.enter_context(nc.sbuf_tensor("f2_" + name, shape, dt))

            w1 = sb("w1", [C + 1, E2, HID], F32)
            w2 = sb("w2", [P, 2, E2, C], F32)
            w2b = sb("w2b", [P, C], F32)
            hid = sb("hid", [P, 2, E2, B], F32)
            outs = sb("outs", [B, E2, C], F32)
            ps_h = inner.enter_context(nc.psum_tensor("f2_ps_h", [P, 2, E2, B], F32))
            ps_y = inner.enter_context(nc.psum_tensor("f2_ps_y", [B, E2, C], F32))
            w_loaded, hid_ready, gelued, out_ready, out_taken, bounced, back = (sem("f2_" + s) for s in (
                "w_loaded", "hid_ready", "gelued", "out_ready", "out_taken", "bounced", "back"))
            biased = sem("f2_biased")
            with nc.Block() as block:
                @block.sync
                def _(sp):
                    sp.dma_start(w1[:], d["L2_ffn_weight1"].rearrange("e d h -> d e h")).then_inc(w_loaded, 16)
                    for a in range(2):
                        sp.dma_start(w2[:, a], d["L2_ffn_weight2"][:, P * a:P * a + P, :].rearrange("e p o -> p e o")
                                     ).then_inc(w_loaded, 16)
                    for j in range(GRP):
                        sp.dma_start(w2b[E2 * j:E2 * j + E2, :], d["L2_ffn_weight2"][:, HID, :]).then_inc(w_loaded, 16)
                    sp.wait_ge(out_taken, 1)
                    sp.dma_start(scratch, outs[:]).then_inc(bounced, 16)
                    sp.wait_ge(bounced, 16)
                    sp.dma_start(experts[:], scratch.rearrange("(g j) e o -> (j e) g o", j=GRP)).then_inc(back, 16)

                @block.tensor
                def _(pe):
                    pe.wait_ge(w_loaded, 16 * 7)
                    for a in range(2):
                        for e in range(E2):
                            last = nc.tensor.matmul(ps_h[:, a, e], w1[:, e, P * a:P * a + P], pooled[:, e], start=True,
                                                    stop=True)
                        last.then_inc(hid_ready, 1)
                    pe.wait_ge(gelued, 2)
                    for e in range(E2):
                        nc.tensor.matmul(ps_y[:, e], hid[:, 0, e], w2[:, 0, e], start=True, stop=False)
                        last = nc.tensor.matmul(ps_y[:, e], hid[:, 1, e], w2[:, 1, e], start=False, stop=True)
                    last.then_inc(out_ready, 1)

                @block.scalar
                def _(act):
                    for a in range(2):
                        act.wait_ge(hid_ready, 2)
                        nc.scalar.activation(hid[:, a], ps_h[:, a], ACT.Gelu).then_inc(gelued, 1)

                @block.vector
                def _(dve):
                    dve.wait_ge(out_ready, 1)
                    nc.vector.tensor_copy(outs[:], ps_y[:]).then_inc(out_taken, 1)
                    dve.wait_ge(back, 16)
                    dve.wait_ge(w_loaded, 16 * 7)
                    nc.vector.tensor_tensor(experts[:], experts[:], over(w2b[:], NG), ALU.add).then_inc(biased, 1)
                    dve.wait_ge(biased, 1)

        with ExitStack() as inner:
            def sb(name, shape, dt):
                return inner.enter_context(nc.sbuf_tensor("f2_" + name, shape, dt))

            mask = [sb(f"maskb{q}", [P, TOK], F32) for q in range(2)]
            diag = [sb(f"diag{q}", [P, GRP, C], F32) for q in range(2)]
            ps_s = [inner.enter_context(nc.psum_tensor(f"f2_ps_s{q}", [P, NT, GRP, C], F32)) for q in range(2)]
            diag_zero, ready, spread_out, added = (sem("f2_" + s) for s in (
                "diag_zero", "ready", "spread_out", "added"))
            kq = kept[:].rearrange("p (i q) s -> p i q s", q=2)
            eq = experts[:].rearrange("p (i q) c -> p i q c", q=2)
            tq = net.t[:].rearrange("p (i q j) g c -> p i q j g c", q=2, j=GRP)
            with nc.Block() as block:
                @block.vector
                def _(dve):
                    for q in range(2):
                        nc.vector.memset(diag[q][:], 0.0).then_inc(diag_zero, 1)
                    dve.wait_ge(diag_zero, 2)

                    def prepare(i, q):
                        nc.vector.tensor_copy(mask[q][:], kq[:, i, q])
                        for j in range(GRP):
                            rows = slice(E2 * j, E2 * j + E2)
                            last = nc.vector.tensor_copy(diag[q][rows, j], eq[rows, i, q])
                        last.then_inc(ready, 1)

                    with dve.Fori(0, max(NG // 2, 1)) as i:
                        for q in range(min(2, NG)):
                            prepare(i, q)
                        for q in range(min(2, NG)):
                            dve.wait_ge(spread_out, 2 * i + q + 1)
                            for j in range(GRP):
                                last = nc.vector.tensor_tensor(tq[:, i, q, j], tq[:, i, q, j], ps_s[q][:, :, j, :],
                                                               ALU.add)
                            last.then_inc(added, 1)
                    dve.wait_ge(added, NG)

                @block.tensor
                def _(pe):
                    with pe.Fori(0, max(NG // 2, 1)) as i:
                        for q in range(min(2, NG)):
                            pe.wait_ge(ready, 2 * i + q + 1)
                            for g in range(NT):
                                last = nc.tensor.matmul(ps_s[q][:, g].rearrange("p j c -> p (j c)"),
                                                        mask[q][:, P * g:P * g + P],
                                                        diag[q][:].rearrange("p j c -> p (j c)"), start=True, stop=True)
                            last.then_inc(spread_out, 1)


def tile_at(i, h, m):
    while m < 0:
        i, h, m = (i, 0, m + NT) if h else (i - 1, 1, m + NT)
    while m >= NT:
        i, h, m = (i + 1, 0, m - NT) if h else (i, 1, m - NT)
    if isinstance(i, int) and not 0 <= i < PAIRS:
        return None
    return i, h, m


def stream(engine, step, near, far, lag, near_first=False):
    def image(i, h, next_one, next_but_one):
        for m in range(NT):
            if next_one and near_first:
                near(*next_one, m)
            step(i, h, m)
            if next_one and not near_first:
                near(*next_one, m)
            if next_but_one:
                far(*next_but_one, m)

    for m in range(NT):
        far(0, 0, m)
    for m in range(NT):
        near(0, 0, m)
        far(0, 1, m)
    step(0, 0, -1)
    image(0, 0, (0, 1), (1, 0))
    with engine.Fori(0, PAIRS - 2) as i:
        image(i, 1, (i + 1, 0), (i + 1, 1))
        image(i + 1, 0, (i + 1, 1), (i + 2, 0))
    image(PAIRS - 2, 1, (PAIRS - 1, 0), (PAIRS - 1, 1))
    image(PAIRS - 1, 0, (PAIRS - 1, 1), None)
    image(PAIRS - 1, 1, None, None)
    for m in range(NT, NT + lag):
        step(PAIRS - 1, 1, m)


def stage_attend_qkv(net, d):
    nc, sem = net.nc, net.sem
    RING, LAG = 4, 3
    with ExitStack() as ctx:
        def sb(name, shape, dt):
            return ctx.enter_context(nc.sbuf_tensor("a3_" + name, shape, dt))

        wk = [work_buffers(sb, f"w{h}") for h in range(2)]
        qx, kh, kl = ([sb(f"{s}{h}", [P, TOK], F16) for h in range(2)] for s in ("qx", "kh", "kl"))
        vh, vl = ([sb(f"{s}{h}", [P, NT, C + 1], F16) for h in range(2)] for s in ("vh", "vl"))
        pr = sb("pr", [P, RING, TOK], F32)
        prh, prl = (sb(s, [P, RING, TOK], F16) for s in ("prh", "prl"))
        ones = sb("ones", [P, P], F16)
        nmax = sb("nmax", [P, RING], F32)
        diag = sb("diag", [P, RING, P], F16)
        rinv = sb("rinv", [P, RING], F32)
        ps_a = ctx.enter_context(nc.psum_tensor("a3_ps_a", [P, TOK], F32))
        ps_s = ctx.enter_context(nc.psum_tensor("a3_ps_s", [P, 2, TOK], F32))
        ps_o = ctx.enter_context(nc.psum_tensor("a3_ps_o", [P, 512], F32))
        ps_w = ctx.enter_context(nc.psum_tensor("a3_ps_w", [P, 512], F32))
        ln = net.norms[0]
        base = 3 * B
        proj, proj_high, proj_low, set_up = (sem("a3_" + s) for s in ("proj", "proj_high", "proj_low", "set_up"))
        ranged, maxed, diagonal, scored, exped, high, low, weighed, inverted, added = (sem("a3_" + s) for s in (
            "ranged", "maxed", "diagonal", "scored", "exped", "high", "low", "weighed", "inverted", "added"))
        tv = net.t[:].rearrange("p (i h) g c -> p i h g c", h=2)
        PROJ = 5

        def half_of(k):
            return slice(512 * (k % 2), 512 * (k % 2) + 512)

        def count(at, lag=0):
            i, h, m = at
            return NT * (2 * i + h) + m - lag + 1

        def past(at, lag):
            return tile_at(at[0], at[1], at[2] - lag) is not None

        with nc.Block() as block:
            @block.vector
            def _(dve):
                def near(i, h, m):
                    n, k = 2 * i + h, m - 1
                    if not 0 <= k < PROJ:
                        return
                    dve.wait_ge(proj_high, piece_count(n, PROJ, k))
                    if k < 2:
                        part = qx[h][C:P, half_of(k)]
                        ins = nc.vector.scalar_tensor_tensor(part, ps_w[C:P, :], IWS / TEMP, part, ALU.mult,
                                                             ALU.subtract)
                    elif k < 4:
                        ins = nc.vector.scalar_tensor_tensor(kl[h][:, half_of(k)], ps_w[:], IWS,
                                                             kh[h][:, half_of(k)], ALU.mult, ALU.subtract)
                    else:
                        ins = nc.vector.scalar_tensor_tensor(vl[h][:, :, 0:C], tiles(ps_w[:]), IWS,
                                                             vh[h][:, :, 0:C], ALU.mult, ALU.subtract)
                    ins.then_inc(proj_low, 1)

                def far(i, h, m):
                    n1, w = base + 2 * i + h + 1, wk[h]
                    if m == 0:
                        norm_sum(nc, ln, n1, tv[:, i, h], w)
                    if m == 1:
                        norm_centre(nc, ln, n1, tv[:, i, h], w)
                    if m == 2:
                        norm_sumsq(nc, ln, n1, w)
                    if m == 4:
                        norm_apply(nc, ln, n1, w)
                    if m == 5:
                        cut_low(nc, ln, n1, w, w["xn"])
                    if m == 7:
                        take_turned(nc, ln, n1, w, ps_w[:].bitcast(F16))

                def step(i, h, m):
                    at = tile_at(i, h, m + 1)
                    if at:
                        r = at[2] % RING
                        dve.wait_ge(ranged, count(at))
                        if past(at, RING):
                            dve.wait_ge(scored, count(at, RING))
                        nc.vector.tensor_reduce(nmax[:, r:r + 1], ps_a[:], AX.X, ALU.max, negate=True).then_inc(maxed, 1)
                        dve.wait_ge(maxed, count(at))
                        nc.vector.tensor_scalar(diag[:, r], net.ident16[:], nmax[:, r:r + 1], None,
                                                ALU.mult).then_inc(diagonal, 1)
                    at = tile_at(i, h, m - LAG)
                    if at:
                        ia, ha, g = at
                        dve.wait_ge(weighed, count(at))
                        nc.vector.reciprocal(rinv[:, g % RING:g % RING + 1], ps_o[:, C:C + 1]).then_inc(inverted, 1)
                        dve.wait_ge(inverted, count(at))
                        nc.vector.scalar_tensor_tensor(tv[:, ia, ha, g], ps_o[:, 0:C], rinv[:, g % RING:g % RING + 1],
                                                       tv[:, ia, ha, g], ALU.mult, ALU.add).then_inc(added, 1)

                for h in range(2):
                    nc.vector.memset(vh[h][:, :, C:C + 1], 1.0)
                    nc.vector.memset(vl[h][:, :, C:C + 1], 0.0)
                nc.vector.memset(ones[:], 1.0).then_inc(set_up, 1)
                stream(dve, step, near, far, LAG, near_first=True)
                dve.wait_ge(added, B * NT)

            @block.scalar
            def _(act):
                def near(i, h, k):
                    if k >= PROJ:
                        return
                    act.wait_ge(proj, piece_count(2 * i + h, PROJ, k))
                    if k < 2:
                        ins = nc.scalar.activation(qx[h][:, half_of(k)], ps_w[:], ACT.Copy, scale=IWS / TEMP)
                    elif k < 4:
                        ins = nc.scalar.activation(kh[h][:, half_of(k)], ps_w[:], ACT.Copy, scale=IWS)
                    else:
                        ins = nc.scalar.activation(vh[h][:, :, 0:C], tiles(ps_w[:]), ACT.Copy, scale=IWS)
                    ins.then_inc(proj_high, 1)

                def far(i, h, m):
                    n1, w = base + 2 * i + h + 1, wk[h]
                    if m == 1:
                        norm_square(nc, ln, n1, w)
                    if m == 4:
                        cut_high(nc, ln, n1, w, w["xn"])

                def step(i, h, m):
                    at = tile_at(i, h, m) if m >= 0 else None
                    if at:
                        r = at[2] % RING
                        act.wait_ge(scored, count(at))
                        if past(at, RING):
                            act.wait_ge(low, count(at, RING))
                        nc.scalar.activation(pr[:, r], ps_s[:, m % 2], ACT.Exp).then_inc(exped, 1)
                        act.wait_ge(exped, count(at))
                        if past(at, RING):
                            act.wait_ge(weighed, count(at, RING))
                        nc.scalar.activation(prh[:, r], pr[:, r], ACT.Copy).then_inc(high, 1)

                stream(act, step, near, far, 0)

            @block.gpsimd
            def _(pool):
                def near(i, h, m):
                    pass

                def far(i, h, m):
                    if m == 2:
                        norm_rstd(nc, ln, base + 2 * i + h + 1, wk[h], net.nhalf[:], net.eps[:])

                def step(i, h, m):
                    at = tile_at(i, h, m) if m >= 0 else None
                    if at:
                        r = at[2] % RING
                        pool.wait_ge(high, count(at))
                        nc.gpsimd.tensor_tensor(prl[:, r], pr[:, r], prh[:, r], ALU.subtract).then_inc(low, 1)

                stream(pool, step, near, far, 0)

            @block.tensor
            def _(pe):
                def near(i, h, k):
                    n, xT = 2 * i + h, wk[h]["xT"]
                    if k >= PROJ:
                        return
                    if k == 0:
                        pe.wait_ge(ln["xT"], base + n + 1)
                    else:
                        pe.wait_ge(proj_low, piece_count(n, PROJ, k - 1))
                    if k < 4:
                        tok = half_of(k)
                        last = upright(nc, net, ps_w[:], xT, COLS["q3" if k < 2 else "k3"], tok.start, tok.stop)
                    else:
                        for g in range(NT):
                            last = natural(nc, net, ps_w[:, C * g:C * g + C], xT, g, "v3")
                    last.then_inc(proj, 1)

                def far(i, h, m):
                    n = 2 * i + h
                    if m == 6:
                        if not isinstance(i, int) or n >= 1:
                            pe.wait_ge(proj_low, PROJ * n)
                        turn(nc, ln, base + n + 1, wk[h], ps_w[:].bitcast(F16), net.ident16[:])

                def step(i, h, m):
                    at = tile_at(i, h, m + 1)
                    if at:
                        ia, ha, g = at
                        if g == 0:
                            pe.wait_ge(proj_low, piece_count(2 * ia + ha, PROJ, PROJ - 1))
                        if past(at, 1):
                            pe.wait_ge(maxed, count(at, 1))
                        for half in range(2):
                            keys = slice(512 * half, 512 * half + 512)
                            last = nc.tensor.matmul(ps_a[:, keys], qx[ha][:, P * g:P * g + P], kh[ha][:, keys],
                                                    start=True, stop=True)
                        last.then_inc(ranged, 1)
                    at = tile_at(i, h, m) if m >= 0 else None
                    if at:
                        ia, ha, g = at
                        pe.wait_ge(diagonal, count(at))
                        if past(at, 2):
                            pe.wait_ge(exped, count(at, 2))
                        for half in range(2):
                            nc.tensor.matmul(ps_s[:, g % 2, 512 * half:512 * half + 512], ones[:],
                                             over(diag[:, g % RING], 4), start=True, stop=False, skip_group_check=True)
                            for j in range(4 * half, 4 * half + 4):
                                keys, out = slice(P * j, P * j + P), ps_s[:, g % 2, P * j:P * j + P]
                                query = qx[ha][:, P * g:P * g + P]
                                nc.tensor.matmul(out, kh[ha][:, keys], query, start=False, stop=False,
                                                 skip_group_check=True)
                                last = nc.tensor.matmul(out, kl[ha][:, keys], query, start=False, stop=(j % 4 == 3),
                                                        skip_group_check=True)
                        last.then_inc(scored, 1)
                    at = tile_at(i, h, m - LAG)
                    if at:
                        ia, ha, g = at
                        if past(at, 1):
                            pe.wait_ge(added, count(at, 1))
                        pe.wait_ge(low, count(at))
                        for j in range(NT):
                            high_j, low_j = (s[:, g % RING, P * j:P * j + P] for s in (prh, prl))
                            out = ps_o[:, 0:C + 1]
                            nc.tensor.matmul(out, high_j, vh[ha][:, j], start=(j == 0), stop=False)
                            nc.tensor.matmul(out, high_j, vl[ha][:, j], start=False, stop=False)
                            last = nc.tensor.matmul(out, low_j, vh[ha][:, j], start=False, stop=(j == NT - 1))
                        last.then_inc(weighed, 1)

                pe.wait_ge(set_up, 1)
                stream(pe, step, near, far, LAG)


def stage_route(net, d):
    nc, sem = net.nc, net.sem
    with ExitStack() as ctx:
        def sb(name, shape, dt):
            return ctx.enter_context(nc.sbuf_tensor("f3_" + name, shape, dt))

        wk = [work_buffers(sb, f"w{h}") for h in range(2)]
        acc = [sb(f"acc{h}", [P, NT, C], F32) for h in range(2)]
        order = sb("order", [P, E3], F32)
        sm = [{k: sb(f"{k}{h}", [P, NT, E3], F32) for k in ("lg", "eq", "first", "rest", "second", "gates")}
              for h in range(2)]
        st = [{k: sb(f"{k}{h}", [P, NT], F32) for k in ("m1", "k1", "m2", "k2", "dl", "e2", "den", "g1", "g2")}
              for h in range(2)]
        mixed = sb("mixed", [P, 3, E3, C], F32)
        ps_e = ctx.enter_context(nc.psum_tensor("f3_ps_e", [P, 4, 512], F32))
        ps_t = ctx.enter_context(nc.psum_tensor("f3_ps_t", [P, 2, TOK], F16))
        ps_r = ctx.enter_context(nc.psum_tensor("f3_ps_r", [P, 2, 512], F32))
        ln = net.norms[0]
        base = 4 * B
        routed, gate_step, diffed, e2_done = (sem("f3_" + s) for s in ("routed", "gate_step", "diffed", "e2_done"))
        expert_out, weighted, summed, added, stored = (sem("f3_" + s) for s in (
            "expert_out", "weighted", "summed", "added", "stored"))
        order_set = sem("f3_order_set")
        tv = net.t[:].rearrange("p (i h) g c -> p i h g c", h=2)
        tp, ov = pairs_of_tiles(net.t, net.out)
        STEPS = 18

        with nc.Block() as block:
            @block.sync
            def _(sp):
                with sp.Fori(0, PAIRS) as i:
                    sp.wait_ge(added, 2 * i + 2)
                    sp.dma_start(ov[:, i], tp[:, i]).then_inc(stored, 16)
                sp.wait_ge(stored, 16 * PAIRS)

            @block.vector
            def _(dve):
                for e in range(E3):
                    last = nc.vector.memset(order[:, e:e + 1], float(E3 - e))
                last.then_inc(order_set, 1)
                dve.wait_ge(order_set, 1)
                with dve.Fori(0, PAIRS) as i:
                    def n1(h):
                        return base + 2 * i + h + 1

                    for h in range(2):
                        norm_sum(nc, ln, n1(h), tv[:, i, h], wk[h])
                    for h in range(2):
                        norm_centre(nc, ln, n1(h), tv[:, i, h], wk[h])
                    for h in range(2):
                        norm_sumsq(nc, ln, n1(h), wk[h])
                    for h in range(2):
                        norm_apply(nc, ln, n1(h), wk[h])
                    for h in range(2):
                        cut_low(nc, ln, n1(h), wk[h], wk[h]["xn"])
                    for h in range(2):
                        take_turned(nc, ln, n1(h), wk[h], ps_t[:, h])
                    for h in range(2):
                        n, a, b = 2 * i + h, sm[h], st[h]
                        lg = a["lg"][:]
                        dve.wait_ge(routed, n + 1)
                        weights = over(order[:], NT)

                        def step(ins):
                            ins.then_inc(gate_step, 1)

                        step(nc.vector.tensor_copy(lg, ps_r[:, h, 0:NT * E3].rearrange("p (g e) -> p g e", e=E3)))
                        dve.wait_ge(gate_step, piece_count(n, STEPS, 0))
                        step(nc.vector.tensor_reduce(b["m1"][:], lg, AX.X, ALU.max))
                        dve.wait_ge(gate_step, piece_count(n, STEPS, 1))
                        step(nc.vector.tensor_tensor(a["eq"][:], lg, spread(b["m1"][:], E3), ALU.is_equal))
                        dve.wait_ge(gate_step, piece_count(n, STEPS, 2))
                        step(nc.vector.tensor_tensor(a["first"][:], a["eq"][:], weights, ALU.mult))
                        dve.wait_ge(gate_step, piece_count(n, STEPS, 3))
                        step(nc.vector.tensor_reduce(b["k1"][:], a["first"][:], AX.X, ALU.max))
                        dve.wait_ge(gate_step, piece_count(n, STEPS, 4))
                        step(nc.vector.tensor_tensor(a["first"][:], a["first"][:], spread(b["k1"][:], E3),
                                                     ALU.is_equal))
                        dve.wait_ge(gate_step, piece_count(n, STEPS, 5))
                        step(nc.vector.scalar_tensor_tensor(a["rest"][:], a["first"][:], -1e30, lg, ALU.mult, ALU.add))
                        dve.wait_ge(gate_step, piece_count(n, STEPS, 6))
                        step(nc.vector.tensor_reduce(b["m2"][:], a["rest"][:], AX.X, ALU.max))
                        dve.wait_ge(gate_step, piece_count(n, STEPS, 7))
                        nc.vector.tensor_tensor(b["dl"][:], b["m2"][:], b["m1"][:], ALU.subtract).then_inc(diffed, 1)
                        step(nc.vector.tensor_tensor(a["eq"][:], a["rest"][:], spread(b["m2"][:], E3), ALU.is_equal))
                        dve.wait_ge(gate_step, piece_count(n, STEPS, 8))
                        step(nc.vector.tensor_tensor(a["second"][:], a["eq"][:], weights, ALU.mult))
                        dve.wait_ge(gate_step, piece_count(n, STEPS, 9))
                        step(nc.vector.tensor_reduce(b["k2"][:], a["second"][:], AX.X, ALU.max))
                        dve.wait_ge(gate_step, piece_count(n, STEPS, 10))
                        step(nc.vector.tensor_tensor(a["second"][:], a["second"][:], spread(b["k2"][:], E3),
                                                     ALU.is_equal))
                        dve.wait_ge(e2_done, n + 1)
                        step(nc.vector.tensor_scalar(b["den"][:], b["e2"][:], WS, WS, ALU.mult, ALU.add))
                        dve.wait_ge(gate_step, piece_count(n, STEPS, 12))
                        step(nc.vector.reciprocal(b["g1"][:], b["den"][:]))
                        dve.wait_ge(gate_step, piece_count(n, STEPS, 13))
                        step(nc.vector.tensor_tensor(b["g2"][:], b["e2"][:], b["g1"][:], ALU.mult))
                        step(nc.vector.tensor_tensor(a["first"][:], a["first"][:], spread(b["g1"][:], E3), ALU.mult))
                        dve.wait_ge(gate_step, piece_count(n, STEPS, 15))
                        step(nc.vector.tensor_tensor(a["second"][:], a["second"][:], spread(b["g2"][:], E3), ALU.mult))
                        dve.wait_ge(gate_step, piece_count(n, STEPS, 16))
                        step(nc.vector.tensor_tensor(a["gates"][:], a["first"][:], a["second"][:], ALU.add))
                    for h in range(2):
                        n = 2 * i + h
                        dve.wait_ge(gate_step, piece_count(n, STEPS, 17))
                        for g in range(NT + 1):
                            if g < NT:
                                dve.wait_ge(expert_out, piece_count(n, NT, g))
                                if g >= 3:
                                    dve.wait_ge(summed, piece_count(n, NT, g - 3))
                                nc.vector.tensor_tensor(mixed[:, g % 3], ps_e[:, g % 4].rearrange("p (e c) -> p e c", e=E3),
                                                        spread(sm[h]["gates"][:, g], C), ALU.mult).then_inc(weighted, 1)
                            if g >= 1:
                                k = g - 1
                                dve.wait_ge(weighted, piece_count(n, NT, k))
                                nc.vector.tensor_reduce(acc[h][:, k], mixed[:, k % 3].rearrange("p e c -> p c e"), AX.X,
                                                        ALU.add).then_inc(summed, 1)
                        dve.wait_ge(summed, piece_count(n, NT, NT - 1))
                        nc.vector.tensor_tensor(tv[:, i, h], tv[:, i, h], acc[h][:], ALU.add).then_inc(added, 1)

            @block.scalar
            def _(act):
                with act.Fori(0, PAIRS) as i:
                    def n1(h):
                        return base + 2 * i + h + 1

                    for h in range(2):
                        norm_square(nc, ln, n1(h), wk[h])
                    for h in range(2):
                        cut_high(nc, ln, n1(h), wk[h], wk[h]["xn"])
                    for h in range(2):
                        act.wait_ge(diffed, 2 * i + h + 1)
                        nc.scalar.activation(st[h]["e2"][:], st[h]["dl"][:], ACT.Exp, scale=IWS).then_inc(e2_done, 1)

            @block.gpsimd
            def _(pool):
                with pool.Fori(0, PAIRS) as i:
                    for h in range(2):
                        norm_rstd(nc, ln, base + 2 * i + h + 1, wk[h], net.nhalf[:], net.eps[:])

            @block.tensor
            def _(pe):
                with pe.Fori(0, PAIRS) as i:
                    def n1(h):
                        return base + 2 * i + h + 1

                    for h in range(2):
                        turn(nc, ln, n1(h), wk[h], ps_t[:, h], net.ident16[:])
                    for h in range(2):
                        pe.wait_ge(ln["xT"], n1(h))
                        for g in range(NT):
                            last = natural(nc, net, ps_r[:, h, E3 * g:E3 * g + E3], wk[h]["xT"], g, "router")
                        last.then_inc(routed, 1)
                    for h in range(2):
                        n = 2 * i + h
                        for g in range(NT):
                            if g >= 4:
                                pe.wait_ge(weighted, piece_count(n, NT, g - 4))
                            elif h == 1:
                                pe.wait_ge(weighted, piece_count(2 * i, NT, NT + g - 4))
                            natural(nc, net, ps_e[:, g % 4], wk[h]["xT"], g, "exp3").then_inc(expert_out, 1)


STAGES = [stage_attend, stage_pool, stage_attend_qkv, stage_route]


INPUTS = ['x', 'L0_conv_ln1_g', 'L0_conv_ln1_b', 'L0_conv_qkv_w', 'L0_conv_qkv_b', 'L0_conv_proj_w', 'L0_conv_proj_b',
          'L0_conv_rpb', 'L0_conv_ln2_g', 'L0_conv_ln2_b', 'L0_conv_fc1_w', 'L0_conv_fc1_b', 'L0_conv_fc2_w',
          'L0_conv_fc2_b', 'L1_conv_W_left', 'L1_conv_b_left', 'L1_conv_W_right', 'L1_conv_b_right', 'L1_conv_W_gate',
          'L1_conv_b_gate', 'L1_conv_W_eq', 'L1_conv_b_eq', 'L1_conv_W_out', 'L1_conv_b_out', 'L1_conv_ln_scale',
          'L1_conv_ln_bias', 'L2_ffn_gate_w', 'L2_ffn_gate_b', 'L2_ffn_weight1', 'L2_ffn_weight2', 'L3_attn_Wq',
          'L3_attn_bq', 'L3_attn_Wk', 'L3_attn_bk', 'L3_attn_Wv', 'L3_attn_bv', 'L3_ffn_router_w', 'L3_ffn_router_b',
          'L3_ffn_expert_w', 'L3_ffn_expert_b']


def build(nc, d, k, out, stages=None):
    with ExitStack() as ctx:
        def sb(name, shape, dt):
            return ctx.enter_context(nc.sbuf_tensor(name, shape, dt))

        net = Net()
        net.nc, net.out = nc, out
        held = []

        def sem(name):
            held.append(nc.alloc_semaphore(name=name))
            return held[-1]

        net.sem = sem
        net.t = sb("tokens", [P, B, NT, C], F32)
        net.ident = sb("ident", [P, P], F32)
        net.ident16 = sb("ident16", [P, P], F16)
        net.perm16 = sb("perm16", [P, 2, P], F16)
        net.same16 = sb("same16", [P, P], F16)
        net.hmask = sb("hmask", [P, HEADS], F32)
        net.nhalf = sb("nhalf", [P, NT], F32)
        net.eps = sb("eps", [P, NT], F32)
        net.ones16 = sb("ones16", [2, 512], F16)
        net.wa = sb("wa", [P, NWC], F16)
        net.wb = sb("wb", [P, NWC], F16)
        net.bias = sb("bias", [2, NWC + C], F16)
        net.fc2h = sb("fc2h", [P, 2, C], F16)
        net.fc2l = sb("fc2l", [P, 2, C], F16)
        net.sbias = sb("sbias", [P, 2, 2, HEADS, C], F32)
        net.lns = sb("lns", [P, C], F32)
        net.lnb = sb("lnb", [P, C], F32)
        net.norms = [{part: net.sem(f"norm{j}_{part}") for part in NORM_PARTS} for j in range(3)]
        net.cuts = [{part: net.sem(f"cut{j}_{part}") for part in NORM_PARTS[6:]} for j in range(3)]
        net.t_ready = {part: net.sem(f"{part}_ready") for part in ("x1", "y", "t")}
        held.clear()

        def release():
            nc.clear_and_free_semaphores(held)
            nc.all_engine_barrier()
            held.clear()

        stage_setup(net, d, k)
        release()
        stage_blocks(net, d["x"])
        release()
        for st in STAGES:
            if stages is None or st.__name__ in stages:
                st(net, d)
                release()
        if stages is not None and "stage_route" not in stages:
            finish_store(net, out)



def constants():
    import numpy as np

    p, key = np.arange(P), np.arange(WIN * WIN)
    window, row, col = p // 64, p % 64 // WIN, p % WIN
    mask = np.zeros((P, 2, 2, 64), np.float32)
    for last_row in range(2):
        for jp in range(2):
            hidden = np.zeros((P, 64), bool)
            if last_row:
                hidden |= (row // 4)[:, None] != (key // 32)[None]
            if jp:
                hidden |= (window == 1)[:, None] & ((col // 4)[:, None] != (key % WIN // 4)[None])
            mask[:, last_row, jp] = np.where(hidden, np.float32(-1e9), np.float32(0))
    source = (np.arange(4)[None, :, None] * W
              + (WIN * np.arange(4)[:, None, None] + np.arange(WIN)[None, None, :] + WIN // 2) % W).reshape(-1)
    to_windows = np.zeros((P, P), np.float32)
    to_windows[source, p] = 1
    source = (64 * np.arange(2)[None, :, None] + WIN * np.arange(WIN)[:, None, None]
              + np.arange(WIN)[None, None, :]).reshape(-1)
    from_windows = np.zeros((P, P), np.float32)
    from_windows[source, p] = 1
    head = (np.arange(P) % 64 // HD)[:, None] == np.arange(HEADS)[None]
    return {"ident": np.eye(P, dtype=np.float32), "mask": mask, "hmask": head.astype(np.float32),
            "samerow": (p[:, None] // W == p[None] // W).astype(np.float32),
            "to_windows": to_windows, "from_windows": from_windows}


def kernel(**inputs):
    import numpy as _np
    import concourse.bacc as _bacc
    from concourse import mybir as _mybir
    from concourse.bass_utils import run_bass_kernel_spmd as _run

    nc = _bacc.Bacc("TRN2", target_bir_lowering=False, num_devices=1)
    arrays, d, k = {}, {}, {}
    for name in INPUTS:
        a = _np.ascontiguousarray(inputs[name])
        arrays[f"in_{name}_dram"] = a
        d[name] = nc.dram_tensor(f"in_{name}_dram", a.shape, _mybir.dt.from_np(a.dtype), kind="ExternalInput").ap()
    for name, a in constants().items():
        arrays[f"const_{name}_dram"] = a
        k[name] = nc.dram_tensor(f"const_{name}_dram", a.shape, _mybir.dt.from_np(a.dtype), kind="ExternalInput").ap()
    out = nc.dram_tensor("out_0_dram", (B, H, W, C), F32, kind="ExternalOutput").ap()
    build(nc, d, k, out)
    r = _run(nc, [arrays], core_ids=[0])
    return r.results[0]["out_0_dram"]
```

```python
from contextlib import ExitStack
from functools import partial

import concourse.bass as bass
from concourse import mybir

ALU = mybir.AluOpType
ACT = mybir.ActivationFunctionType
AX = mybir.AxisListType
F32 = mybir.dt.float32
F16 = mybir.dt.float16

P = 128
B, H, W, C = 32, 32, 32, 64
TOK = H * W
NT = TOK // P
WIN = 8
NW_IMG = (H // WIN) * (W // WIN)
HEADS, HD = 4, C // 4
E2, HID = 32, 256
E3 = 8
FF = 4 * C
GRP = 4
NG = B // GRP
PAIRS = B // 2
WS = 64.0
IWS = 1.0 / WS
TEMP = (2 * C) ** 0.5
SHIFT2 = 55.0

COLS = {}
NWC = 0
for _name, _n in (("q", 2 * C), ("k", 2 * C), ("v", C), ("fc1", FF), ("proj", C), ("left", C), ("gatel", C),
                  ("right", C), ("out", C), ("gate2", E2), ("q3", 2 * C), ("k3", 2 * C), ("v3", C),
                  ("router", E3), ("exp3", E3 * C)):
    COLS[_name] = slice(NWC, NWC + _n)
    NWC += _n
LN1_COLS = slice(0, COLS["v"].stop)
LN2_COLS = COLS["fc1"]

NORM_PARTS = ("sum", "centred", "squared", "sumsq", "var", "rstd", "normed", "high", "pair", "turned", "xT")


def spread(ap, n):
    return ap.unsqueeze(2).to_broadcast([ap.shape[0], ap.shape[1], n])


def over(ap, n):
    return ap.unsqueeze(1).to_broadcast([ap.shape[0], n, ap.shape[1]])


def tiles(ap, a=NT):
    return ap.rearrange("p (a b) -> p a b", a=a)



def norm_sum(nc, ln, n1, src, w):
    nc.vector.tensor_reduce(w["sum"], src, AX.X, ALU.add).then_inc(ln["sum"], 1)


def norm_centre(nc, ln, n1, src, w):
    nc.vector.wait_ge(ln["sum"], n1)
    nc.vector.scalar_tensor_tensor(w["xc"], spread(w["sum"], C), -1.0 / C, src, ALU.mult,
                                   ALU.add).then_inc(ln["centred"], 1)


def norm_square(nc, ln, n1, w):
    nc.scalar.wait_ge(ln["centred"], n1)
    nc.scalar.activation(w["sq"], w["xc"], ACT.Square, scale=C ** -0.5).then_inc(ln["squared"], 1)


def norm_sumsq(nc, ln, n1, w):
    nc.vector.wait_ge(ln["squared"], n1)
    nc.vector.tensor_reduce(w["ss"], w["sq"], AX.X, ALU.add).then_inc(ln["sumsq"], 1)


def norm_rstd(nc, ln, n1, w, nhalf, eps):
    nc.gpsimd.wait_ge(ln["sumsq"], n1)
    nc.gpsimd.tensor_tensor(w["var"], w["ss"], eps, ALU.add).then_inc(ln["var"], 1)
    nc.gpsimd.wait_ge(ln["var"], n1)
    nc.gpsimd.tensor_tensor(w["rstd"], w["var"], nhalf, ALU.pow).then_inc(ln["rstd"], 1)


def norm_apply(nc, ln, n1, w, engine=None):
    engine = engine or nc.vector
    engine.wait_ge(ln["rstd"], n1)
    engine.tensor_tensor(w["xn"], w["xc"], spread(w["rstd"], C), ALU.mult).then_inc(ln["normed"], 1)



def cut_high(nc, ln, n1, w, x):
    nc.scalar.wait_ge(ln["normed"], n1)
    nc.scalar.activation(w["hl"][:, :, 0:C], x, ACT.Identity).then_inc(ln["high"], 1)


def cut_low(nc, ln, n1, w, x, engine=None):
    engine = engine or nc.vector
    engine.wait_ge(ln["high"], n1)
    engine.tensor_tensor(w["hl"][:, :, C:2 * C], x, w["hl"][:, :, 0:C], ALU.subtract).then_inc(ln["pair"], 1)


def turn(nc, ln, n1, w, bank, ident16):
    nc.tensor.wait_ge(ln["pair"], n1)
    for g in range(NT):
        last = nc.tensor.transpose(bank[:, g * P:(g + 1) * P], w["hl"][:, g, 0:2 * C], ident16)
    last.then_inc(ln["turned"], 1)


def take_turned(nc, ln, n1, w, bank):
    nc.vector.wait_ge(ln["turned"], n1)
    nc.vector.tensor_copy(w["xT"], bank).then_inc(ln["xT"], 1)


def turn_to_windows(nc, ln, n1, w, bank, perm):
    nc.tensor.wait_ge(ln["pair"], n1)
    for g in range(NT):
        half = (g + NT - 1) % NT
        at = (half // 2) * 4 * WIN * WIN + (half % 2) * WIN * WIN // 2
        out = bank.rearrange("p (w t) -> p w t", t=WIN * WIN)[:, at // 64:at // 64 + 4, at % 64:at % 64 + 32]
        last = nc.tensor.transpose(out, w["hl"][:, g, 0:2 * C], perm)
    last.then_inc(ln["turned"], 1)


def turn_from_windows(nc, ln, n1, w, bank, perm):
    nc.tensor.wait_ge(ln["pair"], n1)
    for g in range(NT):
        rows = bank.rearrange("p (r c) -> p r c", c=W)[:, WIN * (g // 2):WIN * (g // 2) + WIN,
                                                       16 * (g % 2):16 * (g % 2) + 16]
        last = nc.tensor.transpose(rows, w["hl"][:, g, 0:2 * C], perm)
    last.then_inc(ln["turned"], 1)


def take_unrolled(nc, ln, n1, w, bank):
    nc.vector.wait_ge(ln["turned"], n1)
    s, image = WIN // 2, w["xT"].rearrange("p (r c) -> p r c", c=W)
    rolled = bank.rearrange("p (r c) -> p r c", c=W)
    for r0, r1, to_r in ((0, H - s, s), (H - s, H, 0)):
        for c0, c1, to_c in ((0, W - s, s), (W - s, W, 0)):
            last = nc.vector.tensor_copy(image[:, to_r:to_r + r1 - r0, to_c:to_c + c1 - c0], rolled[:, r0:r1, c0:c1])
    last.then_inc(ln["xT"], 1)


class Net:
    pass


def work_buffers(sb, name):
    w = {}
    for k, shape, dt in (("sum", [P, NT], F32), ("ss", [P, NT], F32), ("var", [P, NT], F32), ("rstd", [P, NT], F32),
                         ("xc", [P, NT, C], F32), ("sq", [P, NT, C], F32), ("xn", [P, NT, C], F32),
                         ("hl", [P, NT, 3 * C], F16), ("xT", [P, TOK], F16)):
        w[k] = sb(f"{name}_{k}", shape, dt)[:]
    return w


def stage_setup(net, d, k):
    nc, sem = net.nc, net.sem
    with ExitStack() as ctx:
        def sb(name, shape, dt):
            return ctx.enter_context(nc.sbuf_tensor("su_" + name, shape, dt))

        wc = sb("wc", [P, NWC], F32)
        wh = sb("wh", [P, NWC], F16)
        wl = sb("wl", [P, NWC], F16)
        weq = sb("weq", [P, C], F32)
        raw3 = sb("raw3", [C, 3, 2, C], F32)
        rawg = sb("rawg", [E2, 2, C], F32)
        gains = sb("gains", [P, 2], F32)
        lnb = sb("lnb", [C, 2, 2], F32)
        brf = sb("brf", [2, NWC + C], F32)
        beq = sb("beq", [2, C], F32)
        bh = sb("bh", [2, NWC + C], F16)
        bl = sb("bl", [2, NWC + C], F16)
        fc2 = sb("fc2", [P, 2, C], F32)
        rb = sb("rb", [P, C, HEADS], F32)
        mask = sb("mask", [P, 2, 2, C], F32)
        same = sb("same", [P, P], F32)
        perms = sb("perms", [P, 2, P], F32)
        ps_t = ctx.enter_context(nc.psum_tensor("su_ps_t", [P, 512], F32))
        ps_b = ctx.enter_context(nc.psum_tensor("su_ps_b", [2, 512], F32))
        ps_c = ctx.enter_context(nc.psum_tensor("su_ps_c", [2, 512], F32))

        loaded, chain = sem("setup_loaded"), sem("setup_chain")
        turned, folded = sem("setup_turned"), sem("setup_folded")
        b_loaded, doubled, paired = sem("setup_b_loaded"), sem("setup_doubled"), sem("setup_paired")
        raw_doubled = sem("setup_raw_doubled")
        ndma, nb = [0], [0]

        with nc.Block() as block:
            @block.sync
            def _(sp):
                def load(dst, src):
                    sp.dma_start(dst, src).then_inc(loaded, 16)
                    ndma[0] += 1

                load(net.ident[:], k["ident"])
                load(net.hmask[:], k["hmask"])
                load(perms[:, 0], k["to_windows"])
                load(perms[:, 1], k["from_windows"])
                load(same[:], k["samerow"])
                load(mask[:], k["mask"])
                pieces = [("q", 2 * C, d["L0_conv_qkv_w"]), ("fc1", 0, d["L0_conv_fc1_w"]),
                          ("proj", 0, d["L0_conv_proj_w"]), ("left", 0, d["L1_conv_W_left"]),
                          ("gatel", 0, d["L1_conv_W_gate"]), ("right", 0, d["L1_conv_W_right"]),
                          ("out", 0, d["L1_conv_W_out"]), ("router", 0, d["L3_ffn_router_w"])]
                for name, at, src in pieces:
                    a = COLS[name].start + at
                    load(wc[0:C, a:a + src.shape[1]], src)
                load(wc[0:C, COLS["exp3"]].rearrange("p (e c) -> p e c", e=E3),
                     d["L3_ffn_expert_w"].rearrange("e d c -> d e c"))
                load(weq[0:C, :], d["L1_conv_W_eq"])
                for half in (0, C):
                    load(gains[half:half + C, 0:1], d["L0_conv_ln1_g"].unsqueeze(1))
                    load(gains[half:half + C, 1:2], d["L0_conv_ln2_g"].unsqueeze(1))
                for j, name in enumerate(("L3_attn_Wq", "L3_attn_Wk", "L3_attn_Wv")):
                    load(raw3[:, j, 0, :], d[name])
                load(rawg[:, 0, :], d["L2_ffn_gate_w"])
                load(lnb[:, 0, 0:1], d["L0_conv_ln1_b"].unsqueeze(1))
                load(lnb[:, 1, 0:1], d["L0_conv_ln2_b"].unsqueeze(1))
                load(fc2[:], d["L0_conv_fc2_w"].rearrange("(a p) n -> p a n", a=2))
                load(net.lns[:], d["L1_conv_ln_scale"].unsqueeze(0).to_broadcast([P, C]))
                load(net.lnb[:], d["L1_conv_ln_bias"].unsqueeze(0).to_broadcast([P, C]))
                table = d["L0_conv_rpb"]
                side = 2 * WIN - 1
                for w2 in range(2):
                    for kr in range(WIN):
                        src = bass.AP(table.tensor, table.offset + side * HEADS * kr,
                                      [[side * HEADS, WIN], [HEADS, WIN], [1, WIN * HEADS]])
                        load(rb[64 * w2:64 * w2 + 64, WIN * kr:WIN * kr + WIN, :].rearrange("p k h -> p (k h)"), src)
                sp.wait_ge(paired, 1)
                sp.dma_start(wc[C:P, :], wc[0:C, :]).then_inc(doubled, 16)
                sp.dma_start(brf[1:2, :], brf[0:1, :]).then_inc(doubled, 16)

            @block.gpsimd
            def _(pool):
                qb = d["L0_conv_qkv_b"]
                rows = [("q", 2 * C, qb), ("fc1", 0, d["L0_conv_fc1_b"]), ("proj", 0, d["L0_conv_proj_b"]),
                        ("left", 0, d["L1_conv_b_left"]), ("gatel", 0, d["L1_conv_b_gate"]),
                        ("right", 0, d["L1_conv_b_right"]), ("out", 0, d["L1_conv_b_out"]),
                        ("gate2", 0, d["L2_ffn_gate_b"]), ("q3", 0, d["L3_attn_bq"]),
                        ("k3", 0, d["L3_attn_bk"]), ("v3", 0, d["L3_attn_bv"]),
                        ("router", 0, d["L3_ffn_router_b"]),
                        ("exp3", 0, d["L3_ffn_expert_b"].rearrange("e c -> (e c)"))]
                for name, at, src in rows:
                    a = COLS[name].start + at
                    pool.dma_start(brf[0:1, a:a + src.shape[0]], src.unsqueeze(0)).then_inc(b_loaded, 16)
                pool.dma_start(brf[0:1, NWC:NWC + C], d["L0_conv_fc2_b"].unsqueeze(0)).then_inc(b_loaded, 16)
                pool.dma_start(beq[0:1, :], d["L1_conv_b_eq"].unsqueeze(0)).then_inc(b_loaded, 16)
                nb[0] = len(rows) + 2

            @block.vector
            def _(dve):
                done = [0]

                def link(ins):
                    done[0] += 1
                    ins.then_inc(chain, 1)
                    dve.wait_ge(chain, done[0])

                nc.vector.memset(net.nhalf[:], -0.5)
                nc.vector.memset(net.eps[:], 1e-5)
                nc.vector.memset(net.ones16[:], 1.0)
                dve.wait_ge(loaded, 16 * ndma[0])
                nc.vector.tensor_copy(net.ident16[:], net.ident[:])
                nc.vector.tensor_copy(net.same16[:], same[:])
                nc.vector.tensor_copy(net.perm16[:], perms[:])
                dve.wait_ge(b_loaded, 16 * nb[0])
                nc.vector.tensor_copy(raw3[:, :, 1, :], raw3[:, :, 0, :])
                nc.vector.tensor_copy(rawg[:, 1, :], rawg[:, 0, :])
                link(nc.vector.tensor_copy(lnb[:, :, 1:2], lnb[:, :, 0:1]))
                nc.vector.engine_nop().then_inc(raw_doubled, 1)
                q, k_, v_ = COLS["q"].start, COLS["k"].start, COLS["v"].start
                for tensor in (wc[0:C, :], brf[0:1, :]):
                    link(nc.vector.tensor_copy(tensor[:, q:q + C], tensor[:, q + 2 * C:q + 3 * C]))
                    link(nc.vector.tensor_copy(tensor[:, q + C:q + 2 * C], tensor[:, q:q + C]))
                    link(nc.vector.tensor_copy(tensor[:, k_:k_ + C], tensor[:, k_ + C:k_ + 2 * C]))
                link(nc.vector.tensor_tensor(wc[0:C, COLS["left"]], wc[0:C, COLS["left"]], weq[0:C, :], ALU.add))
                link(nc.vector.tensor_tensor(brf[0:1, COLS["left"]], brf[0:1, COLS["left"]], beq[0:1, :], ALU.add))
                for name in ("q3", "k3"):
                    a = COLS[name].start
                    link(nc.vector.tensor_copy(brf[0:1, a + C:a + 2 * C], brf[0:1, a:a + C]))
                dve.wait_ge(turned, 1)
                for j, name in enumerate(("q3", "k3")):
                    for r in range(2):
                        a = COLS[name].start + r * C
                        nc.vector.tensor_copy(wc[0:C, a:a + C], ps_t[0:C, j * C:(j + 1) * C])
                nc.vector.tensor_copy(wc[0:C, COLS["v3"]], ps_t[0:C, 2 * C:3 * C])
                nc.vector.tensor_copy(wc[0:C, COLS["gate2"]], ps_t[0:C, 3 * C:3 * C + E2]).then_inc(paired, 1)
                dve.wait_ge(doubled, 32)
                dve.wait_ge(folded, 1)
                link(nc.vector.tensor_tensor(brf[:, LN1_COLS], brf[:, LN1_COLS], ps_b[:, LN1_COLS], ALU.add))
                link(nc.vector.tensor_tensor(brf[:, LN2_COLS], brf[:, LN2_COLS], ps_c[:, 0:FF], ALU.add))
                link(nc.vector.tensor_scalar(brf[:], brf[:], WS, None, ALU.mult))
                link(nc.vector.tensor_copy(bh[:], brf[:]))
                link(nc.vector.tensor_tensor(bl[:], brf[:], bh[:], ALU.subtract))
                link(nc.vector.tensor_scalar(bh[:], bh[:], net.ident[0:2, 0:1], None, ALU.mult))
                link(nc.vector.scalar_tensor_tensor(net.bias[:], bl[:], net.ident[0:2, 1:2], bh[:], ALU.mult,
                                                    ALU.add))
                link(nc.vector.tensor_scalar(wc[:, LN1_COLS], wc[:, LN1_COLS], gains[:, 0:1], WS, ALU.mult, ALU.mult))
                link(nc.vector.tensor_scalar(wc[:, LN2_COLS], wc[:, LN2_COLS], gains[:, 1:2], WS, ALU.mult, ALU.mult))
                rest = slice(LN2_COLS.stop, NWC)
                link(nc.vector.tensor_scalar(wc[:, rest], wc[:, rest], WS, None, ALU.mult))
                link(nc.vector.tensor_copy(wh[:], wc[:]))
                link(nc.vector.tensor_tensor(wl[:], wc[:], wh[:], ALU.subtract))
                nc.vector.tensor_copy(net.wa[0:C, :], wh[0:C, :])
                nc.vector.tensor_copy(net.wa[C:P, :], wl[C:P, :])
                nc.vector.tensor_copy(net.wb[0:C, :], wl[0:C, :])
                nc.vector.tensor_copy(net.wb[C:P, :], wh[C:P, :])
                link(nc.vector.tensor_scalar(fc2[:], fc2[:], WS, None, ALU.mult))
                link(nc.vector.tensor_copy(net.fc2h[:], fc2[:]))
                nc.vector.tensor_tensor(net.fc2l[:], fc2[:], net.fc2h[:], ALU.subtract)
                for last_row in range(2):
                    for jp in range(2):
                        back = rb[:].rearrange("p (r c) h -> p h r c", r=WIN)[:, :, ::-1, ::-1]
                        for hd in range(HEADS):
                            nc.vector.tensor_tensor(
                                net.sbias[:, last_row, jp, hd].rearrange("p (r c) -> p r c", c=WIN), back[:, hd],
                                mask[:, last_row, jp].rearrange("p (r c) -> p r c", c=WIN), ALU.add)

            @block.tensor
            def _(pe):
                pe.wait_ge(loaded, 16 * ndma[0])
                pe.wait_ge(raw_doubled, 1)
                for j in range(3):
                    nc.tensor.transpose(ps_t[:, j * C:(j + 1) * C], raw3[:, j].rearrange("p r c -> p (r c)"),
                                        net.ident[0:C, 0:C])
                nc.tensor.transpose(ps_t[:, 3 * C:3 * C + E2], rawg[:].rearrange("p r c -> p (r c)"),
                                    net.ident[0:E2, 0:E2]).then_inc(turned, 1)
                pe.wait_ge(doubled, 32)
                nc.tensor.matmul(ps_b[:, LN1_COLS], lnb[:, 0, :], wc[0:C, LN1_COLS], start=True, stop=True)
                nc.tensor.matmul(ps_c[:, 0:FF], lnb[:, 1, :], wc[0:C, LN2_COLS], start=True,
                                 stop=True).then_inc(folded, 1)


def matmul_pair(nc, out, lhsT, rhs_a, rhs_b, bias_l, bias_r, stop=True):
    nc.tensor.matmul(out, lhsT, rhs_a, start=True, stop=False)
    nc.tensor.matmul(out, lhsT, rhs_b, start=False, stop=False)
    return nc.tensor.matmul(out, bias_l, bias_r, start=False, stop=stop)


def natural(nc, net, out, xT, g, name):
    c = COLS[name]
    return matmul_pair(nc, out, xT[:, g * P:(g + 1) * P], net.wa[:, c], net.wb[:, c], net.ones16[:, 0:P],
                       net.bias[:, c])


def upright(nc, net, out, xT, c, lo, hi):
    nc.tensor.matmul(out, net.wa[:, c], xT[:, lo:hi], start=True, stop=False)
    nc.tensor.matmul(out, net.wb[:, c], xT[:, lo:hi], start=False, stop=False)
    return nc.tensor.matmul(out, net.bias[:, c], net.ones16[:, 0:hi - lo], start=False, stop=True)


def run_steps(engine, steps, ahead, streams, count=B):
    first, last = -max(ahead.values()), count - 1 - min(ahead.values())

    def iteration(i):
        for stream, step in steps:
            n = i + ahead[stream]
            if not isinstance(i, int) or 0 <= n < count:
                streams[stream](n, step)

    full_from, full_to = 1 - min(ahead.values()), count - max(ahead.values())
    for i in range(first, full_from):
        iteration(i)
    with engine.Fori(full_from, full_to) as i:
        iteration(i)
    for i in range(full_to, last + 1):
        iteration(i)


WINDOW_STEPS = [("score", 0), ("score", 1), ("turn", 0), ("score", 2), ("turn", 1), ("weigh", 0), ("score", 3), ("turn", 2),
                ("weigh", 1), ("turn", 3), ("weigh", 2), ("weigh", 3), ("divide", 0), ("unroll", 0), ("project", 0)]


def stage_blocks(net, x):
    nc, sem = net.nc, net.sem
    with ExitStack() as ctx:
        def sb(name, shape, dt):
            return ctx.enter_context(nc.sbuf_tensor("bl_" + name, shape, dt))

        wn, wa, ww, wg, wl = (work_buffers(sb, s) for s in ("norm", "win", "wide", "gate", "last"))
        qx, kh, kl = (sb(s, [P, TOK], F16) for s in ("qx", "kh", "kl"))
        kxh, kxl = (sb(s, [P, HEADS, TOK], F16) for s in ("kxh", "kxl"))
        vh, vl = (sb(s, [P, NW_IMG, 2, 2, HD], F16) for s in ("vh", "vl"))
        att = sb("att", [P, 2, 2, HEADS, C], F32)
        top = sb("top", [P, 2, 2 * HEADS], F32)
        pth, ptl = (sb(s, [P, 2, 4, P], F16) for s in ("pth", "ptl"))
        rs, rinv = (sb(s, [P, NT, HEADS], F32) for s in ("rs", "rinv"))
        on = sb("on", [P, NT, C], F32)
        gel = sb("gel", [P, 2, TOK], F32)
        glh, gll = (sb(s, [P, 2, TOK], F16) for s in ("glh", "gll"))
        x2, rss, th, u, y, scaled_y = (sb(s, [P, NT, C], F32) for s in ("x2", "rss", "th", "u", "y", "scaled_y"))
        rh, rl = (sb(s, [P, NT, C], F16) for s in ("rh", "rl"))
        ps = ctx.enter_context(nc.psum_tensor("bl_ps", [P, 8, 512], F32))
        WINDOW_BANKS, WIDE_BANKS, GATE_BANKS = 0, 4, 6

        def bank(j, n=1):
            return ps[:, j:j + n, :].rearrange("p b n -> p (b n)")

        def bank16(j):
            return ps[:, j, :].bitcast(F16)

        wb, fb, gb = WINDOW_BANKS, WIDE_BANKS, GATE_BANKS
        ln1, ln2, ln3 = net.norms
        co, cx, cu = net.cuts
        x_loaded = sem("x_loaded")
        q_ready, q_taken, kh_taken, kl_taken, k_spread = (sem("bl_" + s) for s in (
            "q_projected", "qh_taken", "kh_taken", "kl_taken", "k_spread"))
        k_ready, ql_taken, v_ready, vh_taken, v_taken = (sem("bl_" + s) for s in (
            "k_projected", "q_taken", "v_projected", "vh_taken", "v_taken"))
        scored, biased, maxed, shifted, exped, summed = (sem("bl_" + s) for s in (
            "scored", "biased", "maxed", "shifted", "exped", "summed"))
        p_turned, ph_taken, pl_taken, weighed, inverted = (sem("bl_" + s) for s in (
            "p_turned", "ph_taken", "pl_taken", "weighed", "inverted"))
        projected, hid_ready, gelued, gh_cut, gl_cut, ffn_out = (sem("bl_" + s) for s in (
            "projected", "hid_ready", "gelued", "gh_cut", "gl_cut", "ffn_out"))
        r_ready, rh_taken, rl_taken, left_ready, gate_ready, rowsummed = (sem("bl_" + s) for s in (
            "r_ready", "rh_taken", "rl_taken", "left_ready", "gate_ready", "rowsummed"))
        rss_taken, tanhed, lefted, outed, scaled, zeroed = (sem("bl_" + s) for s in (
            "rss_taken", "tanhed", "lefted", "outed", "scaled", "zeroed"))
        stored = net.t_ready
        t = net.t
        xv = x.rearrange("n (g r) c k -> (r c) n g k", g=NT)

        STEPS = [("wide", 0), ("windows", 0), ("gate", 0), ("windows", 1), ("wide", 1), ("windows", 2), ("gate", 1),
                 ("windows", 3), ("gate", 2), ("windows", 4), ("wide", 2), ("gate", 3), ("windows", 5), ("norm", 0),
                 ("windows", 6), ("windows", 7), ("windows", 8), ("gate", 4), ("wide", 3), ("gate", 5),
                 ("windows", 9), ("gate", 6), ("wide", 4), ("wide", 5), ("windows", 10), ("windows", 11),
                 ("norm", 1), ("windows", 12), ("wide", 6), ("gate", 7), ("norm", 2), ("wide", 7), ("windows", 13),
                 ("gate", 8), ("last", 0), ("norm", 3), ("last", 1), ("windows", 14), ("wide", 8), ("norm", 4),
                 ("wide", 9), ("last", 2), ("norm", 5), ("norm", 7), ("norm", 6), ("last", 3)]

        AHEAD = {"norm": 2, "windows": 1, "wide": 0, "gate": -1, "last": -1}

        def first(n):
            return isinstance(n, int) and n == 0

        def quarter(q):
            return q // 2, slice(512 * (q % 2), 512 * (q % 2) + 512)

        with nc.Block() as block:
            @block.sync
            def _(sp):
                sp.dma_start(t[:, 0], xv[:, 0]).then_inc(x_loaded, 16)
                with sp.Fori(1, B) as n:
                    sp.wait_ge(x_loaded, 16 * n)
                    sp.dma_start(t[:, n], xv[:, n]).then_inc(x_loaded, 16)

            @block.vector
            def _(dve):
                nc.vector.memset(vh[:], 0.0)
                nc.vector.memset(vl[:], 0.0).then_inc(zeroed, 1)

                def norm(n, step):
                    if step == 0:
                        dve.wait_ge(x_loaded, 16 * n + 16)
                        norm_sum(nc, ln1, n + 1, t[:, n], wn)
                        norm_centre(nc, ln1, n + 1, t[:, n], wn)
                    if step == 1:
                        norm_sumsq(nc, ln1, n + 1, wn)
                    if step == 2:
                        norm_apply(nc, ln1, n + 1, wn)
                    if step == 3:
                        take_turned(nc, ln1, n + 1, wn, bank16(fb))
                    if step == 4:
                        dve.wait_ge(q_taken, n + 1)
                        nc.vector.scalar_tensor_tensor(qx[C:P, :], bank(wb, 2)[C:P, :], IWS, qx[C:P, :],
                                                       ALU.mult, ALU.subtract).then_inc(ql_taken, 1)
                    if step == 5:
                        dve.wait_ge(kh_taken, n + 1)
                        nc.vector.scalar_tensor_tensor(kl[:], bank(wb + 2, 2), IWS, kh[:],
                                                       ALU.mult, ALU.subtract).then_inc(kl_taken, 1)
                    if step == 6:
                        dve.wait_ge(kl_taken, n + 1)
                        for hd in range(HEADS):
                            nc.vector.tensor_scalar(kxh[:, hd, :], kh[:], net.hmask[:, hd:hd + 1], None, ALU.mult)
                            ins = nc.vector.tensor_scalar(kxl[:, hd, :], kl[:], net.hmask[:, hd:hd + 1], None, ALU.mult)
                        ins.then_inc(k_spread, 1)
                    if step == 7:
                        dve.wait_ge(zeroed, 1)
                        dve.wait_ge(vh_taken, n + 1)
                        for hp in range(2):
                            half = slice(C * hp, C * hp + C)
                            ins = nc.vector.scalar_tensor_tensor(
                                vl[half, :, :, hp, :].rearrange("p w a d -> p (w a) d"),
                                bank(wb)[half, :].rearrange("p (w d) -> p w d", d=HD), IWS,
                                vh[half, :, :, hp, :].rearrange("p w a d -> p (w a) d"), ALU.mult, ALU.subtract)
                        ins.then_inc(v_taken, 1)

                def windows(n, step):
                    part, c = WINDOW_STEPS[step]
                    if part == "score":
                        a = att[:, c % 2].rearrange("p t a k -> p (t a) k")
                        dve.wait_ge(scored, piece_count(n, 4, c))
                        if c >= 2:
                            dve.wait_ge(pl_taken, piece_count(n, 4, c - 2))
                        nc.vector.scalar_tensor_tensor(
                            a, tiles(bank(wb + c % 2)), HD ** -0.5,
                            net.sbias[:, int(c == 3)].rearrange("p t a k -> p (t a) k"),
                            ALU.mult, ALU.add).then_inc(biased, 1)
                        dve.wait_ge(biased, piece_count(n, 4, c))
                        nc.vector.tensor_reduce(top[:, c % 2], a, AX.X, ALU.max).then_inc(maxed, 1)
                        dve.wait_ge(maxed, piece_count(n, 4, c))
                        nc.vector.tensor_tensor(a, a, spread(top[:, c % 2], C), ALU.subtract).then_inc(shifted, 1)
                    if part == "turn":
                        a = att[:, c % 2].rearrange("p t a k -> p (t a) k")
                        dve.wait_ge(exped, piece_count(n, 4, c))
                        nc.vector.tensor_reduce(rs[:, 2 * c:2 * c + 2].rearrange("p t a -> p (t a)"), a,
                                                AX.X, ALU.add).then_inc(summed, 1)
                        dve.wait_ge(ph_taken, piece_count(n, 4, c))
                        nc.vector.tensor_tensor(ptl[:, c % 2], tiles(bank(wb + 2), 4),
                                                pth[:, c % 2], ALU.subtract).then_inc(pl_taken, 1)
                    if part == "weigh" and c == 3:
                        dve.wait_ge(summed, piece_count(n, 4, 3))
                        nc.vector.reciprocal(rinv[:], rs[:]).then_inc(inverted, 1)
                    if part == "divide":
                        dve.wait_ge(inverted, n + 1)
                        dve.wait_ge(weighed, piece_count(n, 4, 3))
                        nc.vector.tensor_tensor(
                            on[:].rearrange("p t (a d) -> p (t a) d", a=HEADS),
                            bank(wb + 3).rearrange("p (ta d) -> p ta d", d=HD),
                            spread(rinv[:].rearrange("p t a -> p (t a)"), HD), ALU.mult).then_inc(co["normed"], 1)
                    if part == "unroll":
                        take_unrolled(nc, co, n + 1, wa, bank16(wb))
                    if part == "project":
                        dve.wait_ge(projected, n + 1)
                        nc.vector.scalar_tensor_tensor(t[:, n], tiles(bank(wb + 1)), IWS, t[:, n],
                                                       ALU.mult, ALU.add).then_inc(stored["x1"], 1)

                def wide(n, step):
                    if step == 0:
                        dve.wait_ge(stored["x1"], n + 1)
                        norm_sum(nc, ln2, n + 1, t[:, n], ww)
                        norm_centre(nc, ln2, n + 1, t[:, n], ww)
                    if step == 1:
                        norm_sumsq(nc, ln2, n + 1, ww)
                    if step == 2:
                        norm_apply(nc, ln2, n + 1, ww)
                    if step == 3:
                        take_turned(nc, ln2, n + 1, ww, bank16(fb))
                    if 4 <= step < 8:
                        a, tok = quarter(step - 4)
                        dve.wait_ge(gelued, piece_count(n, 4, step - 4))
                        nc.vector.tensor_copy(glh[:, a, tok], gel[:, a, tok]).then_inc(gh_cut, 1)
                    if step == 9:
                        dve.wait_ge(ffn_out, n + 1)
                        if not first(n):
                            dve.wait_ge(stored["y"], n)
                        nc.vector.scalar_tensor_tensor(x2[:], tiles(bank(fb + 1)), IWS, t[:, n],
                                                       ALU.mult, ALU.add).then_inc(cx["normed"], 1)

                def gate(n, step):
                    if step == 0:
                        take_turned(nc, cx, n + 1, wg, bank16(gb))
                    if step == 1:
                        dve.wait_ge(rh_taken, n + 1)
                        nc.vector.scalar_tensor_tensor(rl[:], tiles(bank(gb + 1)), IWS, rh[:],
                                                       ALU.mult, ALU.subtract).then_inc(rl_taken, 1)
                    if step == 5:
                        dve.wait_ge(rss_taken, n + 1)
                        dve.wait_ge(left_ready, n + 1)
                        nc.vector.tensor_tensor(u[:], tiles(bank(gb)), rss[:], ALU.mult).then_inc(lefted, 1)
                        dve.wait_ge(lefted, n + 1)
                        dve.wait_ge(tanhed, n + 1)
                        nc.vector.scalar_tensor_tensor(u[:], th[:], 1.0, u[:], ALU.add,
                                                       ALU.mult).then_inc(cu["normed"], 1)
                    if step == 7:
                        take_turned(nc, cu, n + 1, wg, bank16(gb + 1))
                    if step == 8:
                        dve.wait_ge(outed, n + 1)
                        nc.vector.scalar_tensor_tensor(y[:], tiles(bank(gb)), IWS, x2[:],
                                                       ALU.mult, ALU.add).then_inc(stored["y"], 1)

                def last(n, step):
                    if step == 0:
                        dve.wait_ge(stored["y"], n + 1)
                        norm_sum(nc, ln3, n + 1, y[:], wl)
                        norm_centre(nc, ln3, n + 1, y[:], wl)
                    if step == 1:
                        norm_sumsq(nc, ln3, n + 1, wl)
                    if step == 2:
                        norm_apply(nc, ln3, n + 1, wl)

                run_steps(dve, STEPS, AHEAD, {"norm": norm, "windows": windows, "wide": wide, "gate": gate, "last": last})

            @block.scalar
            def _(act):
                def norm(n, step):
                    if step == 0:
                        norm_square(nc, ln1, n + 1, wn)
                    if step == 2:
                        cut_high(nc, ln1, n + 1, wn, wn["xn"])
                    if step == 4:
                        act.wait_ge(q_ready, n + 1)
                        nc.scalar.activation(qx[:], bank(wb, 2), ACT.Copy, scale=IWS).then_inc(q_taken, 1)
                    if step == 5:
                        act.wait_ge(k_ready, n + 1)
                        nc.scalar.activation(kh[:], bank(wb + 2, 2), ACT.Copy, scale=IWS).then_inc(kh_taken, 1)
                    if step == 7:
                        act.wait_ge(zeroed, 1)
                        act.wait_ge(v_ready, n + 1)
                        for hp in range(2):
                            half = slice(C * hp, C * hp + C)
                            ins = nc.scalar.activation(
                                vh[half, :, :, hp, :].rearrange("p w a d -> p (w a) d"),
                                bank(wb)[half, :].rearrange("p (w d) -> p w d", d=HD), ACT.Copy, scale=IWS)
                        ins.then_inc(vh_taken, 1)

                def windows(n, step):
                    part, c = WINDOW_STEPS[step]
                    if part == "turn":
                        act.wait_ge(p_turned, piece_count(n, 4, c))
                        nc.scalar.activation(pth[:, c % 2], tiles(bank(wb + 2), 4), ACT.Copy).then_inc(ph_taken, 1)
                    if part == "score":
                        a = att[:, c % 2].rearrange("p t a k -> p (t a k)")
                        act.wait_ge(shifted, piece_count(n, 4, c))
                        nc.scalar.activation(a, a, ACT.Exp).then_inc(exped, 1)
                    if part == "divide":
                        cut_high(nc, co, n + 1, wa, on[:])

                def wide(n, step):
                    if step == 0:
                        norm_square(nc, ln2, n + 1, ww)
                    if step == 2:
                        cut_high(nc, ln2, n + 1, ww, ww["xn"])
                    if 4 <= step < 8:
                        a, tok = quarter(step - 4)
                        act.wait_ge(hid_ready, piece_count(n, 4, step - 4))
                        nc.scalar.activation(gel[:, a, tok], bank(fb + (step + 1) % 2), ACT.Gelu_apprx_tanh,
                                             scale=IWS).then_inc(gelued, 1)
                    if step == 9:
                        cut_high(nc, cx, n + 1, wg, x2[:])

                def gate(n, step):
                    if step == 1:
                        act.wait_ge(r_ready, n + 1)
                        nc.scalar.activation(rh[:], tiles(bank(gb + 1)), ACT.Copy, scale=IWS).then_inc(rh_taken, 1)
                    if step == 3:
                        act.wait_ge(gate_ready, n + 1)
                        nc.scalar.activation(th[:], tiles(bank(gb + 1)), ACT.Tanh, scale=0.5 * IWS).then_inc(tanhed, 1)
                    if step == 4:
                        act.wait_ge(rowsummed, n + 1)
                        nc.scalar.activation(rss[:], tiles(bank(gb + 1)), ACT.Copy,
                                             scale=0.5 * IWS).then_inc(rss_taken, 1)
                    if step == 6:
                        cut_high(nc, cu, n + 1, wg, u[:])

                def last(n, step):
                    if step == 0:
                        norm_square(nc, ln3, n + 1, wl)

                run_steps(act, STEPS, AHEAD, {"norm": norm, "windows": windows, "wide": wide, "gate": gate, "last": last})

            @block.gpsimd
            def _(pool):
                def norm(n, step):
                    if step == 1:
                        norm_rstd(nc, ln1, n + 1, wn, net.nhalf[:], net.eps[:])
                    if step == 2:
                        cut_low(nc, ln1, n + 1, wn, wn["xn"], nc.gpsimd)

                def windows(n, step):
                    part, c = WINDOW_STEPS[step]
                    if part == "divide":
                        cut_low(nc, co, n + 1, wa, on[:], nc.gpsimd)

                def wide(n, step):
                    if step == 1:
                        norm_rstd(nc, ln2, n + 1, ww, net.nhalf[:], net.eps[:])
                    if step == 2:
                        cut_low(nc, ln2, n + 1, ww, ww["xn"], nc.gpsimd)
                    if 4 <= step < 8:
                        a, tok = quarter(step - 4)
                        pool.wait_ge(gh_cut, piece_count(n, 4, step - 4))
                        nc.gpsimd.tensor_tensor(gll[:, a, tok], gel[:, a, tok], glh[:, a, tok],
                                                ALU.subtract).then_inc(gl_cut, 1)
                    if step == 9:
                        cut_low(nc, cx, n + 1, wg, x2[:], nc.gpsimd)

                def gate(n, step):
                    if step == 6:
                        cut_low(nc, cu, n + 1, wg, u[:], nc.gpsimd)

                def last(n, step):
                    if step == 1:
                        norm_rstd(nc, ln3, n + 1, wl, net.nhalf[:], net.eps[:])
                    if step == 2:
                        pool.wait_ge(ln3["normed"], n + 1)
                        nc.gpsimd.tensor_tensor(scaled_y[:], wl["xn"], over(net.lns[:], NT), ALU.mult).then_inc(scaled, 1)
                    if step == 3:
                        pool.wait_ge(scaled, n + 1)
                        nc.gpsimd.tensor_tensor(t[:, n], scaled_y[:], over(net.lnb[:], NT), ALU.add).then_inc(stored["t"], 1)

                run_steps(pool, STEPS, AHEAD, {"norm": norm, "windows": windows, "wide": wide, "gate": gate, "last": last})
                pool.wait_ge(stored["t"], B)

            @block.tensor
            def _(pe):
                def norm(n, step):
                    xT = wn["xT"]
                    if step == 3:
                        if not isinstance(n, int) or n >= 2:
                            pe.wait_ge(gelued, 4 * (n - 1))
                        turn_to_windows(nc, ln1, n + 1, wn, bank16(fb), net.perm16[:, 0])
                    if step == 4:
                        pe.wait_ge(ln1["xT"], n + 1)
                        if not first(n):
                            pe.wait_ge(stored["x1"], n)
                        for half in range(2):
                            ins = upright(nc, net, bank(wb + half), xT, COLS["q"], 512 * half, 512 * half + 512)
                        ins.then_inc(q_ready, 1)
                    if step == 5:
                        for half in range(2):
                            ins = upright(nc, net, bank(wb + 2 + half), xT, COLS["k"], 512 * half, 512 * half + 512)
                        ins.then_inc(k_ready, 1)
                    if step == 7:
                        pe.wait_ge(ql_taken, n + 1)
                        for w in range(NW_IMG):
                            for hp in range(2):
                                def heads(ap):
                                    return ap[:, COLS["v"]].rearrange("p (a b d) -> p a b d", a=2, b=2)[:, :, hp, :]
                                ins = matmul_pair(nc, bank(wb)[C * hp:C * hp + C, 32 * w:32 * w + 32],
                                                  xT[:, C * w:C * w + C], heads(net.wa), heads(net.wb),
                                                  net.ones16[:, 0:C], heads(net.bias))
                        ins.then_inc(v_ready, 1)

                def windows(n, step):
                    part, c = WINDOW_STEPS[step]
                    if part == "score":
                        if c == 0:
                            pe.wait_ge(k_spread, n + 1)
                            pe.wait_ge(v_taken, n + 1)
                        else:
                            pe.wait_ge(biased, piece_count(n, 4, c - 1))
                        for tt in range(2):
                            for w in range(2):
                                tok = slice((2 * c + tt) * P + C * w, (2 * c + tt) * P + C * w + C)
                                out = bank(wb + c % 2)[C * w:C * w + C, 256 * tt:256 * tt + 256]
                                nc.tensor.matmul(out, qx[:, tok], kxh[:, :, tok], start=True, stop=False)
                                ins = nc.tensor.matmul(out, qx[:, tok], kxl[:, :, tok], start=False, stop=True)
                        ins.then_inc(scored, 1)
                    if part == "turn":
                        pe.wait_ge(exped, piece_count(n, 4, c))
                        if c >= 1:
                            pe.wait_ge(pl_taken, piece_count(n, 4, c - 1))
                        for j in range(4):
                            ins = nc.tensor.transpose(
                                bank(wb + 2)[:, P * j:P * j + P],
                                att[:, c % 2, j // 2, 2 * (j % 2):2 * (j % 2) + 2, :].rearrange(
                                    "p a k -> p (a k)"), net.ident[:])
                        ins.then_inc(p_turned, 1)
                    if part == "weigh":
                        pe.wait_ge(pl_taken, piece_count(n, 4, c))
                        for j in range(4):
                            g, hq = 2 * c + j // 2, j % 2
                            for w in range(2):
                                out = bank(wb + 3)[C * w:C * w + C, C * g + 32 * hq:C * g + 32 * hq + 32]
                                high = pth[:, c % 2, j, C * w:C * w + C]
                                low = ptl[:, c % 2, j, C * w:C * w + C]
                                v_high = vh[:, 2 * g + w, hq].rearrange("p a d -> p (a d)")
                                v_low = vl[:, 2 * g + w, hq].rearrange("p a d -> p (a d)")
                                nc.tensor.matmul(out, high, v_high, start=True, stop=False)
                                nc.tensor.matmul(out, high, v_low, start=False, stop=False)
                                ins = nc.tensor.matmul(out, low, v_high, start=False, stop=True)
                        ins.then_inc(weighed, 1)
                    if part == "unroll":
                        turn_from_windows(nc, co, n + 1, wa, bank16(wb), net.perm16[:, 1])
                    if part == "project":
                        pe.wait_ge(co["xT"], n + 1)
                        for g in range(NT):
                            ins = natural(nc, net, bank(wb + 1)[:, C * g:C * g + C], wa["xT"], g, "proj")
                        ins.then_inc(projected, 1)

                def wide(n, step):
                    if step == 3:
                        turn(nc, ln2, n + 1, ww, bank16(fb), net.ident16[:])
                    if 4 <= step < 8:
                        a, tok = quarter(step - 4)
                        if step == 4:
                            pe.wait_ge(ln2["xT"], n + 1)
                            if not first(n):
                                pe.wait_ge(cx["normed"], n)
                        if step >= 6:
                            pe.wait_ge(gelued, piece_count(n, 4, step - 6))
                        c = slice(COLS["fc1"].start + P * a, COLS["fc1"].start + P * a + P)
                        upright(nc, net, bank(fb + (step + 1) % 2), ww["xT"], c, tok.start, tok.stop).then_inc(hid_ready, 1)
                    if step == 8:
                        pe.wait_ge(gl_cut, piece_count(n, 4, 3))
                        for g in range(NT):
                            out = bank(fb + 1)[:, C * g:C * g + C]
                            tok = slice(P * g, P * g + P)
                            nc.tensor.matmul(out, net.ones16[:, 0:P], net.bias[:, NWC:NWC + C], start=True, stop=False)
                            for a in range(2):
                                nc.tensor.matmul(out, glh[:, a, tok], net.fc2h[:, a], start=False, stop=False)
                                nc.tensor.matmul(out, glh[:, a, tok], net.fc2l[:, a], start=False, stop=False)
                                ins = nc.tensor.matmul(out, gll[:, a, tok], net.fc2h[:, a], start=False, stop=(a == 1))
                        ins.then_inc(ffn_out, 1)

                def gate(n, step):
                    xT = wg["xT"]
                    if step == 0:
                        if not first(n):
                            pe.wait_ge(stored["y"], n)
                        turn(nc, cx, n + 1, wg, bank16(gb), net.ident16[:])
                    if step == 1:
                        pe.wait_ge(cx["xT"], n + 1)
                        for g in range(NT):
                            ins = natural(nc, net, bank(gb + 1)[:, C * g:C * g + C], xT, g, "right")
                        ins.then_inc(r_ready, 1)
                    if step == 2:
                        for g in range(NT):
                            ins = natural(nc, net, bank(gb)[:, C * g:C * g + C], xT, g, "left")
                        ins.then_inc(left_ready, 1)
                    if step == 3:
                        pe.wait_ge(rl_taken, n + 1)
                        for g in range(NT):
                            ins = natural(nc, net, bank(gb + 1)[:, C * g:C * g + C], xT, g, "gatel")
                        ins.then_inc(gate_ready, 1)
                    if step == 4:
                        pe.wait_ge(tanhed, n + 1)
                        nc.tensor.matmul(bank(gb + 1), net.same16[:], rh[:].rearrange("p g c -> p (g c)"),
                                         start=True, stop=False)
                        ins = nc.tensor.matmul(bank(gb + 1), net.same16[:], rl[:].rearrange("p g c -> p (g c)"),
                                               start=False, stop=True)
                        ins.then_inc(rowsummed, 1)
                    if step == 7:
                        turn(nc, cu, n + 1, wg, bank16(gb + 1), net.ident16[:])
                    if step == 8:
                        pe.wait_ge(cu["xT"], n + 1)
                        for g in range(NT):
                            ins = natural(nc, net, bank(gb)[:, C * g:C * g + C], xT, g, "out")
                        ins.then_inc(outed, 1)

                def last(n, step):
                    pass

                run_steps(pe, STEPS, AHEAD, {"norm": norm, "windows": windows, "wide": wide, "gate": gate, "last": last})


def pairs_of_tiles(t, image):
    return (t[:].rearrange("p (i h) g c -> p i (h g) c", h=2),
            image.rearrange("(i h) (g r) c k -> (r c) i (h g) k", h=2, g=NT))


def finish_store(net, out):
    nc, sem = net.nc, net.sem
    tp, ov = pairs_of_tiles(net.t, out)
    x_stored = sem("x_stored")
    with nc.Block() as block:
        @block.sync
        def _(sp):
            with sp.Fori(0, PAIRS) as i:
                sp.dma_start(ov[:, i], tp[:, i]).then_inc(x_stored, 16)
            sp.wait_ge(x_stored, 16 * PAIRS)


def piece_count(n, per, k):
    return per * n + k + 1


def tile_at(i, h, m):
    while m < 0:
        i, h, m = (i, 0, m + NT) if h else (i - 1, 1, m + NT)
    while m >= NT:
        i, h, m = (i + 1, 0, m - NT) if h else (i, 1, m - NT)
    if isinstance(i, int) and not 0 <= i < PAIRS:
        return None
    return i, h, m


def stream(engine, step, near, far, lag, near_first=False):
    def image(i, h, next_one, next_but_one):
        for m in range(NT):
            if next_one and near_first:
                near(*next_one, m)
            step(i, h, m)
            if next_one and not near_first:
                near(*next_one, m)
            if next_but_one:
                far(*next_but_one, m)

    for m in range(NT):
        far(0, 0, m)
    for m in range(NT):
        near(0, 0, m)
        far(0, 1, m)
    step(0, 0, -1)
    image(0, 0, (0, 1), (1, 0))
    with engine.Fori(0, PAIRS - 2) as i:
        image(i, 1, (i + 1, 0), (i + 1, 1))
        image(i + 1, 0, (i + 1, 1), (i + 2, 0))
    image(PAIRS - 2, 1, (PAIRS - 1, 0), (PAIRS - 1, 1))
    image(PAIRS - 1, 0, (PAIRS - 1, 1), None)
    image(PAIRS - 1, 1, None, None)
    for m in range(NT, NT + lag):
        step(PAIRS - 1, 1, m)


def stage_attend(net, d):
    nc, sem = net.nc, net.sem
    RING, PARTS, LAG = 8, 8, 3
    with ExitStack() as ctx:
        def sb(name, shape, dt):
            return ctx.enter_context(nc.sbuf_tensor("a2_" + name, shape, dt))

        wk = [work_buffers(sb, f"w{h}") for h in range(2)]
        xTb = [sb(f"xTb{h}", [P, TOK], F16) for h in range(2)]
        ex = sb("ex", [P, RING, TOK], F32)
        exh = sb("exh", [P, PARTS, TOK], F16)
        exl = sb("exl", [P, PARTS, TOK], F16)
        rs = [sb(f"rs{h}", [P, NT], F32) for h in range(2)]
        rinv = [sb(f"rinv{h}", [P, NT], F32) for h in range(2)]
        o = [sb(f"o{h}", [P, NT, C], F32) for h in range(2)]
        shift = sb("shift", [P, 1], F32)
        ps_s = ctx.enter_context(nc.psum_tensor("a2_ps_s", [P, 2, TOK], F32))
        ps_o = ctx.enter_context(nc.psum_tensor("a2_ps_o", [P, 2, 512], F32))
        ps_t = ctx.enter_context(nc.psum_tensor("a2_ps_t", [P, 2, TOK], F16))
        ln = net.norms[0]
        doubled, turned_b, xTb_done, shift_set = (sem("a2_" + s) for s in ("doubled", "turned_b", "xTb", "shift_set"))
        scored, exped, high_s, high_v, low_v, low_g, weighed = (sem("a2_" + s) for s in (
            "scored", "exped", "high_s", "high_v", "low_v", "low_g", "weighed"))
        inverted, normed, added = (sem("a2_" + s) for s in ("inverted", "normed", "added"))
        tv = net.t[:].rearrange("p (i h) g c -> p i h g c", h=2)
        base = net.normed
        net.normed += B

        def count(at, lag=0):
            i, h, m = at
            return NT * (2 * i + h) + m - lag + 1

        def half_count(at, lag=0):
            i, h, m = at
            return (NT // 2) * (2 * i + h) + m // 2 - lag // 2 + 1

        def past(at, lag):
            return tile_at(at[0], at[1], at[2] - lag) is not None

        def now(i, h, m):
            return tile_at(i, h, m) if m >= 0 else None

        def nothing(i, h, m):
            pass

        with nc.Block() as block:
            @block.vector
            def _(dve):
                nc.vector.memset(shift[:], -SHIFT2).then_inc(shift_set, 1)

                def near(i, h, k):
                    n, w = base + 2 * i + h, wk[h]
                    if k == 5:
                        cut_low(nc, ln, n + 1, w, w["xn"])
                        nc.vector.tensor_copy(w["hl"][:, :, 2 * C:3 * C], w["hl"][:, :, 0:C]).then_inc(doubled, 1)
                    if k == 7:
                        take_turned(nc, ln, n + 1, w, ps_t[:, 0])
                        dve.wait_ge(turned_b, 2 * i + h + 1)
                        nc.vector.tensor_copy(xTb[h][:], ps_t[:, 1]).then_inc(xTb_done, 1)

                def far(i, h, k):
                    n, w, src = base + 2 * i + h, wk[h], tv[:, i, h]
                    if k == 0:
                        norm_sum(nc, ln, n + 1, src, w)
                        norm_centre(nc, ln, n + 1, src, w)
                    if k == 3:
                        norm_sumsq(nc, ln, n + 1, w)
                    if k == 6:
                        norm_apply(nc, ln, n + 1, w)

                def step(i, h, m):
                    at = tile_at(i, h, m - 1)
                    if at and at[2] % 2 == 0:
                        r = at[2] % RING
                        dve.wait_ge(high_s, half_count(at))
                        nc.vector.tensor_tensor(exl[:, at[2]], ex[:, r], exh[:, at[2]], ALU.subtract).then_inc(low_v, 1)
                    at = now(i, h, m)
                    if at and at[2] % 2:
                        r = at[2] % RING
                        dve.wait_ge(exped, count(at))
                        if past(at, PARTS):
                            dve.wait_ge(weighed, count(at, PARTS))
                        nc.vector.tensor_copy(exh[:, at[2]], ex[:, r]).then_inc(high_v, 1)
                    at = tile_at(i, h, m - LAG - 1)
                    if at and at[2] == NT - 1:
                        ia, ha, g = at
                        n = 2 * ia + ha
                        nc.vector.reciprocal(rinv[ha][:], rs[ha][:]).then_inc(inverted, 1)
                        dve.wait_ge(inverted, n + 1)
                        dve.wait_ge(weighed, count(at))
                        nc.vector.tensor_tensor(o[ha][:], tiles(ps_o[:, ha]), spread(rinv[ha][:], C),
                                                ALU.mult).then_inc(normed, 1)
                        dve.wait_ge(normed, n + 1)
                        nc.vector.tensor_tensor(tv[:, ia, ha], tv[:, ia, ha], o[ha][:], ALU.add).then_inc(added, 1)

                stream(dve, step, near, far, LAG + 1)
                dve.wait_ge(added, B)

            @block.scalar
            def _(act):
                act.wait_ge(shift_set, 1)

                def near(i, h, k):
                    n, w = base + 2 * i + h, wk[h]
                    if k == 3:
                        if not isinstance(i, int) or 2 * i + h >= 2:
                            act.wait_ge(weighed, NT * (2 * i + h - 1))
                        cut_high(nc, ln, n + 1, w, w["xn"])

                def far(i, h, k):
                    if k == 1:
                        norm_square(nc, ln, base + 2 * i + h + 1, wk[h])

                def step(i, h, m):
                    at = now(i, h, m)
                    if at:
                        r = at[2] % RING
                        act.wait_ge(scored, count(at))
                        if past(at, RING):
                            act.wait_ge(low_v if at[2] % 2 == 0 else low_g, half_count(at, RING))
                        if at[2] == 0 and past(at, 2 * NT):
                            act.wait_ge(added, 2 * at[0] + at[1] - 1)
                        nc.scalar.activation(ex[:, r], ps_s[:, m % 2], ACT.Exp, bias=shift[:],
                                             accum_out=rs[at[1]][:, m:m + 1]).then_inc(exped, 1)
                        if at[2] % 2 == 0:
                            act.wait_ge(exped, count(at))
                            if past(at, PARTS):
                                act.wait_ge(weighed, count(at, PARTS))
                            nc.scalar.activation(exh[:, at[2]], ex[:, r], ACT.Copy).then_inc(high_s, 1)

                stream(act, step, near, far, 0)

            @block.gpsimd
            def _(pool):
                def far(i, h, k):
                    if k == 3:
                        norm_rstd(nc, ln, base + 2 * i + h + 1, wk[h], net.nhalf[:], net.eps[:])

                def step(i, h, m):
                    at = now(i, h, m)
                    if at and at[2] % 2:
                        r = at[2] % RING
                        pool.wait_ge(high_v, half_count(at))
                        nc.gpsimd.tensor_tensor(exl[:, at[2]], ex[:, r], exh[:, at[2]], ALU.subtract).then_inc(low_g, 1)

                stream(pool, step, nothing, far, 0)

            @block.tensor
            def _(pe):
                def near(i, h, k):
                    n, w = base + 2 * i + h, wk[h]
                    if k == 6:
                        turn(nc, ln, n + 1, w, ps_t[:, 0], net.ident16[:])
                        pe.wait_ge(doubled, 2 * i + h + 1)
                        if not isinstance(i, int) or 2 * i + h >= 1:
                            pe.wait_ge(xTb_done, 2 * i + h)
                        for g in range(NT):
                            ins = nc.tensor.transpose(ps_t[:, 1, P * g:P * g + P], w["hl"][:, g, C:3 * C],
                                                      net.ident16[:])
                        ins.then_inc(turned_b, 1)

                def step(i, h, m):
                    at = now(i, h, m)
                    if at:
                        ia, ha, g = at
                        if g == 0:
                            pe.wait_ge(xTb_done, 2 * ia + ha + 1)
                            pe.wait_ge(ln["xT"], base + 2 * ia + ha + 1)
                        if past(at, 2):
                            pe.wait_ge(exped, count(at, 2))
                        tok = slice(P * g, P * g + P)
                        for half in range(2):
                            out = ps_s[:, g % 2, 512 * half:512 * half + 512]
                            z = wk[ha]["xT"][:, 512 * half:512 * half + 512]
                            nc.tensor.matmul(out, wk[ha]["xT"][:, tok], z, start=True, stop=False)
                            ins = nc.tensor.matmul(out, xTb[ha][:, tok], z, start=False, stop=True)
                        ins.then_inc(scored, 1)
                    at = tile_at(i, h, m - LAG)
                    if at:
                        ia, ha, k = at
                        pe.wait_ge(low_v if k % 2 == 0 else low_g, half_count(at))
                        if k == 0 and past(at, 2 * NT):
                            pe.wait_ge(added, 2 * ia + ha - 1)
                        z_high, z_low = wk[ha]["hl"][:, k, 0:C], wk[ha]["hl"][:, k, C:2 * C]
                        for g in range(NT):
                            out = ps_o[:, ha, C * g:C * g + C]
                            e_high = exh[:, k, P * g:P * g + P]
                            e_low = exl[:, k, P * g:P * g + P]
                            nc.tensor.matmul(out, e_high, z_high, start=(k == 0 and g == 0), stop=False,
                                             skip_group_check=True)
                            nc.tensor.matmul(out, e_high, z_low, start=False, stop=False, skip_group_check=True)
                            ins = nc.tensor.matmul(out, e_low, z_high, start=False, stop=(k == NT - 1),
                                                   skip_group_check=True)
                        ins.then_inc(weighed, 1)

                stream(pe, step, near, nothing, LAG)


def stage_pool(net, d):
    nc, sem = net.nc, net.sem
    with ExitStack() as ctx:
        def sb(name, shape, dt):
            return ctx.enter_context(nc.sbuf_tensor("f2_" + name, shape, dt))

        kept = sb("kept", [P, NG, TOK], F32)
        pooled = sb("pooled", [C + 1, E2, B], F32)
        experts = sb("experts", [P, NG, C], F32)
        pooled_ready, zero_set = sem("f2_pooled_ready"), sem("f2_zero_set")
        base = net.normed
        net.normed += B
        with ExitStack() as inner:
            def sb(name, shape, dt):
                return inner.enter_context(nc.sbuf_tensor("f2_" + name, shape, dt))

            wk = [work_buffers(sb, f"w{j}") for j in range(GRP)]
            prob = sb("prob", [P, TOK], F32)
            rest = sb("rest", [P, TOK], F32)
            mask = sb("mask", [P, TOK], F32)
            mask_t = sb("mask_t", [P, NT, P], F32)
            small = sb("small", [P, 4], F32)
            top = sb("top", [P, 8], F32)
            idle = sb("idle", [P, 1], F32)
            ps_t = inner.enter_context(nc.psum_tensor("f2_ps_t", [P, 2, TOK], F16))
            ps_l = inner.enter_context(nc.psum_tensor("f2_ps_l", [P, TOK], F32))
            ps_m = inner.enter_context(nc.psum_tensor("f2_ps_m", [P, TOK], F32))
            ps_p = inner.enter_context(nc.psum_tensor("f2_ps_p", [C, P], F32))
            ln = net.norms[0]
            logits, maxed, negated, exped, inverted, probs = (sem("f2_" + s) for s in (
                "logits", "maxed", "negated", "exped", "inverted", "probs"))
            topped, replaced, masked, mask_kept, mask_turned, mask_t_taken = (sem("f2_" + s) for s in (
                "topped", "replaced", "masked", "mask_kept", "mask_turned", "mask_t_taken"))
            pool_ready = sem("f2_pool_ready")
            tg = net.t[:].rearrange("p (i j) g c -> p i j g c", j=GRP)
            pg = pooled[:].rearrange("p e (i j) -> p i j e", j=GRP)

            with nc.Block() as block:
                @block.vector
                def _(dve):
                    nc.vector.memset(pooled[C:C + 1], 1.0)
                    with dve.Fori(0, NG) as i:
                        def n1(j):
                            return base + GRP * i + j + 1

                        for j in range(GRP):
                            norm_sum(nc, ln, n1(j), tg[:, i, j], wk[j])
                        for j in range(GRP):
                            norm_centre(nc, ln, n1(j), tg[:, i, j], wk[j])
                        for j in range(GRP):
                            norm_sumsq(nc, ln, n1(j), wk[j])
                        for j in range(GRP):
                            norm_apply(nc, ln, n1(j), wk[j])
                        for j in range(GRP):
                            cut_low(nc, ln, n1(j), wk[j], wk[j]["xn"])
                        for j in range(GRP):
                            take_turned(nc, ln, n1(j), wk[j], ps_t[:, j % 2])
                        dve.wait_ge(logits, i + 1)
                        nc.vector.tensor_reduce(small[:, 0:1], ps_l[:], AX.X, ALU.max).then_inc(maxed, 1)
                        dve.wait_ge(maxed, i + 1)
                        nc.vector.tensor_scalar(small[:, 1:2], small[:, 0:1], -IWS, None, ALU.mult).then_inc(negated, 1)
                        dve.wait_ge(exped, i + 1)
                        nc.vector.reciprocal(small[:, 3:4], small[:, 2:3]).then_inc(inverted, 1)
                        dve.wait_ge(inverted, i + 1)
                        nc.vector.tensor_scalar(prob[:], rest[:], small[:, 3:4], None, ALU.mult).then_inc(probs, 1)
                        dve.wait_ge(probs, i + 1)
                        nc.vector.memset(idle[:], 0.0)
                        nc.vector.max(top[:], prob[:]).then_inc(topped, 1)
                        dve.wait_ge(topped, i + 1)
                        nc.vector.memset(idle[:], 0.0)
                        nc.vector.match_replace(rest[:], top[:], prob[:], 0.0).then_inc(replaced, 1)
                        dve.wait_ge(replaced, i + 1)
                        nc.vector.tensor_tensor(mask[:], prob[:], rest[:], ALU.subtract).then_inc(masked, 1)
                        dve.wait_ge(mask_turned, i + 1)
                        nc.vector.tensor_copy(mask_t[:].rearrange("p a b -> p (a b)"), ps_m[:]).then_inc(mask_t_taken, 1)
                        dve.wait_ge(pool_ready, i + 1)
                        nc.vector.tensor_copy(pg[0:C, i], ps_p[:].rearrange("p (j e) -> p j e", j=GRP)
                                              ).then_inc(pooled_ready, 1)
                        dve.wait_ge(pooled_ready, i + 1)
                        dve.wait_ge(mask_kept, i + 1)

                @block.scalar
                def _(act):
                    with act.Fori(0, NG) as i:
                        def n1(j):
                            return base + GRP * i + j + 1

                        for j in range(GRP):
                            norm_square(nc, ln, n1(j), wk[j])
                        for j in range(GRP):
                            cut_high(nc, ln, n1(j), wk[j], wk[j]["xn"])
                        act.wait_ge(negated, i + 1)
                        nc.scalar.activation(rest[:], ps_l[:], ACT.Exp, bias=small[:, 1:2], scale=IWS,
                                             accum_out=small[:, 2:3]).then_inc(exped, 1)
                        act.wait_ge(masked, i + 1)
                        nc.scalar.activation(kept[:, i], mask[:], ACT.Copy).then_inc(mask_kept, 1)

                @block.gpsimd
                def _(pool):
                    with pool.Fori(0, NG) as i:
                        for j in range(GRP):
                            norm_rstd(nc, ln, base + GRP * i + j + 1, wk[j], net.nhalf[:], net.eps[:])

                @block.tensor
                def _(pe):
                    with pe.Fori(0, NG) as i:
                        def n1(j):
                            return base + GRP * i + j + 1

                        for j in range(GRP):
                            if j >= 2:
                                pe.wait_ge(ln["xT"], n1(j - 2))
                            turn(nc, ln, n1(j), wk[j], ps_t[:, j % 2], net.ident16[:])
                        c = COLS["gate2"]
                        for j in range(GRP):
                            pe.wait_ge(ln["xT"], n1(j))
                            for half in range(2):
                                tok = slice(512 * half, 512 * half + 512)
                                out, x = ps_l[E2 * j:E2 * j + E2, tok], wk[j]["xT"][:, tok]
                                nc.tensor.matmul(out, net.wa[:, c], x, start=True, stop=False, tile_position=(0, E2 * j))
                                nc.tensor.matmul(out, net.wb[:, c], x, start=False, stop=False,
                                                 tile_position=(0, E2 * j))
                                last = nc.tensor.matmul(out, net.bias[:, c], net.ones16[:, 0:512], start=False,
                                                        stop=True, tile_position=(0, E2 * j))
                        last.then_inc(logits, 1)
                        pe.wait_ge(masked, i + 1)
                        for g in range(NT):
                            last = nc.tensor.transpose(ps_m[:, P * g:P * g + P], mask[:, P * g:P * g + P], net.ident[:])
                        last.then_inc(mask_turned, 1)
                        pe.wait_ge(mask_t_taken, i + 1)
                        for j in range(GRP):
                            for g in range(NT):
                                last = nc.tensor.matmul(ps_p[:, E2 * j:E2 * j + E2], wk[j]["xn"][:, g],
                                                        mask_t[:, g, E2 * j:E2 * j + E2], start=(g == 0),
                                                        stop=(g == NT - 1))
                        last.then_inc(pool_ready, 1)

        scratch = nc.dram_tensor("expert_outputs", (B, E2, C), F32, kind="Internal").ap()
        with ExitStack() as inner:
            def sb(name, shape, dt):
                return inner.enter_context(nc.sbuf_tensor("f2_" + name, shape, dt))

            w1 = sb("w1", [C + 1, E2, HID], F32)
            w2 = sb("w2", [P, 2, E2, C], F32)
            w2b = sb("w2b", [P, C], F32)
            hid = sb("hid", [P, 2, E2, B], F32)
            outs = sb("outs", [B, E2, C], F32)
            ps_h = inner.enter_context(nc.psum_tensor("f2_ps_h", [P, 2, E2, B], F32))
            ps_y = inner.enter_context(nc.psum_tensor("f2_ps_y", [B, E2, C], F32))
            w_loaded, hid_ready, gelued, out_ready, out_taken, bounced, back = (sem("f2_" + s) for s in (
                "w_loaded", "hid_ready", "gelued", "out_ready", "out_taken", "bounced", "back"))
            biased = sem("f2_biased")
            with nc.Block() as block:
                @block.sync
                def _(sp):
                    sp.dma_start(w1[:], d["L2_ffn_weight1"].rearrange("e d h -> d e h")).then_inc(w_loaded, 16)
                    for a in range(2):
                        sp.dma_start(w2[:, a], d["L2_ffn_weight2"][:, P * a:P * a + P, :].rearrange("e p o -> p e o")
                                     ).then_inc(w_loaded, 16)
                    for j in range(GRP):
                        sp.dma_start(w2b[E2 * j:E2 * j + E2, :], d["L2_ffn_weight2"][:, HID, :]).then_inc(w_loaded, 16)
                    sp.wait_ge(out_taken, 1)
                    sp.dma_start(scratch, outs[:]).then_inc(bounced, 16)
                    sp.wait_ge(bounced, 16)
                    sp.dma_start(experts[:], scratch.rearrange("(g j) e o -> (j e) g o", j=GRP)).then_inc(back, 16)

                @block.tensor
                def _(pe):
                    pe.wait_ge(w_loaded, 16 * 7)
                    for a in range(2):
                        for e in range(E2):
                            last = nc.tensor.matmul(ps_h[:, a, e], w1[:, e, P * a:P * a + P], pooled[:, e], start=True,
                                                    stop=True)
                        last.then_inc(hid_ready, 1)
                    pe.wait_ge(gelued, 2)
                    for e in range(E2):
                        nc.tensor.matmul(ps_y[:, e], hid[:, 0, e], w2[:, 0, e], start=True, stop=False)
                        last = nc.tensor.matmul(ps_y[:, e], hid[:, 1, e], w2[:, 1, e], start=False, stop=True)
                    last.then_inc(out_ready, 1)

                @block.scalar
                def _(act):
                    for a in range(2):
                        act.wait_ge(hid_ready, 2)
                        nc.scalar.activation(hid[:, a], ps_h[:, a], ACT.Gelu).then_inc(gelued, 1)

                @block.vector
                def _(dve):
                    dve.wait_ge(out_ready, 1)
                    nc.vector.tensor_copy(outs[:], ps_y[:]).then_inc(out_taken, 1)
                    dve.wait_ge(back, 16)
                    dve.wait_ge(w_loaded, 16 * 7)
                    nc.vector.tensor_tensor(experts[:], experts[:], over(w2b[:], NG), ALU.add).then_inc(biased, 1)
                    dve.wait_ge(biased, 1)

        with ExitStack() as inner:
            def sb(name, shape, dt):
                return inner.enter_context(nc.sbuf_tensor("f2_" + name, shape, dt))

            mask = [sb(f"maskb{q}", [P, TOK], F32) for q in range(2)]
            diag = [sb(f"diag{q}", [P, GRP, C], F32) for q in range(2)]
            ps_s = [inner.enter_context(nc.psum_tensor(f"f2_ps_s{q}", [P, NT, GRP, C], F32)) for q in range(2)]
            diag_zero, ready, spread_out, added = (sem("f2_" + s) for s in (
                "diag_zero", "ready", "spread_out", "added"))
            kq = kept[:].rearrange("p (i q) s -> p i q s", q=2)
            eq = experts[:].rearrange("p (i q) c -> p i q c", q=2)
            tq = net.t[:].rearrange("p (i q j) g c -> p i q j g c", q=2, j=GRP)
            with nc.Block() as block:
                @block.vector
                def _(dve):
                    for q in range(2):
                        nc.vector.memset(diag[q][:], 0.0).then_inc(diag_zero, 1)
                    dve.wait_ge(diag_zero, 2)

                    def prepare(i, q):
                        nc.vector.tensor_copy(mask[q][:], kq[:, i, q])
                        for j in range(GRP):
                            rows = slice(E2 * j, E2 * j + E2)
                            last = nc.vector.tensor_copy(diag[q][rows, j], eq[rows, i, q])
                        last.then_inc(ready, 1)

                    with dve.Fori(0, max(NG // 2, 1)) as i:
                        for q in range(min(2, NG)):
                            prepare(i, q)
                        for q in range(min(2, NG)):
                            dve.wait_ge(spread_out, 2 * i + q + 1)
                            for j in range(GRP):
                                last = nc.vector.tensor_tensor(tq[:, i, q, j], tq[:, i, q, j], ps_s[q][:, :, j, :],
                                                               ALU.add)
                            last.then_inc(added, 1)
                    dve.wait_ge(added, NG)

                @block.tensor
                def _(pe):
                    with pe.Fori(0, max(NG // 2, 1)) as i:
                        for q in range(min(2, NG)):
                            pe.wait_ge(ready, 2 * i + q + 1)
                            for g in range(NT):
                                last = nc.tensor.matmul(ps_s[q][:, g].rearrange("p j c -> p (j c)"),
                                                        mask[q][:, P * g:P * g + P],
                                                        diag[q][:].rearrange("p j c -> p (j c)"), start=True, stop=True)
                            last.then_inc(spread_out, 1)


def stage_attend_qkv(net, d):
    nc, sem = net.nc, net.sem
    RING, LAG = 4, 3
    with ExitStack() as ctx:
        def sb(name, shape, dt):
            return ctx.enter_context(nc.sbuf_tensor("a3_" + name, shape, dt))

        wk = [work_buffers(sb, f"w{h}") for h in range(2)]
        qx, kh, kl = ([sb(f"{s}{h}", [P, TOK], F16) for h in range(2)] for s in ("qx", "kh", "kl"))
        vh, vl = ([sb(f"{s}{h}", [P, NT, C + 1], F16) for h in range(2)] for s in ("vh", "vl"))
        pr = sb("pr", [P, RING, TOK], F32)
        prh, prl = (sb(s, [P, RING, TOK], F16) for s in ("prh", "prl"))
        ones = sb("ones", [P, P], F16)
        nmax = sb("nmax", [P, RING], F32)
        diag = sb("diag", [P, RING, P], F16)
        rinv = sb("rinv", [P, RING], F32)
        ps_a = ctx.enter_context(nc.psum_tensor("a3_ps_a", [P, TOK], F32))
        ps_s = ctx.enter_context(nc.psum_tensor("a3_ps_s", [P, 2, TOK], F32))
        ps_o = ctx.enter_context(nc.psum_tensor("a3_ps_o", [P, 512], F32))
        ps_w = ctx.enter_context(nc.psum_tensor("a3_ps_w", [P, 512], F32))
        ln = net.norms[0]
        base = net.normed
        net.normed += B
        proj, proj_high, proj_low, set_up = (sem("a3_" + s) for s in ("proj", "proj_high", "proj_low", "set_up"))
        ranged, maxed, diagonal, scored, exped, high, low, weighed, inverted, added = (sem("a3_" + s) for s in (
            "ranged", "maxed", "diagonal", "scored", "exped", "high", "low", "weighed", "inverted", "added"))
        tv = net.t[:].rearrange("p (i h) g c -> p i h g c", h=2)
        PROJ = 5

        def half_of(k):
            return slice(512 * (k % 2), 512 * (k % 2) + 512)

        def count(at, lag=0):
            i, h, m = at
            return NT * (2 * i + h) + m - lag + 1

        def past(at, lag):
            return tile_at(at[0], at[1], at[2] - lag) is not None

        with nc.Block() as block:
            @block.vector
            def _(dve):
                def near(i, h, m):
                    n, k = 2 * i + h, m - 1
                    if not 0 <= k < PROJ:
                        return
                    dve.wait_ge(proj_high, piece_count(n, PROJ, k))
                    if k < 2:
                        part = qx[h][C:P, half_of(k)]
                        ins = nc.vector.scalar_tensor_tensor(part, ps_w[C:P, :], IWS / TEMP, part, ALU.mult,
                                                             ALU.subtract)
                    elif k < 4:
                        ins = nc.vector.scalar_tensor_tensor(kl[h][:, half_of(k)], ps_w[:], IWS,
                                                             kh[h][:, half_of(k)], ALU.mult, ALU.subtract)
                    else:
                        ins = nc.vector.scalar_tensor_tensor(vl[h][:, :, 0:C], tiles(ps_w[:]), IWS,
                                                             vh[h][:, :, 0:C], ALU.mult, ALU.subtract)
                    ins.then_inc(proj_low, 1)

                def far(i, h, m):
                    n1, w = base + 2 * i + h + 1, wk[h]
                    if m == 0:
                        norm_sum(nc, ln, n1, tv[:, i, h], w)
                    if m == 1:
                        norm_centre(nc, ln, n1, tv[:, i, h], w)
                    if m == 2:
                        norm_sumsq(nc, ln, n1, w)
                    if m == 4:
                        norm_apply(nc, ln, n1, w)
                    if m == 5:
                        cut_low(nc, ln, n1, w, w["xn"])
                    if m == 7:
                        take_turned(nc, ln, n1, w, ps_w[:].bitcast(F16))

                def step(i, h, m):
                    at = tile_at(i, h, m + 1)
                    if at:
                        r = at[2] % RING
                        dve.wait_ge(ranged, count(at))
                        if past(at, RING):
                            dve.wait_ge(scored, count(at, RING))
                        nc.vector.tensor_reduce(nmax[:, r:r + 1], ps_a[:], AX.X, ALU.max, negate=True).then_inc(maxed, 1)
                        dve.wait_ge(maxed, count(at))
                        nc.vector.tensor_scalar(diag[:, r], net.ident16[:], nmax[:, r:r + 1], None,
                                                ALU.mult).then_inc(diagonal, 1)
                    at = tile_at(i, h, m - LAG)
                    if at:
                        ia, ha, g = at
                        dve.wait_ge(weighed, count(at))
                        nc.vector.reciprocal(rinv[:, g % RING:g % RING + 1], ps_o[:, C:C + 1]).then_inc(inverted, 1)
                        dve.wait_ge(inverted, count(at))
                        nc.vector.scalar_tensor_tensor(tv[:, ia, ha, g], ps_o[:, 0:C], rinv[:, g % RING:g % RING + 1],
                                                       tv[:, ia, ha, g], ALU.mult, ALU.add).then_inc(added, 1)

                for h in range(2):
                    nc.vector.memset(vh[h][:, :, C:C + 1], 1.0)
                    nc.vector.memset(vl[h][:, :, C:C + 1], 0.0)
                nc.vector.memset(ones[:], 1.0).then_inc(set_up, 1)
                stream(dve, step, near, far, LAG, near_first=True)
                dve.wait_ge(added, B * NT)

            @block.scalar
            def _(act):
                def near(i, h, k):
                    if k >= PROJ:
                        return
                    act.wait_ge(proj, piece_count(2 * i + h, PROJ, k))
                    if k < 2:
                        ins = nc.scalar.activation(qx[h][:, half_of(k)], ps_w[:], ACT.Copy, scale=IWS / TEMP)
                    elif k < 4:
                        ins = nc.scalar.activation(kh[h][:, half_of(k)], ps_w[:], ACT.Copy, scale=IWS)
                    else:
                        ins = nc.scalar.activation(vh[h][:, :, 0:C], tiles(ps_w[:]), ACT.Copy, scale=IWS)
                    ins.then_inc(proj_high, 1)

                def far(i, h, m):
                    n1, w = base + 2 * i + h + 1, wk[h]
                    if m == 1:
                        norm_square(nc, ln, n1, w)
                    if m == 4:
                        cut_high(nc, ln, n1, w, w["xn"])

                def step(i, h, m):
                    at = tile_at(i, h, m) if m >= 0 else None
                    if at:
                        r = at[2] % RING
                        act.wait_ge(scored, count(at))
                        if past(at, RING):
                            act.wait_ge(low, count(at, RING))
                        nc.scalar.activation(pr[:, r], ps_s[:, m % 2], ACT.Exp).then_inc(exped, 1)
                        act.wait_ge(exped, count(at))
                        if past(at, RING):
                            act.wait_ge(weighed, count(at, RING))
                        nc.scalar.activation(prh[:, r], pr[:, r], ACT.Copy).then_inc(high, 1)

                stream(act, step, near, far, 0)

            @block.gpsimd
            def _(pool):
                def near(i, h, m):
                    pass

                def far(i, h, m):
                    if m == 2:
                        norm_rstd(nc, ln, base + 2 * i + h + 1, wk[h], net.nhalf[:], net.eps[:])

                def step(i, h, m):
                    at = tile_at(i, h, m) if m >= 0 else None
                    if at:
                        r = at[2] % RING
                        pool.wait_ge(high, count(at))
                        nc.gpsimd.tensor_tensor(prl[:, r], pr[:, r], prh[:, r], ALU.subtract).then_inc(low, 1)

                stream(pool, step, near, far, 0)

            @block.tensor
            def _(pe):
                def near(i, h, k):
                    n, xT = 2 * i + h, wk[h]["xT"]
                    if k >= PROJ:
                        return
                    if k == 0:
                        pe.wait_ge(ln["xT"], base + n + 1)
                    else:
                        pe.wait_ge(proj_low, piece_count(n, PROJ, k - 1))
                    if k < 4:
                        tok = half_of(k)
                        last = upright(nc, net, ps_w[:], xT, COLS["q3" if k < 2 else "k3"], tok.start, tok.stop)
                    else:
                        for g in range(NT):
                            last = natural(nc, net, ps_w[:, C * g:C * g + C], xT, g, "v3")
                    last.then_inc(proj, 1)

                def far(i, h, m):
                    n = 2 * i + h
                    if m == 6:
                        if not isinstance(i, int) or n >= 1:
                            pe.wait_ge(proj_low, PROJ * n)
                        turn(nc, ln, base + n + 1, wk[h], ps_w[:].bitcast(F16), net.ident16[:])

                def step(i, h, m):
                    at = tile_at(i, h, m + 1)
                    if at:
                        ia, ha, g = at
                        if g == 0:
                            pe.wait_ge(proj_low, piece_count(2 * ia + ha, PROJ, PROJ - 1))
                        if past(at, 1):
                            pe.wait_ge(maxed, count(at, 1))
                        for half in range(2):
                            keys = slice(512 * half, 512 * half + 512)
                            last = nc.tensor.matmul(ps_a[:, keys], qx[ha][:, P * g:P * g + P], kh[ha][:, keys],
                                                    start=True, stop=True)
                        last.then_inc(ranged, 1)
                    at = tile_at(i, h, m) if m >= 0 else None
                    if at:
                        ia, ha, g = at
                        pe.wait_ge(diagonal, count(at))
                        if past(at, 2):
                            pe.wait_ge(exped, count(at, 2))
                        for half in range(2):
                            nc.tensor.matmul(ps_s[:, g % 2, 512 * half:512 * half + 512], ones[:],
                                             over(diag[:, g % RING], 4), start=True, stop=False, skip_group_check=True)
                            for j in range(4 * half, 4 * half + 4):
                                keys, out = slice(P * j, P * j + P), ps_s[:, g % 2, P * j:P * j + P]
                                query = qx[ha][:, P * g:P * g + P]
                                nc.tensor.matmul(out, kh[ha][:, keys], query, start=False, stop=False,
                                                 skip_group_check=True)
                                last = nc.tensor.matmul(out, kl[ha][:, keys], query, start=False, stop=(j % 4 == 3),
                                                        skip_group_check=True)
                        last.then_inc(scored, 1)
                    at = tile_at(i, h, m - LAG)
                    if at:
                        ia, ha, g = at
                        if past(at, 1):
                            pe.wait_ge(added, count(at, 1))
                        pe.wait_ge(low, count(at))
                        for j in range(NT):
                            high_j, low_j = (s[:, g % RING, P * j:P * j + P] for s in (prh, prl))
                            out = ps_o[:, 0:C + 1]
                            nc.tensor.matmul(out, high_j, vh[ha][:, j], start=(j == 0), stop=False)
                            nc.tensor.matmul(out, high_j, vl[ha][:, j], start=False, stop=False)
                            last = nc.tensor.matmul(out, low_j, vh[ha][:, j], start=False, stop=(j == NT - 1))
                        last.then_inc(weighed, 1)

                pe.wait_ge(set_up, 1)
                stream(pe, step, near, far, LAG)


def stage_route(net, d):
    nc, sem = net.nc, net.sem
    BANKS, MIXED = 5, 4
    with ExitStack() as ctx:
        def sb(name, shape, dt):
            return ctx.enter_context(nc.sbuf_tensor("f3_" + name, shape, dt))

        wk = [work_buffers(sb, f"w{h}") for h in range(2)]
        acc = [sb(f"acc{h}", [P, NT, C], F32) for h in range(2)]
        gates = [sb(f"gates{h}", [P, NT, E3], F32) for h in range(2)]
        order = sb("order", [P, E3], F32)
        a = {k: sb(k, [P, NT, E3], F32) for k in ("lg", "eq", "first", "rest", "second")}
        b = {k: sb(k, [P, NT], F32) for k in ("m1", "k1", "m2", "k2", "dl", "e2", "den", "g1", "g2")}
        mixed = sb("mixed", [P, MIXED, E3, C], F32)
        ps_e = ctx.enter_context(nc.psum_tensor("f3_ps_e", [P, BANKS, 512], F32))
        ps_t = ctx.enter_context(nc.psum_tensor("f3_ps_t", [P, TOK], F16))
        ps_r = ctx.enter_context(nc.psum_tensor("f3_ps_r", [P, 512], F32))
        ln = net.norms[0]
        base = net.normed
        net.normed += B
        routed, gate_step, diffed, e2_done = (sem("f3_" + s) for s in ("routed", "gate_step", "diffed", "e2_done"))
        expert_out, weighted, folded, summed_v, summed_g, added, stored = (sem("f3_" + s) for s in (
            "expert_out", "weighted", "folded", "summed_v", "summed_g", "added", "stored"))
        order_set = sem("f3_order_set")
        tv = net.t[:].rearrange("p (i h) g c -> p i h g c", h=2)
        ov = net.out.rearrange("n (g r) c k -> (r c) n g k", g=NT)
        CHAIN = 18
        STEPS = [("gate1", 0), ("norm0", 0), ("gate1", 1), ("mix0", 0), ("mix0", 1), ("gate1", 2), ("gate1", 3),
                 ("norm0", 1), ("gate1", 4), ("mix0", 2), ("gate1", 5), ("mix0", 3), ("mix0", 4), ("gate1", 6),
                 ("norm0", 2), ("gate1", 7), ("gate1", 8), ("mix0", 5), ("gate1", 9), ("norm1", 0), ("gate1", 10),
                 ("mix0", 6), ("gate1", 11), ("gate1", 12), ("gate1", 13), ("norm0", 3), ("gate1", 14), ("norm1", 1),
                 ("gate1", 15), ("gate1", 16), ("mix0", 7), ("gate1", 17), ("norm0", 4), ("mix1", 0), ("mix1", 1),
                 ("gate0", 0), ("gate0", 1), ("norm1", 2), ("mix0", 8), ("gate0", 2), ("norm0", 5), ("mix1", 2),
                 ("gate0", 3), ("gate0", 4), ("gate0", 5), ("gate0", 6), ("mix1", 3), ("gate0", 7), ("norm1", 3),
                 ("gate0", 8), ("mix1", 4), ("gate0", 9), ("gate0", 10), ("mix1", 5), ("mix1", 6), ("gate0", 11),
                 ("gate0", 12), ("mix1", 7), ("gate0", 13), ("norm1", 4), ("gate0", 14), ("norm1", 5), ("gate0", 15),
                 ("gate0", 16), ("mix1", 8), ("gate0", 17)]
        AHEAD = {"mix0": 0, "gate1": 0, "norm0": 1, "mix1": 0, "gate0": 1, "norm1": 1}

        def run(engine, norm, gate, mix):
            run_steps(engine, STEPS, AHEAD, {f"{name}{h}": partial(stream, h) for h in range(2)
                                             for name, stream in (("norm", norm), ("gate", gate), ("mix", mix))}, PAIRS)

        def past(n, g, lag):
            return not isinstance(n, int) or NT * n + g - lag >= 0

        def half(n, g, lag=0):
            return (NT // 2) * n + (g - lag) // 2 + 1

        with nc.Block() as block:
            @block.sync
            def _(sp):
                with sp.Fori(0, B) as n:
                    sp.wait_ge(added, n + 1)
                    sp.dma_start(ov[:, n], net.t[:, n]).then_inc(stored, 16)
                sp.wait_ge(stored, 16 * B)

            @block.vector
            def _(dve):
                for e in range(E3):
                    ins = nc.vector.memset(order[:, e:e + 1], float(E3 - e))
                ins.then_inc(order_set, 1)
                dve.wait_ge(order_set, 1)
                weights = over(order[:], NT)

                def norm(h, i, step):
                    n, w = 2 * i + h, wk[h]
                    if step == 0:
                        norm_sum(nc, ln, base + n + 1, tv[:, i, h], w)
                        norm_centre(nc, ln, base + n + 1, tv[:, i, h], w)
                    if step == 1:
                        norm_sumsq(nc, ln, base + n + 1, w)
                    if step == 4:
                        take_turned(nc, ln, base + n + 1, w, ps_t[:])

                def gate(h, i, step):
                    n = 2 * i + h
                    v, lg, eq, first, rest, second = nc.vector, *(a[k][:] for k in ("lg", "eq", "first", "rest", "second"))
                    if step == 0:
                        dve.wait_ge(routed, n + 1)
                    elif step == 12:
                        dve.wait_ge(e2_done, n + 1)
                    else:
                        dve.wait_ge(gate_step, piece_count(n, CHAIN, step - 1))
                    if step == 0:
                        ins = v.tensor_copy(lg, ps_r[:, 0:NT * E3].rearrange("p (g e) -> p g e", e=E3))
                    if step == 1:
                        ins = v.tensor_reduce(b["m1"][:], lg, AX.X, ALU.max)
                    if step == 2:
                        ins = v.tensor_tensor(eq, lg, spread(b["m1"][:], E3), ALU.is_equal)
                    if step == 3:
                        ins = v.tensor_tensor(first, eq, weights, ALU.mult)
                    if step == 4:
                        ins = v.tensor_reduce(b["k1"][:], first, AX.X, ALU.max)
                    if step == 5:
                        ins = v.tensor_tensor(first, first, spread(b["k1"][:], E3), ALU.is_equal)
                    if step == 6:
                        ins = v.scalar_tensor_tensor(rest, first, -1e30, lg, ALU.mult, ALU.add)
                    if step == 7:
                        ins = v.tensor_reduce(b["m2"][:], rest, AX.X, ALU.max)
                    if step == 8:
                        v.tensor_tensor(b["dl"][:], b["m2"][:], b["m1"][:], ALU.subtract).then_inc(diffed, 1)
                        ins = v.tensor_tensor(eq, rest, spread(b["m2"][:], E3), ALU.is_equal)
                    if step == 9:
                        ins = v.tensor_tensor(second, eq, weights, ALU.mult)
                    if step == 10:
                        ins = v.tensor_reduce(b["k2"][:], second, AX.X, ALU.max)
                    if step == 11:
                        ins = v.tensor_tensor(second, second, spread(b["k2"][:], E3), ALU.is_equal)
                    if step == 12:
                        ins = v.tensor_scalar(b["den"][:], b["e2"][:], WS, WS, ALU.mult, ALU.add)
                    if step == 13:
                        ins = v.reciprocal(b["g1"][:], b["den"][:])
                    if step == 14:
                        ins = v.tensor_tensor(b["g2"][:], b["e2"][:], b["g1"][:], ALU.mult)
                    if step == 15:
                        ins = v.tensor_tensor(first, first, spread(b["g1"][:], E3), ALU.mult)
                    if step == 16:
                        ins = v.tensor_tensor(second, second, spread(b["g2"][:], E3), ALU.mult)
                    if step == 17:
                        ins = v.tensor_tensor(gates[h][:], first, second, ALU.add)
                    ins.then_inc(gate_step, 1)

                def reduce(n, h, g):
                    dve.wait_ge(weighted, piece_count(n, NT, g))
                    nc.vector.tensor_reduce(acc[h][:, g], mixed[:, g % MIXED].rearrange("p e c -> p c e"), AX.X,
                                            ALU.add).then_inc(summed_v, 1)

                def mix(h, i, g):
                    n = 2 * i + h
                    if g < NT:
                        dve.wait_ge(expert_out, piece_count(n, NT, g))
                        if g == 0:
                            dve.wait_ge(gate_step, piece_count(n, CHAIN, CHAIN - 1))
                        if past(n, g, MIXED):
                            dve.wait_ge(summed_v if g % 2 == 0 else summed_g, half(n, g, MIXED))
                        nc.vector.tensor_tensor(mixed[:, g % MIXED], ps_e[:, g % BANKS].rearrange("p (e c) -> p e c", e=E3),
                                                spread(gates[h][:, g], C), ALU.mult).then_inc(weighted, 1)
                        if g % 2:
                            reduce(n, h, g - 1)
                    if g == NT:
                        dve.wait_ge(summed_v, half(n, NT - 2))
                        dve.wait_ge(summed_g, half(n, NT - 1))
                        nc.vector.tensor_tensor(tv[:, i, h], tv[:, i, h], acc[h][:], ALU.add).then_inc(added, 1)

                run(dve, norm, gate, mix)

            @block.scalar
            def _(act):
                def norm(h, i, step):
                    n, w = 2 * i + h, wk[h]
                    if step == 0:
                        norm_square(nc, ln, base + n + 1, w)
                    if step == 2:
                        cut_high(nc, ln, base + n + 1, w, w["xn"])

                def gate(h, i, step):
                    n = 2 * i + h
                    if step == 8:
                        act.wait_ge(diffed, n + 1)
                        nc.scalar.activation(b["e2"][:], b["dl"][:], ACT.Exp, scale=IWS).then_inc(e2_done, 1)

                def mix(h, i, g):
                    pass

                run(act, norm, gate, mix)

            @block.gpsimd
            def _(pool):
                def norm(h, i, step):
                    n, w = 2 * i + h, wk[h]
                    if step == 1:
                        norm_rstd(nc, ln, base + n + 1, w, net.nhalf[:], net.eps[:])
                    if step == 2:
                        norm_apply(nc, ln, base + n + 1, w, nc.gpsimd)
                    if step == 3:
                        cut_low(nc, ln, base + n + 1, w, w["xn"], nc.gpsimd)

                def gate(h, i, step):
                    pass

                def mix(h, i, g):
                    n = 2 * i + h
                    if g < NT and g % 2:
                        m = mixed[:, g % MIXED]
                        pool.wait_ge(weighted, piece_count(n, NT, g))
                        nc.gpsimd.tensor_tensor(m[:, 0:4], m[:, 0:4], m[:, 4:8], ALU.add).then_inc(folded, 1)
                        pool.wait_ge(folded, 2 * half(n, g) - 1)
                        nc.gpsimd.tensor_tensor(m[:, 0:2], m[:, 0:2], m[:, 2:4], ALU.add).then_inc(folded, 1)
                        pool.wait_ge(folded, 2 * half(n, g))
                        nc.gpsimd.tensor_tensor(acc[h][:, g], m[:, 0], m[:, 1], ALU.add).then_inc(summed_g, 1)

                run(pool, norm, gate, mix)

            @block.tensor
            def _(pe):
                def norm(h, i, step):
                    n, w = 2 * i + h, wk[h]
                    if step == 4:
                        turn(nc, ln, base + n + 1, w, ps_t[:], net.ident16[:])
                    if step == 5:
                        pe.wait_ge(ln["xT"], base + n + 1)
                        if not isinstance(n, int) or n >= 1:
                            pe.wait_ge(gate_step, CHAIN * (n - 1) + 1)
                        for g in range(NT):
                            ins = natural(nc, net, ps_r[:, E3 * g:E3 * g + E3], w["xT"], g, "router")
                        ins.then_inc(routed, 1)

                def gate(h, i, step):
                    pass

                def mix(h, i, g):
                    n = 2 * i + h
                    if g < NT:
                        if g >= BANKS:
                            pe.wait_ge(weighted, piece_count(n, NT, g - BANKS))
                        elif past(n, g, NT):
                            before = g + BANKS if g + BANKS < NT else g
                            pe.wait_ge(weighted, piece_count(n - 1, NT, before))
                        natural(nc, net, ps_e[:, g % BANKS], wk[h]["xT"], g, "exp3").then_inc(expert_out, 1)

                run(pe, norm, gate, mix)


STAGES = [stage_attend, stage_pool, stage_attend_qkv, stage_route]


INPUTS = ['x', 'L0_conv_ln1_g', 'L0_conv_ln1_b', 'L0_conv_qkv_w', 'L0_conv_qkv_b', 'L0_conv_proj_w', 'L0_conv_proj_b',
          'L0_conv_rpb', 'L0_conv_ln2_g', 'L0_conv_ln2_b', 'L0_conv_fc1_w', 'L0_conv_fc1_b', 'L0_conv_fc2_w',
          'L0_conv_fc2_b', 'L1_conv_W_left', 'L1_conv_b_left', 'L1_conv_W_right', 'L1_conv_b_right', 'L1_conv_W_gate',
          'L1_conv_b_gate', 'L1_conv_W_eq', 'L1_conv_b_eq', 'L1_conv_W_out', 'L1_conv_b_out', 'L1_conv_ln_scale',
          'L1_conv_ln_bias', 'L2_ffn_gate_w', 'L2_ffn_gate_b', 'L2_ffn_weight1', 'L2_ffn_weight2', 'L3_attn_Wq',
          'L3_attn_bq', 'L3_attn_Wk', 'L3_attn_bk', 'L3_attn_Wv', 'L3_attn_bv', 'L3_ffn_router_w', 'L3_ffn_router_b',
          'L3_ffn_expert_w', 'L3_ffn_expert_b']


def build(nc, d, k, out, stages=None):
    with ExitStack() as ctx:
        def sb(name, shape, dt):
            return ctx.enter_context(nc.sbuf_tensor(name, shape, dt))

        net = Net()
        net.nc, net.out = nc, out
        held = []

        def sem(name):
            held.append(nc.alloc_semaphore(name=name))
            return held[-1]

        net.sem = sem
        net.t = sb("tokens", [P, B, NT, C], F32)
        net.ident = sb("ident", [P, P], F32)
        net.ident16 = sb("ident16", [P, P], F16)
        net.perm16 = sb("perm16", [P, 2, P], F16)
        net.same16 = sb("same16", [P, P], F16)
        net.hmask = sb("hmask", [P, HEADS], F32)
        net.nhalf = sb("nhalf", [P, NT], F32)
        net.eps = sb("eps", [P, NT], F32)
        net.ones16 = sb("ones16", [2, 512], F16)
        net.wa = sb("wa", [P, NWC], F16)
        net.wb = sb("wb", [P, NWC], F16)
        net.bias = sb("bias", [2, NWC + C], F16)
        net.fc2h = sb("fc2h", [P, 2, C], F16)
        net.fc2l = sb("fc2l", [P, 2, C], F16)
        net.sbias = sb("sbias", [P, 2, 2, HEADS, C], F32)
        net.lns = sb("lns", [P, C], F32)
        net.lnb = sb("lnb", [P, C], F32)
        net.norms = [{part: net.sem(f"norm{j}_{part}") for part in NORM_PARTS} for j in range(3)]
        net.cuts = [{part: net.sem(f"cut{j}_{part}") for part in NORM_PARTS[6:]} for j in range(3)]
        net.t_ready = {part: net.sem(f"{part}_ready") for part in ("x1", "y", "t")}
        held.clear()

        def release():
            nc.clear_and_free_semaphores(held)
            nc.all_engine_barrier()
            held.clear()

        stage_setup(net, d, k)
        release()
        stage_blocks(net, d["x"])
        net.normed = B
        release()
        for st in STAGES:
            if stages is None or st.__name__ in stages:
                st(net, d)
                release()
        if stages is not None and "stage_route" not in stages:
            finish_store(net, out)



def constants():
    import numpy as np

    p, key = np.arange(P), np.arange(WIN * WIN)
    window, row, col = p // 64, p % 64 // WIN, p % WIN
    mask = np.zeros((P, 2, 2, 64), np.float32)
    for last_row in range(2):
        for jp in range(2):
            hidden = np.zeros((P, 64), bool)
            if last_row:
                hidden |= (row // 4)[:, None] != (key // 32)[None]
            if jp:
                hidden |= (window == 1)[:, None] & ((col // 4)[:, None] != (key % WIN // 4)[None])
            mask[:, last_row, jp] = np.where(hidden, np.float32(-1e9), np.float32(0))
    source = (np.arange(4)[None, :, None] * W
              + (WIN * np.arange(4)[:, None, None] + np.arange(WIN)[None, None, :] + WIN // 2) % W).reshape(-1)
    to_windows = np.zeros((P, P), np.float32)
    to_windows[source, p] = 1
    source = (64 * np.arange(2)[None, :, None] + WIN * np.arange(WIN)[:, None, None]
              + np.arange(WIN)[None, None, :]).reshape(-1)
    from_windows = np.zeros((P, P), np.float32)
    from_windows[source, p] = 1
    head = (np.arange(P) % 64 // HD)[:, None] == np.arange(HEADS)[None]
    return {"ident": np.eye(P, dtype=np.float32), "mask": mask, "hmask": head.astype(np.float32),
            "samerow": (p[:, None] // W == p[None] // W).astype(np.float32),
            "to_windows": to_windows, "from_windows": from_windows}


def kernel(**inputs):
    import numpy as _np
    import concourse.bacc as _bacc
    from concourse import mybir as _mybir
    from concourse.bass_utils import run_bass_kernel_spmd as _run

    nc = _bacc.Bacc("TRN2", target_bir_lowering=False, num_devices=1)
    arrays, d, k = {}, {}, {}
    for name in INPUTS:
        a = _np.ascontiguousarray(inputs[name])
        arrays[f"in_{name}_dram"] = a
        d[name] = nc.dram_tensor(f"in_{name}_dram", a.shape, _mybir.dt.from_np(a.dtype), kind="ExternalInput").ap()
    for name, a in constants().items():
        arrays[f"const_{name}_dram"] = a
        k[name] = nc.dram_tensor(f"const_{name}_dram", a.shape, _mybir.dt.from_np(a.dtype), kind="ExternalInput").ap()
    out = nc.dram_tensor("out_0_dram", (B, H, W, C), F32, kind="ExternalOutput").ap()
    build(nc, d, k, out)
    r = _run(nc, [arrays], core_ids=[0])
    return r.results[0]["out_0_dram"]
```
